# Optimizing a Trainium2 kernel written in Bass

```python
import numpy as np
import jax
import jax.numpy as jnp

def _softmax(x, axis=-1):
    return jax.nn.softmax(x, axis=axis)

def _gelu(x):
    return jax.nn.gelu(x, approximate=True)

def _silu(x):
    return jax.nn.silu(x)

def _sigmoid(x):
    return jax.nn.sigmoid(x)

def _layernorm(x, axis=-1, eps=1e-05):
    m = jnp.mean(x, axis=axis, keepdims=True)
    v = jnp.var(x, axis=axis, keepdims=True)
    return (x - m) / jnp.sqrt(v + eps)

def _scatter_add(tgt, idx, src, axis=0):
    return tgt.at[idx].add(src)

def _segment_sum(src, seg, n):
    return jax.ops.segment_sum(src, seg, n)
kernel_name = 'mk_hybrid_d2_jaxref_r8_23b3e7'

def setup_inputs(seed: int=0):
    np.random.seed(seed)
    _w = jnp.asarray

    def _L0_attn_a_setup():
        import math
        import jax, jax.numpy as jnp
        import numpy as np

        def _expmap0(u):
            u0 = u[..., :1]
            us = u[..., 1:]
            mink = -u0 * u0 + jnp.sum(us * us, axis=-1, keepdims=True)
            nomin = jnp.sqrt(jnp.maximum(mink, 1e-08))
            r = jnp.sinh(nomin) * u / nomin
            space = r[..., 1:]
            time = jnp.sqrt(1.0 + jnp.sum(space * space, axis=-1, keepdims=True))
            return jnp.concatenate([time, space], axis=-1)
        key = jax.random.key(seed)
        B, T, E, H = (2, 128, 128, 16)
        ks = jax.random.split(key, 8)
        s = 0.02
        return {'x': jax.random.normal(ks[0], (B, T, E), jnp.float32), 'Wqkv': jax.random.normal(ks[1], (3 * E, E), jnp.float32) * s, 'bqkv': jnp.zeros((3 * E,), jnp.float32), 'Wout': jax.random.normal(ks[2], (E, E), jnp.float32) * s, 'bout': jnp.zeros((E,), jnp.float32), 'Wimp': jax.random.normal(ks[3], (1, E), jnp.float32) * s, 'bimp': jnp.zeros((1,), jnp.float32), 'Walpha': jax.random.normal(ks[4], (H, E), jnp.float32) * s, 'balpha': jnp.zeros((H,), jnp.float32), 'spike_threshold': jnp.asarray(0.5, jnp.float32), 'log_k': jnp.full((H,), 0.54, jnp.float32), 'qk_scale': jnp.asarray(0.1, jnp.float32)}
    _L0_attn_a_in = _L0_attn_a_setup()

    def _L0_attn_b_setup():
        import jax, jax.numpy as jnp
        import numpy as np
        D_MODEL = 128
        NUM_HEADS = 16
        D_HEAD = D_MODEL // NUM_HEADS
        B, T = (2, 256)
        key = jax.random.key(seed)
        k1, k2, k3 = jax.random.split(key, 3)
        std_qkv = np.sqrt(2.0 / (3 * D_MODEL + D_MODEL))
        std_out = np.sqrt(2.0 / (D_MODEL + D_MODEL))
        x = jax.random.normal(k1, (B, T, D_MODEL), dtype=jnp.float32)
        Wqkv = jax.random.normal(k2, (3 * D_MODEL, D_MODEL), dtype=jnp.float32) * std_qkv
        Wout = jax.random.normal(k3, (D_MODEL, D_MODEL), dtype=jnp.float32) * std_out
        return {'x': x, 'Wqkv': Wqkv, 'Wout': Wout}
    _L0_attn_b_in = _L0_attn_b_setup()

    def _L0_ffn_setup():
        import jax, jax.numpy as jnp
        import numpy as np
        D = 128
        H = 16
        DH = D // H
        DC = D // 4
        HID = 256
        G = 2
        EPG = 4
        E = G * EPG
        TOPK = 2
        EPS = 1e-06
        B, T = (2, 256)

        def _rope_sincos(t, dh):
            inv_freq = 1.0 / 10000.0 ** (jnp.arange(0, dh, 2, dtype=jnp.float32) / dh)
            ang = jnp.arange(t, dtype=jnp.float32)[:, None] * inv_freq[None, :]
            return (jnp.sin(ang), jnp.cos(ang))

        def _apply_rope(x, sin, cos):
            x1 = x[..., ::2]
            x2 = x[..., 1::2]
            r = jnp.stack([x1 * cos - x2 * sin, x1 * sin + x2 * cos], axis=-1)
            return r.reshape(x.shape)

        def _swiglu(x):
            a, b = jnp.split(x, 2, axis=-1)
            return jax.nn.silu(a) * b

        def _rmsnorm(x, w):
            return x * jax.lax.rsqrt(jnp.mean(x * x, axis=-1, keepdims=True) + EPS) * w
        key = jax.random.key(seed)
        ks = jax.random.split(key, 14)
        s = 0.02
        return {'src': jax.random.normal(ks[0], (B, T, D), jnp.float32), 'Wq': jax.random.normal(ks[1], (D, D), jnp.float32) * s, 'Wk_c': jax.random.normal(ks[2], (D, DC), jnp.float32) * s, 'Wv_c': jax.random.normal(ks[3], (D, DC), jnp.float32) * s, 'Wk': jax.random.normal(ks[4], (DC, D), jnp.float32) * s, 'Wv': jax.random.normal(ks[5], (DC, D), jnp.float32) * s, 'Wo': jax.random.normal(ks[6], (D, D), jnp.float32) * s, 'W_shared_in': jax.random.normal(ks[7], (D, 2 * HID), jnp.float32) * s, 'W_shared_out': jax.random.normal(ks[8], (HID, D), jnp.float32) * s, 'W1_shared': jax.random.normal(ks[9], (D, 2 * HID), jnp.float32) * s, 'W2_experts': jax.random.normal(ks[10], (E, HID, D), jnp.float32) * s, 'Wg_gate': jax.random.normal(ks[11], (D, G), jnp.float32) * s, 'We_gate': jax.random.normal(ks[12], (D, E), jnp.float32) * s, 'group_bias': jnp.zeros((G,), jnp.float32), 'expert_bias': jnp.zeros((E,), jnp.float32), 'norm1_w': jnp.ones((D,), jnp.float32), 'norm2_w': jnp.ones((D,), jnp.float32)}
    _L0_ffn_in = _L0_ffn_setup()

    def _L1_attn_a_setup():
        import jax, jax.numpy as jnp
        import numpy as np
        from math import sqrt
        ROPE_BASE = 6000.0

        def _rope_tables(seq_len, rope_dim, dtype):
            inv_freq = 1.0 / ROPE_BASE ** (jnp.arange(0, rope_dim, 2, dtype=jnp.float32) / rope_dim)
            t = jnp.arange(seq_len, dtype=jnp.float32)
            freqs = jnp.outer(t, inv_freq)
            emb = jnp.concatenate([freqs, freqs], axis=-1)
            return (jnp.cos(emb).astype(dtype), jnp.sin(emb).astype(dtype))

        def _rotate_half(x):
            x1, x2 = jnp.split(x, 2, axis=-1)
            return jnp.concatenate([-x2, x1], axis=-1)
        key = jax.random.key(seed)
        k1, k2, k3 = jax.random.split(key, 3)
        B, S, D = (2, 256, 128)
        H, DK = (16, 64)
        x = jax.random.normal(k1, (B, S, D), dtype=jnp.float32)
        W_qkv = jax.random.normal(k2, (3, H, DK, D), dtype=jnp.float32) * 0.02
        W_o = jax.random.normal(k3, (D, H * DK), dtype=jnp.float32) * 0.02
        return {'x': x, 'W_qkv': W_qkv, 'W_o': W_o}
    _L1_attn_a_in = _L1_attn_a_setup()

    def _L1_attn_b_setup():
        import jax, jax.numpy as jnp
        import numpy as np
        import math
        DIM = 128
        N_HEADS = 16
        HEAD_DIM = DIM // N_HEADS
        B, S = (2, 256)
        key = jax.random.key(seed)
        k_x, k_wqkv, k_bqkv, k_wout, k_bout = jax.random.split(key, 5)
        scale_in = 1.0 / math.sqrt(DIM)
        x = jax.random.normal(k_x, (B, S, DIM), dtype=jnp.float32)
        Wqkv = jax.random.uniform(k_wqkv, (N_HEADS, DIM, 3 * HEAD_DIM), dtype=jnp.float32, minval=-scale_in, maxval=scale_in)
        bqkv = jax.random.uniform(k_bqkv, (N_HEADS, 3 * HEAD_DIM), dtype=jnp.float32, minval=-scale_in, maxval=scale_in)
        Wout = jax.random.uniform(k_wout, (DIM, DIM), dtype=jnp.float32, minval=-scale_in, maxval=scale_in)
        bout = jax.random.uniform(k_bout, (DIM,), dtype=jnp.float32, minval=-scale_in, maxval=scale_in)
        return {'x': x, 'Wqkv': Wqkv, 'bqkv': bqkv, 'Wout': Wout, 'bout': bout}
    _L1_attn_b_in = _L1_attn_b_setup()

    def _L1_ffn_setup():
        import jax, jax.numpy as jnp
        import numpy as np
        GROUP = 16
        EPS = 1e-05

        def _dequant(q, scale):
            w = q.astype(jnp.float32) / 7.5 - 1.0
            return w * jnp.repeat(scale, GROUP, axis=1)

        def _qlora_linear(x, q, scale, bias, la, lb):
            w = _dequant(q, scale)
            base = jnp.einsum('btd,od->bto', x, w) + bias
            lora = jnp.einsum('btr,or->bto', jnp.einsum('btd,rd->btr', x, la), lb)
            return base + lora

        def _layernorm(x, g, b):
            mu = jnp.mean(x, axis=-1, keepdims=True)
            var = jnp.mean(jnp.square(x - mu), axis=-1, keepdims=True)
            return (x - mu) * jax.lax.rsqrt(var + EPS) * g + b
        key = jax.random.key(seed)
        ks = jax.random.split(key, 6)
        D, R, B, T = (128, 32, 8, 512)
        x = jax.random.normal(ks[0], (B, T, D), dtype=jnp.float32)
        qweights = jax.random.randint(ks[1], (6, D, D), 0, 16, dtype=jnp.int32)
        scales = jax.random.uniform(ks[2], (6, D, D // GROUP), dtype=jnp.float32)
        biases = jax.random.normal(ks[3], (6, D), dtype=jnp.float32) * 0.02
        lora_a = jax.random.normal(ks[4], (6, R, D), dtype=jnp.float32) * 0.02
        lora_b = jax.random.normal(ks[5], (6, D, R), dtype=jnp.float32) * 0.02
        ln_gamma = jnp.ones((3, D), dtype=jnp.float32)
        ln_beta = jnp.zeros((3, D), dtype=jnp.float32)
        return {'x': x, 'qweights': qweights, 'scales': scales, 'biases': biases, 'lora_a': lora_a, 'lora_b': lora_b, 'ln_gamma': ln_gamma, 'ln_beta': ln_beta}
    _L1_ffn_in = _L1_ffn_setup()
    _d = {'L0_attn_a_x': _L0_attn_a_in['x'], 'L0_attn_a_Wqkv': _L0_attn_a_in['Wqkv'], 'L0_attn_a_bqkv': _L0_attn_a_in['bqkv'], 'L0_attn_a_Wout': _L0_attn_a_in['Wout'], 'L0_attn_a_bout': _L0_attn_a_in['bout'], 'L0_attn_a_Wimp': _L0_attn_a_in['Wimp'], 'L0_attn_a_bimp': _L0_attn_a_in['bimp'], 'L0_attn_a_Walpha': _L0_attn_a_in['Walpha'], 'L0_attn_a_balpha': _L0_attn_a_in['balpha'], 'L0_attn_a_spike_threshold': _L0_attn_a_in['spike_threshold'], 'L0_attn_a_log_k': _L0_attn_a_in['log_k'], 'L0_attn_a_qk_scale': _L0_attn_a_in['qk_scale'], 'L0_attn_b_Wqkv': _L0_attn_b_in['Wqkv'], 'L0_attn_b_Wout': _L0_attn_b_in['Wout'], 'L0_ffn_Wq': _L0_ffn_in['Wq'], 'L0_ffn_Wk_c': _L0_ffn_in['Wk_c'], 'L0_ffn_Wv_c': _L0_ffn_in['Wv_c'], 'L0_ffn_Wk': _L0_ffn_in['Wk'], 'L0_ffn_Wv': _L0_ffn_in['Wv'], 'L0_ffn_Wo': _L0_ffn_in['Wo'], 'L0_ffn_W_shared_in': _L0_ffn_in['W_shared_in'], 'L0_ffn_W_shared_out': _L0_ffn_in['W_shared_out'], 'L0_ffn_W1_shared': _L0_ffn_in['W1_shared'], 'L0_ffn_W2_experts': _L0_ffn_in['W2_experts'], 'L0_ffn_Wg_gate': _L0_ffn_in['Wg_gate'], 'L0_ffn_We_gate': _L0_ffn_in['We_gate'], 'L0_ffn_group_bias': _L0_ffn_in['group_bias'], 'L0_ffn_expert_bias': _L0_ffn_in['expert_bias'], 'L0_ffn_norm1_w': _L0_ffn_in['norm1_w'], 'L0_ffn_norm2_w': _L0_ffn_in['norm2_w'], 'L1_attn_a_W_qkv': _L1_attn_a_in['W_qkv'], 'L1_attn_a_W_o': _L1_attn_a_in['W_o'], 'L1_attn_b_Wqkv': _L1_attn_b_in['Wqkv'], 'L1_attn_b_bqkv': _L1_attn_b_in['bqkv'], 'L1_attn_b_Wout': _L1_attn_b_in['Wout'], 'L1_attn_b_bout': _L1_attn_b_in['bout'], 'L1_ffn_qweights': _L1_ffn_in['qweights'], 'L1_ffn_scales': _L1_ffn_in['scales'], 'L1_ffn_biases': _L1_ffn_in['biases'], 'L1_ffn_lora_a': _L1_ffn_in['lora_a'], 'L1_ffn_lora_b': _L1_ffn_in['lora_b'], 'L1_ffn_ln_gamma': _L1_ffn_in['ln_gamma'], 'L1_ffn_ln_beta': _L1_ffn_in['ln_beta']}
    _x0 = _d['L0_attn_a_x']
    _d['L0_attn_a_x'] = jax.random.normal(jax.random.fold_in(jax.random.key(seed), 1), (16, 256, 128), dtype=_x0.dtype)
    del _x0
    return _d

def reference(L0_attn_a_x, L0_attn_a_Wqkv, L0_attn_a_bqkv, L0_attn_a_Wout, L0_attn_a_bout, L0_attn_a_Wimp, L0_attn_a_bimp, L0_attn_a_Walpha, L0_attn_a_balpha, L0_attn_a_spike_threshold, L0_attn_a_log_k, L0_attn_a_qk_scale, L0_attn_b_Wqkv, L0_attn_b_Wout, L0_ffn_Wq, L0_ffn_Wk_c, L0_ffn_Wv_c, L0_ffn_Wk, L0_ffn_Wv, L0_ffn_Wo, L0_ffn_W_shared_in, L0_ffn_W_shared_out, L0_ffn_W1_shared, L0_ffn_W2_experts, L0_ffn_Wg_gate, L0_ffn_We_gate, L0_ffn_group_bias, L0_ffn_expert_bias, L0_ffn_norm1_w, L0_ffn_norm2_w, L1_attn_a_W_qkv, L1_attn_a_W_o, L1_attn_b_Wqkv, L1_attn_b_bqkv, L1_attn_b_Wout, L1_attn_b_bout, L1_ffn_qweights, L1_ffn_scales, L1_ffn_biases, L1_ffn_lora_a, L1_ffn_lora_b, L1_ffn_ln_gamma, L1_ffn_ln_beta):

    def _L0_attn_a_ref(x, Wqkv, bqkv, Wout, bout, Wimp, bimp, Walpha, balpha, spike_threshold, log_k, qk_scale):
        import math
        import jax, jax.numpy as jnp
        import numpy as np

        def _expmap0(u):
            u0 = u[..., :1]
            us = u[..., 1:]
            mink = -u0 * u0 + jnp.sum(us * us, axis=-1, keepdims=True)
            nomin = jnp.sqrt(jnp.maximum(mink, 1e-08))
            r = jnp.sinh(nomin) * u / nomin
            space = r[..., 1:]
            time = jnp.sqrt(1.0 + jnp.sum(space * space, axis=-1, keepdims=True))
            return jnp.concatenate([time, space], axis=-1)
        B, T, C = x.shape
        H = log_k.shape[0]
        D = C // H
        importance = jax.nn.sigmoid(x @ Wimp.T + bimp)
        spikes = (importance > spike_threshold).astype(x.dtype)
        spike_mask = spikes.reshape(B, 1, T, 1)
        alpha = jax.nn.sigmoid(x @ Walpha.T + balpha)
        alpha = jnp.transpose(alpha, (0, 2, 1))[..., None]
        qkv = (x @ Wqkv.T + bqkv).reshape(B, T, 3, H, D)
        q = jnp.transpose(qkv[:, :, 0], (0, 2, 1, 3))
        k = jnp.transpose(qkv[:, :, 1], (0, 2, 1, 3))
        v = jnp.transpose(qkv[:, :, 2], (0, 2, 1, 3))
        scores_euclid = jnp.einsum('bhtd,bhsd->bhts', q, k) / math.sqrt(D)
        safe_scale = jax.nn.sigmoid(qk_scale) * 1.5
        qn = q / jnp.maximum(jnp.linalg.norm(q, axis=-1, keepdims=True), 1e-12) * safe_scale
        kn = k / jnp.maximum(jnp.linalg.norm(k, axis=-1, keepdims=True), 1e-12) * safe_scale
        q_hyp = _expmap0(qn)
        k_hyp = _expmap0(kn)
        inner = -jnp.einsum('bhti,bhsi->bhts', q_hyp[..., :1], k_hyp[..., :1]) + jnp.einsum('bhtd,bhsd->bhts', q_hyp[..., 1:], k_hyp[..., 1:])
        curv_k = (jax.nn.softplus(log_k) + 1e-06).reshape(1, H, 1, 1)
        mdot = jnp.maximum(-inner, 1.0 + 1e-06)
        dist = jnp.arccosh(mdot)
        scores_hyper = -(dist * dist) / curv_k
        scores = (1.0 - alpha) * scores_euclid + alpha * scores_hyper
        causal = jnp.tril(jnp.ones((T, T), bool))
        scores = jnp.where(causal[None, None], scores, -jnp.inf)
        attn = jax.nn.softmax(scores, axis=-1) * spike_mask
        y = jnp.einsum('bhts,bhsd->bhtd', attn, v)
        y = jnp.transpose(y, (0, 2, 1, 3)).reshape(B, T, C)
        return y @ Wout.T + bout

    def _L0_attn_b_ref(x, Wqkv, Wout):
        import jax, jax.numpy as jnp
        import numpy as np
        D_MODEL = 128
        NUM_HEADS = 16
        D_HEAD = D_MODEL // NUM_HEADS
        B, T = (2, 256)
        Bz, Tz, _ = x.shape
        qkv = jnp.einsum('btd,ed->bte', x, Wqkv)
        q, k, v = jnp.split(qkv, 3, axis=-1)

        def to_heads(t):
            return t.reshape(Bz, Tz, NUM_HEADS, D_HEAD).transpose(0, 2, 1, 3)
        q, k, v = (to_heads(q), to_heads(k), to_heads(v))
        scale = 1.0 / jnp.sqrt(jnp.asarray(D_HEAD, dtype=x.dtype))
        scores = jnp.einsum('bhqd,bhkd->bhqk', q, k) * scale
        causal = jnp.tril(jnp.ones((Tz, Tz), dtype=bool))
        scores = jnp.where(causal, scores, -jnp.inf)
        weights = jax.nn.softmax(scores, axis=-1)
        y = jnp.einsum('bhqk,bhkd->bhqd', weights, v)
        y = y.transpose(0, 2, 1, 3).reshape(Bz, Tz, D_MODEL)
        return jnp.einsum('btd,ed->bte', y, Wout)

    def _L0_ffn_ref(src, Wq, Wk_c, Wv_c, Wk, Wv, Wo, W_shared_in, W_shared_out, W1_shared, W2_experts, Wg_gate, We_gate, group_bias, expert_bias, norm1_w, norm2_w):
        import jax, jax.numpy as jnp
        import numpy as np
        D = 128
        H = 16
        DH = D // H
        DC = D // 4
        HID = 256
        G = 2
        EPG = 4
        E = G * EPG
        TOPK = 2
        EPS = 1e-06
        B, T = (2, 256)

        def _rope_sincos(t, dh):
            inv_freq = 1.0 / 10000.0 ** (jnp.arange(0, dh, 2, dtype=jnp.float32) / dh)
            ang = jnp.arange(t, dtype=jnp.float32)[:, None] * inv_freq[None, :]
            return (jnp.sin(ang), jnp.cos(ang))

        def _apply_rope(x, sin, cos):
            x1 = x[..., ::2]
            x2 = x[..., 1::2]
            r = jnp.stack([x1 * cos - x2 * sin, x1 * sin + x2 * cos], axis=-1)
            return r.reshape(x.shape)

        def _swiglu(x):
            a, b = jnp.split(x, 2, axis=-1)
            return jax.nn.silu(a) * b

        def _rmsnorm(x, w):
            return x * jax.lax.rsqrt(jnp.mean(x * x, axis=-1, keepdims=True) + EPS) * w
        Bb, Tt, C = src.shape
        q = (src @ Wq).reshape(Bb, Tt, H, DH).transpose(0, 2, 1, 3)
        k = (src @ Wk_c @ Wk).reshape(Bb, Tt, H, DH).transpose(0, 2, 1, 3)
        v = (src @ Wv_c @ Wv).reshape(Bb, Tt, H, DH).transpose(0, 2, 1, 3)
        sin, cos = _rope_sincos(Tt, DH)
        q = _apply_rope(q, sin, cos)
        k = _apply_rope(k, sin, cos)
        attn = jnp.einsum('bhqd,bhkd->bhqk', q, k) / np.sqrt(DH).astype(np.float32)
        attn = jax.nn.softmax(attn, axis=-1)
        sa = jnp.einsum('bhqk,bhkd->bhqd', attn, v)
        sa = sa.transpose(0, 2, 1, 3).reshape(Bb, Tt, C) @ Wo
        x = _rmsnorm(src + sa, norm1_w)
        S = Bb * Tt
        flat = x.reshape(S, C)
        shared = _swiglu(flat @ W_shared_in) @ W_shared_out
        g_probs = jax.nn.softmax(flat @ Wg_gate + group_bias, -1)
        g_idx = jnp.argmax(g_probs, axis=-1)
        e_logits = flat @ We_gate + expert_bias
        e_group = jnp.arange(E) // EPG
        in_group = e_group[None, :] == g_idx[:, None]
        e_probs = jax.nn.softmax(jnp.where(in_group, e_logits, -jnp.inf), -1)
        g_prob = jnp.take_along_axis(g_probs, g_idx[:, None], axis=1)
        p_expert = e_probs * g_prob
        topv, topi = jax.lax.top_k(p_expert, TOPK)
        w = jnp.zeros((S, E), flat.dtype).at[jnp.arange(S)[:, None], topi].set(topv)
        h = _swiglu(flat @ W1_shared)
        routed = jnp.zeros_like(shared)
        for e in range(E):
            routed = routed + h @ W2_experts[e] * w[:, e:e + 1]
        out = x + (shared + routed).reshape(Bb, Tt, C)
        return _rmsnorm(out, norm2_w)

    def _L1_attn_a_ref(x, W_qkv, W_o):
        import jax, jax.numpy as jnp
        import numpy as np
        from math import sqrt
        ROPE_BASE = 6000.0

        def _rope_tables(seq_len, rope_dim, dtype):
            inv_freq = 1.0 / ROPE_BASE ** (jnp.arange(0, rope_dim, 2, dtype=jnp.float32) / rope_dim)
            t = jnp.arange(seq_len, dtype=jnp.float32)
            freqs = jnp.outer(t, inv_freq)
            emb = jnp.concatenate([freqs, freqs], axis=-1)
            return (jnp.cos(emb).astype(dtype), jnp.sin(emb).astype(dtype))

        def _rotate_half(x):
            x1, x2 = jnp.split(x, 2, axis=-1)
            return jnp.concatenate([-x2, x1], axis=-1)
        B, S, D = x.shape
        _, H, DK, _ = W_qkv.shape
        rope_dim = DK // 2
        qkv = jnp.einsum('bsm,qhdm->bqhsd', x, W_qkv)
        cos, sin = _rope_tables(S, rope_dim, x.dtype)
        qk = qkv[:, :2, :, :, :rope_dim]
        qk_rot = qk * cos + _rotate_half(qk) * sin
        qkv = qkv.at[:, :2, :, :, :rope_dim].set(qk_rot)
        Q, K, V = (qkv[:, 0], qkv[:, 1], qkv[:, 2])
        scores = jnp.einsum('bhqd,bhkd->bhqk', Q, K)
        causal = jnp.triu(jnp.ones((S, S), dtype=bool), k=1)
        scores = jnp.where(causal, -jnp.inf, scores) / sqrt(DK)
        attn = jax.nn.softmax(scores, axis=-1)
        out = jnp.einsum('bhqk,bhkd->bhqd', attn, V)
        out = out.transpose(0, 2, 1, 3).reshape(B, S, H * DK)
        return jnp.einsum('bsh,dh->bsd', out, W_o)

    def _L1_attn_b_ref(x, Wqkv, bqkv, Wout, bout):
        import jax, jax.numpy as jnp
        import numpy as np
        import math
        DIM = 128
        N_HEADS = 16
        HEAD_DIM = DIM // N_HEADS
        B, S = (2, 256)
        b, s, d = x.shape
        qkv = jnp.einsum('bsd,hde->bhse', x, Wqkv) + bqkv[None, :, None, :]
        q, k, v = jnp.split(qkv, 3, axis=-1)
        score = jnp.einsum('bhsd,bhtd->bhst', q, k)
        causal = jnp.tril(jnp.ones((s, s), dtype=bool))
        score = jnp.where(causal[None, None], score, -jnp.inf)
        attn = jax.nn.softmax(score / jnp.sqrt(jnp.asarray(HEAD_DIM, x.dtype)), axis=-1)
        y = jnp.einsum('bhst,bhtd->bhsd', attn, v)
        y = jnp.transpose(y, (0, 2, 1, 3)).reshape(b, s, d)
        out = y @ Wout + bout
        return out

    def _L1_ffn_ref(x, qweights, scales, biases, lora_a, lora_b, ln_gamma, ln_beta):
        import jax, jax.numpy as jnp
        import numpy as np
        GROUP = 16
        EPS = 1e-05

        def _dequant(q, scale):
            w = q.astype(jnp.float32) / 7.5 - 1.0
            return w * jnp.repeat(scale, GROUP, axis=1)

        def _qlora_linear(x, q, scale, bias, la, lb):
            w = _dequant(q, scale)
            base = jnp.einsum('btd,od->bto', x, w) + bias
            lora = jnp.einsum('btr,or->bto', jnp.einsum('btd,rd->btr', x, la), lb)
            return base + lora

        def _layernorm(x, g, b):
            mu = jnp.mean(x, axis=-1, keepdims=True)
            var = jnp.mean(jnp.square(x - mu), axis=-1, keepdims=True)
            return (x - mu) * jax.lax.rsqrt(var + EPS) * g + b
        h = x
        for blk in range(3):
            i0, i1 = (2 * blk, 2 * blk + 1)
            y = _qlora_linear(h, qweights[i0], scales[i0], biases[i0], lora_a[i0], lora_b[i0])
            y = _layernorm(y, ln_gamma[blk], ln_beta[blk])
            y = jax.nn.gelu(y, approximate=False)
            y = _qlora_linear(y, qweights[i1], scales[i1], biases[i1], lora_a[i1], lora_b[i1])
            h = y + h
        return h
    x = L0_attn_a_x
    x = x + _L0_attn_a_ref(_layernorm(x, axis=-1), L0_attn_a_Wqkv, L0_attn_a_bqkv, L0_attn_a_Wout, L0_attn_a_bout, L0_attn_a_Wimp, L0_attn_a_bimp, L0_attn_a_Walpha, L0_attn_a_balpha, L0_attn_a_spike_threshold, L0_attn_a_log_k, L0_attn_a_qk_scale)
    x = x + _L0_ffn_ref(_layernorm(x, axis=-1), L0_ffn_Wq, L0_ffn_Wk_c, L0_ffn_Wv_c, L0_ffn_Wk, L0_ffn_Wv, L0_ffn_Wo, L0_ffn_W_shared_in, L0_ffn_W_shared_out, L0_ffn_W1_shared, L0_ffn_W2_experts, L0_ffn_Wg_gate, L0_ffn_We_gate, L0_ffn_group_bias, L0_ffn_expert_bias, L0_ffn_norm1_w, L0_ffn_norm2_w)
    x = x + _L0_attn_b_ref(_layernorm(x, axis=-1), L0_attn_b_Wqkv, L0_attn_b_Wout)
    x = x + _L0_ffn_ref(_layernorm(x, axis=-1), L0_ffn_Wq, L0_ffn_Wk_c, L0_ffn_Wv_c, L0_ffn_Wk, L0_ffn_Wv, L0_ffn_Wo, L0_ffn_W_shared_in, L0_ffn_W_shared_out, L0_ffn_W1_shared, L0_ffn_W2_experts, L0_ffn_Wg_gate, L0_ffn_We_gate, L0_ffn_group_bias, L0_ffn_expert_bias, L0_ffn_norm1_w, L0_ffn_norm2_w)
    x = x + _L1_attn_a_ref(_layernorm(x, axis=-1), L1_attn_a_W_qkv, L1_attn_a_W_o)
    x = x + _L1_ffn_ref(_layernorm(x, axis=-1), L1_ffn_qweights, L1_ffn_scales, L1_ffn_biases, L1_ffn_lora_a, L1_ffn_lora_b, L1_ffn_ln_gamma, L1_ffn_ln_beta)
    x = x + _L1_attn_b_ref(_layernorm(x, axis=-1), L1_attn_b_Wqkv, L1_attn_b_bqkv, L1_attn_b_Wout, L1_attn_b_bout)
    x = x + _L1_ffn_ref(_layernorm(x, axis=-1), L1_ffn_qweights, L1_ffn_scales, L1_ffn_biases, L1_ffn_lora_a, L1_ffn_lora_b, L1_ffn_ln_gamma, L1_ffn_ln_beta)
    return x

_drawn_inputs = setup_inputs


def setup_inputs(seed=0):
    import zlib

    import numpy as np

    out = dict(_drawn_inputs(seed))
    spreads = {'L0_attn_a_bqkv': (0.0, 0.536),
     'L0_attn_a_bout': (0.0, 0.1),
     'L0_attn_a_balpha': (0.0, 0.8),
     'L0_attn_a_log_k': (0.5400000214576721, 0.6),
     'L0_ffn_group_bias': (0.0, 0.8),
     'L0_ffn_expert_bias': (0.0, 0.8),
     'L0_ffn_norm1_w': (1.0, 0.2),
     'L0_ffn_norm2_w': (1.0, 0.2),
     'L1_ffn_ln_gamma': (1.0, 0.2),
     'L1_ffn_ln_beta': (0.0, 0.1)}
    factors = {'L0_attn_a_Wqkv': 8.0,
     'L0_attn_a_Wout': 3.621,
     'L0_attn_a_Wimp': 5.165,
     'L0_attn_a_Walpha': 8.0,
     'L0_ffn_Wq': 8.0,
     'L0_ffn_Wk_c': 8.0,
     'L0_ffn_Wv_c': 8.0,
     'L0_ffn_Wk': 8.0,
     'L0_ffn_Wv': 8.0,
     'L0_ffn_Wo': 8.0,
     'L0_ffn_W_shared_in': 8.0,
     'L0_ffn_W_shared_out': 8.0,
     'L0_ffn_W1_shared': 8.0,
     'L0_ffn_W2_experts': 8.0,
     'L0_ffn_Wg_gate': 8.0,
     'L0_ffn_We_gate': 8.0,
     'L1_attn_a_W_qkv': 6.418,
     'L1_attn_a_W_o': 6.835,
     'L1_attn_b_Wqkv': 3.27,
     'L1_attn_b_bqkv': 8.0,
     'L1_attn_b_Wout': 3.222,
     'L1_attn_b_bout': 8.0,
     'L1_ffn_biases': 4.9,
     'L1_ffn_lora_a': 5.353,
     'L1_ffn_lora_b': 5.329}
    for name, (base, spread) in spreads.items():
        noise = np.random.default_rng([zlib.crc32(name.encode()), seed]).standard_normal(out[name].shape)
        drawn = base * np.exp(spread * noise) if base else spread * noise
        out[name] = jnp.asarray(drawn.astype(out[name].dtype))
    for name, factor in factors.items():
        out[name] = (out[name] * factor).astype(out[name].dtype)
    return out
```

```python
from contextlib import ExitStack

import numpy as np

import concourse.bass as bass
from concourse import mybir

F32 = mybir.dt.float32
BF16 = mybir.dt.bfloat16
I32 = mybir.dt.int32
ALU = mybir.AluOpType
ACT = mybir.ActivationFunctionType
AX = mybir.AxisListType.X

P = 128
NB, T = 16, 256
TT = T // P
NT = NB * TT
PAD = 2
H = 16
HC = 4
NC = H // HC
UN = TT * NC
NPAIR = H // 2
LAG_T, LAG_V = 3, 4
PRING, SRING, TRING = 4, 2, 2
QPART = (0, 0, 1, 0, 2, 1)
KPART = (0, 1, 0, 2, 0, 1)
NBLK = len(QPART)
MASKED = -3.0e38


def wait(eng, sem, value):
    if isinstance(value, int) and value <= 0:
        return
    eng.wait_ge(sem, value)


def over_sequences(eng, body, epilogue=None):
    body(0, 0)
    with eng.Fori(0, (NB - 2) // 2) as i:
        body(i * 2 + 1, 1)
        body(i * 2 + 2, 0)
    body(NB - 1, (NB - 1) % 2)
    if epilogue is not None:
        epilogue(NB, NB % 2)


def clear_semaphores(nc, sems):
    with nc.Block() as block:
        @block.gpsimd
        def _(pool):
            for s in sems:
                pool.sem_clear(s)


class Scope:

    def __init__(self, nc, ctx, stage):
        self.nc, self.ctx, self.stage, self.sems = nc, ctx, stage, []

    def sb(self, name, shape, dt=F32):
        return self.ctx.enter_context(self.nc.sbuf_tensor(f"{self.stage}_{name}", shape, dt))

    def ps(self, name, shape, dt=F32):
        return self.ctx.enter_context(self.nc.psum_tensor(f"{self.stage}_{name}", shape, dt))

    def sem(self, name):
        s = self.ctx.enter_context(self.nc.semaphore(f"{self.stage}_{name}"))
        self.sems.append(s)
        return s


class Chain:

    def __init__(self, eng, sem, start=0):
        self.eng, self.sem, self.n = eng, sem, start

    def __call__(self, ins):
        self.n = self.n + 1
        ins.then_inc(self.sem, 1)
        self.eng.wait_ge(self.sem, self.n)


def load_stage(nc, x, g):
    with ExitStack() as ctx:
        st = Scope(nc, ctx, "load")
        x_in, made = st.sem("x_in"), st.sem("constants_made")
        with nc.Block() as block:
            @block.sync
            def _(sp):
                xv = x.rearrange("(n p) d -> p n d", p=P)
                for k in range(4):
                    sp.dma_start(g.X[:, k * 8:(k + 1) * 8, :], xv[:, k * 8:(k + 1) * 8, :]).then_inc(x_in, 16)
                sp.wait_ge(x_in, 64)

            @block.gpsimd
            def _(pool):
                c = Chain(pool, made)
                c(pool.memset(g.ident[:, :], 0.0))
                c(pool.affine_select(out=g.ident[:, :], in_=g.ident[:, :], compare_op=ALU.not_equal, fill=1.0,
                                     base=0, pattern=[[-1, P]], channel_multiplier=1))
                c(pool.tensor_copy(g.identb[:, :], g.ident[:, :]))
                c(pool.memset(g.maskb[:, :, :], 0.0))
                c(pool.affine_select(out=g.maskb[:, :, :], in_=g.maskb[:, :, :], compare_op=ALU.is_ge, fill=MASKED,
                                     base=0, pattern=[[0, 2], [-1, P]], channel_multiplier=1))
                c(pool.memset(g.neghalf[:, :], -0.5))
                c(pool.memset(g.half[:, :], 0.5))
                c(pool.memset(g.X[:, NT:, :], 0.0))
                c(pool.memset(g.bn6[:, :], 0.0))
        clear = list(st.sems)
        clear_semaphores(nc, clear)


def moments_sems(st):
    st.bn_done, st.moment_step = st.sem("bn_done"), st.sem("moment_step")
    st.var_ready, st.rstd_ready, st.mean_ready = st.sem("var_ready"), st.sem("rstd_ready"), st.sem("mean_ready")


def halves_vector(dve, g, st, src, ntiles):
    with dve.Fori(0, ntiles // 2) as i:
        for k in range(2):
            g.nc.vector.bn_stats(g.bn6[:, bass.ds(i * 12 + 6 * k, 6)], src[:, bass.ds(i * 2 + k, 1), :]
                                 ).then_inc(st.bn_done, 1)


def moments_vector(dve, g, st, eps, bn_count, turn=0, rms=False):
    nc = g.nc
    six = g.bn6[:, :].rearrange("p (n k) -> p n k", k=6)
    mean_e, sq_e, mean_o, sq_o = six[:, :, 1], six[:, :, 2], six[:, :, 4], six[:, :, 5]
    dve.wait_ge(st.bn_done, bn_count)
    step = Chain(dve, st.moment_step, 5 * turn)
    nc.vector.tensor_tensor(g.mean[:, :], mean_e, mean_o, ALU.mult if rms else ALU.add).then_inc(st.moment_step, 1)
    nc.vector.tensor_tensor(g.rstd[:, :], sq_e, sq_o, ALU.add).then_inc(st.moment_step, 1)
    step.n = step.n + 2
    step(nc.vector.tensor_tensor(g.gap[:, :], mean_e, mean_o, ALU.subtract))
    nc.vector.tensor_scalar(g.rstd[:, :], g.rstd[:, :], 1.0 / P, eps, ALU.mult, ALU.add).then_inc(st.moment_step, 1)
    step.n = step.n + 1
    step(nc.vector.tensor_tensor(g.gap[:, :], g.gap[:, :], g.gap[:, :], ALU.mult))
    if rms:
        nc.vector.scalar_tensor_tensor(out=g.mean[:, :], in0=g.gap[:, :], scalar=0.5, in1=g.mean[:, :],
                                       op0=ALU.mult, op1=ALU.add).then_inc(st.mean_ready, 1)
        dve.wait_ge(st.mean_ready, turn + 1)
        nc.vector.tensor_tensor(g.rstd[:, :], g.rstd[:, :], g.mean[:, :], ALU.add).then_inc(st.var_ready, 1)
    else:
        nc.vector.tensor_scalar(g.mean[:, :], g.mean[:, :], 0.5, None, ALU.mult).then_inc(st.mean_ready, 1)
        nc.vector.scalar_tensor_tensor(out=g.rstd[:, :], in0=g.gap[:, :], scalar=0.25, in1=g.rstd[:, :],
                                       op0=ALU.mult, op1=ALU.add).then_inc(st.var_ready, 1)
        dve.wait_ge(st.mean_ready, turn + 1)
    dve.wait_ge(st.rstd_ready, turn + 1)


def moments_pool(pool, g, st, turn=0):
    pool.wait_ge(st.var_ready, turn + 1)
    g.nc.gpsimd.tensor_tensor(g.rstd[:, :], g.rstd[:, :], g.neghalf[:, 0:NT + 2 * PAD], ALU.pow).then_inc(st.rstd_ready, 1)


def load_weights(sp, sem, pairs):
    for dst, src in pairs:
        sp.dma_start(dst[tuple(slice(None) for _ in dst.shape)], src).then_inc(sem, 16)
    sp.wait_ge(sem, 16 * len(pairs))


def in_order(eng, body, lag):
    body(0, 0)
    body(1, 1)
    with eng.Fori(0, (NB - 2) // 2) as i:
        body(i * 2 + 2, 0)
        body(i * 2 + 3, 1)
    for k in range(lag):
        body(NB + k, k % 2)


def there(b, lag):
    return not isinstance(b, int) or 0 <= b - lag < NB


def attention_stage(nc, g, w, *, causal, rope=False, bias=False, moe=False, name):
    with ExitStack() as ctx:
        st = Scope(nc, ctx, name)
        sb, ps, sem = st.sb, st.ps, st.sem
        wq, wk, wv = sb("wq", [P, P]), sb("wk", [P, P]), sb("wv", [P, P])
        wo = sb("wo", [P, NC, P])
        if rope:
            wqs, wks = sb("wqs", [P, P]), sb("wks", [P, P])
            wkcT, wvcT = sb("wkcT", [32, P]), sb("wvcT", [32, P])
            wk2, wks2, wv2 = sb("wk2", [32, P]), sb("wks2", [32, P]), sb("wv2", [32, P])
            cosT, sinT = sb("cosT", [P, 2, T]), sb("sinT", [P, 2, T])
            roc, ros = sb("roc", [P, 2 * T]), sb("ros", [P, 2 * T])
        if bias:
            bq, bk, bv = sb("bq", [P, 1]), sb("bk", [P, 1]), sb("bv", [P, P])
            bo = sb("bo", [P, P])
        xs = sb("xs", [P, 2, TT, P])
        xnT = sb("xnT", [P, 2, T])
        qkf, resid = sb("qkf", [P, 2 * T]), sb("resid", [P, 2 * T])
        parts = sb("parts", [P, 2, 3, 2 * T], BF16)
        KROWS = NBLK * 16
        qst = [sb(f"qst{i}", [KROWS, NPAIR, T], BF16) for i in range(2)]
        kst = [sb(f"kst{i}", [KROWS, NPAIR, 2, T], BF16) for i in range(2)]
        vp = [sb(f"vp{i}", [P, TT, H, 32]) for i in range(2)]
        probs = sb("probs", [P, PRING, HC, T])
        probsT = sb("probsT", [P, TRING, TT, HC * P])
        negmax, rowsum, rinv = sb("negmax", [P, PRING, HC]), sb("rowsum", [P, PRING, HC]), sb("rinv", [P, PRING, HC])
        osb = sb("osb", [P, TT, NC, P])
        S = [ps(f"S{i}", [P, HC * T]) for i in range(SRING)]
        PT = ps("PT", [P, TT, HC * P])
        O = ps("O", [P, NC, P])
        M = ps("M", [P, 512])
        moments_sems(st)
        w_in, kz_ready, vz_ready = sem("weights_in"), sem("kst_zeroed"), sem("vp_zeroed")
        wc_ready, wc_copied = sem("weights_multiplied"), sem("weights_copied")
        xs_ready, xT_ready, xT_copied = sem("xs_ready"), sem("xT_ready"), sem("xT_copied")
        qk_ready, qk_copied = sem("qk_ready"), sem("qk_copied")
        rot_ready, rot_used = sem("rot_ready"), sem("rot_used")
        hi_ready, res_ready, parts_ready = sem("hi_ready"), sem("residue_ready"), sem("parts_ready")
        parts_out, st_in = sem("parts_out"), [sem("stacks_in0"), sem("stacks_in1")]
        v_ready, v_copied = sem("v_ready"), sem("v_copied")
        s_ready, max_ready, exp_done = sem("s_ready"), sem("max_ready"), sem("exp_done")
        rinv_ready, norm_done, t_ready = sem("rinv_ready"), sem("norm_done"), sem("t_ready")
        t_copied, pv_done, o_copied = sem("t_copied"), sem("pv_done"), sem("o_copied")
        proj_ready, proj_used = sem("proj_ready"), sem("proj_used")
        mine = sem("vector_chain")
        scr = g.scratch
        NIN = NBLK * 3

        def keys(u):
            return 1 if causal and u // NC == 0 else TT

        def split(b, u, lag):
            return (b, u - lag, 0) if u >= lag else (b - 1, u - lag + UN, 1)

        def exists(b, u, lag):
            return not (isinstance(b, int) and UN * b + u - lag < 0)

        def s_view(u):
            n = keys(u) * P
            return S[u % SRING][:, 0:HC * n].rearrange("p (h k) -> p h k", h=HC)

        wloads = [(wq, w["wq"]), (wo, w["wo"])]
        if rope:
            wloads += [(wqs, w["wqs"]), (wkcT, w["wkcT"]), (wvcT, w["wvcT"]), (wk2, w["wk"]), (wks2, w["wks"]),
                       (wv2, w["wv"]), (cosT, w["cosT"]), (sinT, w["sinT"])]
        else:
            wloads += [(wk, w["wk"]), (wv, w["wv"])]
        if bias:
            wloads += [(bq, w["bq"]), (bk, w["bk"]), (bv, w["bv"]), (bo, w["bo"])]
        WIN = 16 * len(wloads)

        with nc.Block() as block:
            @block.sync
            def _(sp):
                load_weights(sp, w_in, wloads)
                for i in range(2):
                    sp.wait_ge(kz_ready, i + 1)

                def counts(j, par):
                    v = (j + 1, (j - par) * (8 * NIN), j * UN - UN, j * 16 + 16)
                    return v if isinstance(j, int) else tuple(sp.to_reg(x) for x in v)

                def bounce(par, first, n):
                    split_n, read_n, used_n, out_n = n
                    wait(sp, parts_ready, split_n)
                    wait(sp, st_in[par], read_n)
                    sp.dma_start(scr[par].rearrange("a p n -> p a n"), parts[:, par, :, :]).then_inc(parts_out, 16)
                    if not first:
                        sp.wait_ge(s_ready, used_n)
                    wait(sp, parts_out, out_n)
                    for i in range(NBLK):
                        r = 16 * i
                        sp.dma_start(qst[par][r:r + 16, :, :],
                                     scr[par, QPART[i], :, 0:T].rearrange("(c r) t -> r c t", r=16)
                                     ).then_inc(st_in[par], 16)
                        for hh in range(2):
                            src = scr[par, KPART[i], :, T:2 * T].rearrange("(c h d) t -> h d c t", h=2, d=8)
                            sp.dma_start(kst[par][r + 8 * hh:r + 8 * hh + 8, :, hh, :], src[hh]
                                         ).then_inc(st_in[par], 16)

                bounce(0, True, counts(0, 0))
                bounce(1, True, counts(1, 1))
                bounce(0, False, counts(2, 0))
                with sp.Fori(0, (NB - 2) // 2) as i:
                    odd, even = counts(i * 2 + 3, 1), counts(i * 2 + 4, 0)
                    bounce(1, False, odd)
                    bounce(0, False, even)
                bounce(1, False, counts(NB + 1, 1))
                sp.wait_ge(parts_out, 16 * (NB + PAD))
                for i in range(2):
                    sp.wait_ge(st_in[i], 16 * NIN * (NB + PAD) // 2)

            @block.gpsimd
            def _(pool):
                for i in range(2):
                    nc.gpsimd.memset(kst[i][:, :, :, :], 0.0).then_inc(kz_ready, 1)
                for i in range(2):
                    nc.gpsimd.memset(vp[i][:, :, :, :], 0.0).then_inc(vz_ready, 1)
                moments_pool(pool, g, st)

                def slot(b, u):
                    if not exists(b, u, 1):
                        return
                    sq, v, _ = split(b, u, 1)
                    r, nk = v % PRING, keys(v) * P
                    wait(pool, rinv_ready, sq * UN + v + 1)
                    pr = probs[:, r, :, 0:nk]
                    nc.gpsimd.tensor_tensor(pr, pr, rinv[:, r, :].unsqueeze(2).broadcast_to([P, HC, nk]),
                                            ALU.mult).then_inc(norm_done, 1)

                over_sequences(pool, lambda b, par: [slot(b, u) for u in range(UN)],
                               lambda b, par: slot(b, 0))

            @block.tensor
            def _(pe):
                pe.wait_ge(w_in, WIN)
                if rope:
                    for k, (a, c) in enumerate(((wkcT, wk2), (wkcT, wks2), (wvcT, wv2))):
                        ins = nc.tensor.matmul(M[:, k * P:(k + 1) * P], a[:, :], c[:, :], start=True, stop=True)
                    ins.then_inc(wc_ready, 1)
                    pe.wait_ge(wc_copied, 1)

                def x_transposes(j, par):
                    wait(pe, xs_ready, j + 1)
                    wait(pe, qk_copied, j)
                    wait(pe, v_copied, j - 1)
                    wait(pe, proj_used, 2 * j - 5)
                    for t in range(TT):
                        ins = nc.tensor.transpose(M[:, t * P:(t + 1) * P], xs[:, par, t, :], g.ident[:, :])
                    ins.then_inc(xT_ready, 1)

                def qk_projections(j, par):
                    wait(pe, xT_copied, j + 1)
                    nc.tensor.matmul(M[:, 0:T], wq[:, :], xnT[:, par, :], start=True, stop=True)
                    nc.tensor.matmul(M[:, T:2 * T], wk[:, :], xnT[:, par, :], start=True, stop=True
                                     ).then_inc(qk_ready, 1)

                def swapped_projections(j, par):
                    wait(pe, rot_used, 2 * j + 1)
                    nc.tensor.matmul(M[:, 0:T], wqs[:, :], xnT[:, par, :], start=True, stop=True)
                    nc.tensor.matmul(M[:, T:2 * T], wks[:, :], xnT[:, par, :], start=True, stop=True
                                     ).then_inc(rot_ready, 1)

                def v_projection(j, par, fronts):
                    wait(pe, qk_copied, fronts)
                    for t in range(TT):
                        ins = nc.tensor.matmul(M[:, t * P:(t + 1) * P], xnT[:, par, t * P:(t + 1) * P], wv[:, :],
                                               start=True, stop=True)
                    ins.then_inc(v_ready, 1)

                def out_projection(j, t, vs):
                    wait(pe, o_copied, 2 * j + t + 1)
                    wait(pe, proj_used, 2 * j + t)
                    wait(pe, v_copied, vs)
                    for c in range(NC):
                        ins = nc.tensor.matmul(M[:, 0:P], osb[:, t, c, :], wo[:, c, :], start=c == 0, stop=c == NC - 1)
                    ins.then_inc(proj_ready, 1)

                def transposes(b, u):
                    if not exists(b, u, LAG_T):
                        return
                    sq, v, _ = split(b, u, LAG_T)
                    n = sq * UN + v
                    wait(pe, norm_done, n + 1)
                    wait(pe, t_copied, n)
                    for kt in range(keys(v)):
                        for h in range(HC):
                            ins = nc.tensor.transpose(PT[:, kt, h * P:(h + 1) * P],
                                                      probs[:, v % PRING, h, kt * P:(kt + 1) * P], g.ident[:, :])
                    ins.then_inc(t_ready, 1)

                def scores(b, u, par):
                    if u == 0:
                        wait(pe, st_in[par], (b - par) * (8 * NIN) + 16 * NIN)
                    wait(pe, exp_done, UN * b + u - SRING + 1)
                    t, c, nk = u // NC, u % NC, keys(u) * P
                    out = s_view(u)
                    for i in range(HC // 2):
                        o2 = out[:, 2 * i:2 * i + 2, :]
                        ins = nc.tensor.matmul(o2, qst[par][:, 2 * c + i, t * P:(t + 1) * P],
                                               kst[par][:, 2 * c + i, :, 0:nk], start=True, stop=True)
                        if causal:
                            ins = nc.tensor.matmul(o2[:, :, t * P:(t + 1) * P], g.identb[:, :], g.maskb[:, :, :],
                                                   start=False, stop=True, skip_group_check=True)
                    ins.then_inc(s_ready, 1)

                def values(b, u, par):
                    if not exists(b, u, LAG_V):
                        return
                    sq, v, shift = split(b, u, LAG_V)
                    n, c, t = sq * UN + v, v % NC, v // NC
                    wait(pe, t_copied, n + 1)
                    if v == 0:
                        wait(pe, v_copied, sq + 1)
                    if c == 0:
                        wait(pe, o_copied, 2 * sq + t)
                    vv = vp[par ^ shift]
                    nk = keys(v)
                    for kt in range(nk):
                        for h in range(HC):
                            ins = nc.tensor.matmul(O[32 * h:32 * h + 32, c, :], vv[:, kt, HC * c + h, :],
                                                   probsT[:, v % TRING, kt, h * P:(h + 1) * P],
                                                   start=kt == 0, stop=kt == nk - 1, tile_position=(0, 32 * h))
                    ins.then_inc(pv_done, 1)

                def front(j, par):
                    x_transposes(j, par)
                    qk_projections(j, par)
                    if rope:
                        swapped_projections(j, par)

                front(0, 0)
                front(1, 1)
                v_projection(0, 0, 2)

                def body(b, par):
                    for u in range(UN):
                        transposes(b, u)
                        scores(b, u, par)
                        values(b, u, par)
                        if u == 1 and exists(b, 0, 1):
                            out_projection(b - 1, 0, b + 1)
                        if u == 2:
                            x_transposes(b + 2, par)
                        if u == 3:
                            qk_projections(b + 2, par)
                        if u == 4 and rope:
                            swapped_projections(b + 2, par)
                        if u == 5:
                            v_projection(b + 1, par ^ 1, b + 3)
                        if u == 6 and exists(b, 0, 1):
                            out_projection(b - 1, 1, b + 2)

                def rest(b, par):
                    for u in range(LAG_V):
                        if u < LAG_T:
                            transposes(b, u)
                        values(b, u, par)
                    for t in range(TT):
                        out_projection(b - 1, t, b + 1)

                over_sequences(pe, body, rest)

            @block.scalar
            def _(act):
                if rope:
                    act.wait_ge(wc_ready, 1)
                    for k, dst in enumerate((wk, wks, wv)):
                        ins = nc.scalar.activation(dst[:, :], M[:, k * P:(k + 1) * P], ACT.Copy)
                    ins.then_inc(wc_copied, 1)
                act.wait_ge(w_in, WIN)
                if bias:
                    nc.scalar.activation(bq[:, :], bq[:, :], ACT.Copy, scale=g.score_scale).then_inc(wc_copied, 1)
                    act.wait_ge(wc_copied, 1)

                def exponentials(b, u):
                    n, r, v = UN * b + u, u % PRING, s_view(u)
                    wait(act, max_ready, n + 1)
                    wait(act, t_ready, n - PRING + 1)
                    for h in range(HC):
                        ins = nc.scalar.activation(probs[:, r, h, 0:keys(u) * P], v[:, h, :], ACT.Exp,
                                                   bias=negmax[:, r, h:h + 1], accum_out=rowsum[:, r, h:h + 1])
                    ins.then_inc(exp_done, 1)

                def x_copy(j, par):
                    wait(act, xT_ready, j + 1)
                    nc.scalar.activation(xnT[:, par, :], M[:, 0:T], ACT.Copy).then_inc(xT_copied, 1)

                def qk_copy(j, par):
                    if not rope:
                        wait(act, qk_ready, j + 1)
                        wait(act, parts_ready, j)
                        if bias:
                            nc.scalar.activation(qkf[:, 0:T], M[:, 0:T], ACT.Identity, scale=g.score_scale,
                                                 bias=bq[:, 0:1]).then_inc(hi_ready, 1)
                            nc.scalar.activation(qkf[:, T:2 * T], M[:, T:2 * T], ACT.Identity, bias=bk[:, 0:1]
                                                 ).then_inc(qk_copied, 1)
                        else:
                            nc.scalar.activation(qkf[:, 0:T], M[:, 0:T], ACT.Copy, scale=g.score_scale
                                                 ).then_inc(hi_ready, 1)
                            nc.scalar.activation(qkf[:, T:2 * T], M[:, T:2 * T], ACT.Copy).then_inc(qk_copied, 1)
                        wait(act, hi_ready, 2 * j + 1)
                    wait(act, qk_copied, j + 1)
                    wait(act, parts_out, (j - 1) * 16)
                    nc.scalar.activation(parts[:, par, 0, :], qkf[:, :], ACT.Copy).then_inc(hi_ready, 1)

                def v_copy(j, par):
                    if bias:
                        return
                    wait(act, v_ready, j + 1)
                    if isinstance(j, int) and j < 2:
                        wait(act, vz_ready, j + 1)
                    wait(act, pv_done, UN * (j - 1))
                    nc.scalar.activation(vp[par][:, :, :, 0:8],
                                         M[:, 0:T].rearrange("p (t h d) -> p t h d", t=TT, h=H), ACT.Copy
                                         ).then_inc(v_copied, 1)

                def o_copy(sq, t):
                    wait(act, pv_done, sq * UN + (t + 1) * NC)
                    wait(act, proj_ready, 2 * sq + t - 1)
                    nc.scalar.activation(osb[:, t, :, :], O[:, :, :], ACT.Copy).then_inc(o_copied, 1)

                for j in range(2):
                    x_copy(j, j)
                    qk_copy(j, j)
                v_copy(0, 0)

                def body(b, par):
                    for u in range(UN):
                        exponentials(b, u)
                        if u == 2:
                            x_copy(b + 2, par)
                        if u == 3:
                            if exists(b, 0, 1):
                                o_copy(b - 1, 1)
                        if u == (5 if rope else 4):
                            qk_copy(b + 2, par)
                        if u == 5:
                            v_copy(b + 1, par ^ 1)
                        if u == 7:
                            o_copy(b, 0)

                over_sequences(act, body, lambda b, par: o_copy(b - 1, 1))

            @block.vector
            def _(dve):
                halves_vector(dve, g, st, g.X, NT + 2 * PAD)
                moments_vector(dve, g, st, 1e-5, NT + 2 * PAD)
                dve.wait_ge(w_in, WIN)

                def x_normalise(j, par):
                    wait(dve, xT_ready, j - 1)
                    for t in range(TT):
                        tile = j * TT + t
                        src = g.X[:, bass.ds(tile, 1), :]
                        mean = g.mean[:, bass.ds(tile, 1)]
                        rs = g.rstd[:, bass.ds(tile, 1)]
                        if moe:
                            nc.vector.tensor_scalar(g.XP[:, bass.ds(tile, 1), :], src, mean, rs, ALU.subtract,
                                                    ALU.mult).then_inc(mine, 1)
                        ins = nc.vector.tensor_scalar(xs[:, par, t:t + 1, :], src, mean, rs, ALU.subtract, ALU.mult)
                    ins.then_inc(xs_ready, 1)

                def rotate(j, par, part):
                    if part == 0:
                        wait(dve, qk_ready, j + 1)
                        wait(dve, rot_used, 2 * j)
                        wait(dve, qk_copied, j)
                        nc.vector.tensor_tensor(roc[:, :], M[:, :], cosT[:, :, :].rearrange("p a t -> p (a t)"),
                                                ALU.mult).then_inc(rot_used, 1)
                    else:
                        wait(dve, rot_ready, j + 1)
                        nc.vector.tensor_tensor(ros[:, :], M[:, :], sinT[:, :, :].rearrange("p a t -> p (a t)"),
                                                ALU.mult).then_inc(rot_used, 1)
                        wait(dve, rot_used, 2 * j + 2)
                        wait(dve, parts_ready, j)
                        nc.vector.tensor_tensor(qkf[:, :], roc[:, :], ros[:, :], ALU.add).then_inc(qk_copied, 1)

                def split_parts(j, par):
                    wait(dve, hi_ready, (j + 1) * (1 if rope else 2))
                    wait(dve, res_ready, 2 * j)
                    nc.vector.tensor_tensor(resid[:, :], qkf[:, :], parts[:, par, 0, :], ALU.subtract
                                            ).then_inc(res_ready, 1)
                    wait(dve, res_ready, 2 * j + 1)
                    nc.vector.tensor_copy(parts[:, par, 1, :], resid[:, :]).then_inc(res_ready, 1)
                    wait(dve, res_ready, 2 * j + 2)
                    nc.vector.tensor_tensor(parts[:, par, 2, :], resid[:, :], parts[:, par, 1, :], ALU.subtract
                                            ).then_inc(parts_ready, 1)

                def v_copy(j, par):
                    if not bias:
                        return
                    wait(dve, v_ready, j + 1)
                    if isinstance(j, int) and j < 2:
                        wait(dve, vz_ready, j + 1)
                    wait(dve, pv_done, UN * (j - 1))
                    bvb = bv[:, :].rearrange("p (h d) -> p h d", h=H)
                    for t in range(TT):
                        ins = nc.vector.tensor_tensor(vp[par][:, t, :, 0:8],
                                                      M[:, t * P:(t + 1) * P].rearrange("p (h d) -> p h d", h=H),
                                                      bvb, ALU.add)
                    ins.then_inc(v_copied, 1)

                def maxima(b, u):
                    n = UN * b + u
                    wait(dve, s_ready, n + 1)
                    wait(dve, exp_done, n - PRING + 1)
                    nc.vector.tensor_reduce(out=negmax[:, u % PRING, :], in_=s_view(u), axis=AX, op=ALU.max,
                                            negate=True).then_inc(max_ready, 1)

                def reciprocals(b, u):
                    if not exists(b, u, 1):
                        return
                    sq, v, _ = split(b, u, 1)
                    n, r = sq * UN + v, v % PRING
                    wait(dve, exp_done, n + 1)
                    wait(dve, norm_done, n - PRING + 1)
                    nc.vector.reciprocal(rinv[:, r, :], rowsum[:, r, :]).then_inc(rinv_ready, 1)

                def t_copy(b, u):
                    if not exists(b, u, LAG_T):
                        return
                    sq, v, _ = split(b, u, LAG_T)
                    n = sq * UN + v
                    wait(dve, t_ready, n + 1)
                    wait(dve, pv_done, n - TRING + 1)
                    nk = keys(v)
                    nc.vector.tensor_copy(probsT[:, v % TRING, 0:nk, :], PT[:, 0:nk, :]).then_inc(t_copied, 1)

                def residual(sq, t):
                    tile = sq * TT + t
                    wait(dve, proj_ready, 2 * sq + t + 1)
                    dst = (g.XP if moe else g.X)[:, bass.ds(tile, 1), :]
                    if moe:
                        wait(dve, mine, 2 * sq + 2)
                    if bias:
                        nc.vector.tensor_tensor(dst, dst, bo[:, :].unsqueeze(1), ALU.add).then_inc(mine, 1)
                        wait(dve, mine, 2 * sq + t + 1)
                    nc.vector.tensor_tensor(dst, dst, M[:, 0:P].unsqueeze(1), ALU.add).then_inc(proj_used, 1)

                for j in range(2):
                    x_normalise(j, j)
                for j in range(2):
                    if rope:
                        rotate(j, j, 0)
                        rotate(j, j, 1)
                    split_parts(j, j)
                v_copy(0, 0)

                def body(b, par):
                    for u in range(UN):
                        t_copy(b, u)
                        maxima(b, u)
                        reciprocals(b, u)
                        if u == 0:
                            x_normalise(b + 2, par)
                        if u == 1 and exists(b, 0, 1):
                            residual(b - 1, 0)
                        if rope and u == 4:
                            rotate(b + 2, par, 0)
                            rotate(b + 2, par, 1)
                        if u == 5:
                            v_copy(b + 1, par ^ 1)
                        if u == (6 if rope else 5):
                            split_parts(b + 2, par)
                        if u == 7 and exists(b, 0, 1):
                            residual(b - 1, 1)

                def rest(b, par):
                    reciprocals(b, 0)
                    for u in range(LAG_T):
                        t_copy(b, u)
                    for t in range(TT):
                        residual(b - 1, t)

                over_sequences(dve, body, rest)
        clear = list(st.sems)
        clear_semaphores(nc, clear)


def wide_attention_stage(nc, g, w, name):
    DH = 64
    with ExitStack() as ctx:
        st = Scope(nc, ctx, name)
        sb, ps, sem = st.sb, st.ps, st.sem
        wqk = [sb(f"w{n}", [P, NPAIR, P]) for n in ("q", "qs", "k", "ks")]
        wv, wo = sb("wv", [P, H * DH]), sb("wo", [P, NPAIR, P])
        turn = [sb("turn_q", [P, 2 * T]), sb("turn_k", [P, 2 * T])]
        xs, xnT = sb("xs", [P, 2, TT, P]), sb("xnT", [P, T])
        NTMP = 4
        tmp = sb("tmp", [P, NTMP, 2 * T])
        qw = [sb(f"qw{i}", [P, NPAIR, T]) for i in range(2)]
        kw = [sb(f"kw{i}", [P, NPAIR, 2, T]) for i in range(2)]
        vw = [sb(f"vw{i}", [P, TT, H, DH]) for i in range(2)]
        probs, probsT = sb("probs", [P, PRING, HC, T]), sb("probsT", [P, TRING, TT, HC * P])
        negmax, rowsum, rinv = sb("negmax", [P, PRING, HC]), sb("rowsum", [P, PRING, HC]), sb("rinv", [P, PRING, HC])
        osb = sb("osb", [P, TT, NPAIR, P])
        S = [ps(f"S{i}", [P, HC * T]) for i in range(SRING)]
        PT, O, M = ps("PT", [P, TT, HC * P]), ps("O", [P, 4, P]), ps("M", [P, 512])
        moments_sems(st)
        w_in, kw_zeroed = sem("weights_in"), sem("kw_zeroed")
        xs_ready, m_ready, m_read, qk_ready = sem("xs_ready"), sem("job_ready"), sem("job_read"), sem("qk_ready")
        s_ready, max_ready, exp_done = sem("s_ready"), sem("max_ready"), sem("exp_done")
        rinv_ready, norm_done, t_ready = sem("rinv_ready"), sem("norm_done"), sem("t_ready")
        t_copied, pv_done, o_copied = sem("t_copied"), sem("pv_done"), sem("o_copied")

        FRONT = [[("x", 0), ("q", 0), ("k", 0)], [("q", 1), ("k", 1)], [("q", 2), ("k", 2), ("q", 3)],
                 [("k", 3), ("q", 4), ("k", 4)], [("q", 5), ("k", 5), ("q", 6)], [("k", 6), ("q", 7)],
                 [("k", 7), ("v", 0), ("v", 1)], [("v", 2), ("v", 3)]]
        OUT = {1: ("o", 0), 5: ("o", 1)}
        FIRST = [j for slot in FRONT for j in slot]
        NF, NJ = len(FIRST), len(FIRST) + len(OUT)
        OUT_PLACE = [sum(len(FRONT[x]) + (x in OUT) for x in range(u + 1)) - 1 for u in OUT]

        NADD = 3 * NPAIR

        def adds(k):
            return 3 * (k // 2) + k % 2

        def base(b):
            return NF if isinstance(b, int) and b == 0 else b * NJ + (2 * NF - NJ)

        def jobs(b, u):
            first = isinstance(b, int) and b == 0
            before = sum(len(FRONT[x]) + (x in OUT and not first) for x in range(u))
            todo = FRONT[u] + ([OUT[u]] if u in OUT and not first else [])
            return [(job, base(b) + before + k) for k, job in enumerate(todo)]

        def keys(u):
            return 1 if u // NC == 0 else TT

        def split(b, u, lag):
            return (b, u - lag, 0) if u >= lag else (b - 1, u - lag + UN, 1)

        def exists(b, u, lag):
            return not (isinstance(b, int) and UN * b + u - lag < 0)

        def s_view(u):
            n = keys(u) * P
            return S[u % SRING][:, 0:HC * n].rearrange("p (h k) -> p h k", h=HC)

        loads = list(zip(wqk, (w["wq"], w["wqs"], w["wk"], w["wks"]))) + [
            (wv, w["wv"]), (wo, w["wo"]), (turn[0], w["turn_q"]), (turn[1], w["turn_k"])]

        with nc.Block() as block:
            @block.sync
            def _(sp):
                load_weights(sp, w_in, loads)

            @block.gpsimd
            def _(pool):
                for i in range(2):
                    nc.gpsimd.memset(kw[i][:, :, :, :], 0.0).then_inc(kw_zeroed, 1)
                moments_pool(pool, g, st)
                pool.wait_ge(kw_zeroed, 2)

                def add_turned(j, par, job, number, normalised):
                    kind, p = job
                    k = 2 * p + (kind == "k")
                    wait(pool, m_read, number + 1)
                    a, c = tmp[:, k % NTMP, 0:T], tmp[:, k % NTMP, T:2 * T]
                    wait(pool, s_ready, UN * (j - 1))
                    if kind == "q":
                        wait(pool, qk_ready, j * NADD + adds(k))
                        nc.gpsimd.tensor_tensor(qw[par][:, p, :], a, c, ALU.add).then_inc(qk_ready, 1)
                    else:
                        wait(pool, norm_done, normalised)
                        for hh in range(2):
                            wait(pool, qk_ready, j * NADD + adds(k) + hh)
                            r = slice(DH * hh, DH * hh + DH)
                            nc.gpsimd.tensor_tensor(kw[par][r, p, hh, :], a[r, :], c[r, :], ALU.add
                                                    ).then_inc(qk_ready, 1)

                def normalise(b, u):
                    if not exists(b, u, 1):
                        return
                    sq, v, _ = split(b, u, 1)
                    r, nk = v % PRING, keys(v) * P
                    added = sum(job[0] in "qk" for x in range(u) for job in FRONT[x])
                    wait(pool, qk_ready, (b + 1) * NADD + adds(added))
                    wait(pool, rinv_ready, sq * UN + v + 1)
                    pr = probs[:, r, :, 0:nk]
                    nc.gpsimd.tensor_tensor(pr, pr, rinv[:, r, :].unsqueeze(2).broadcast_to([P, HC, nk]),
                                            ALU.mult).then_inc(norm_done, 1)

                for n, job in enumerate(FIRST):
                    if job[0] in "qk":
                        add_turned(0, 0, job, n, 0)

                def body(b, par):
                    for u in range(UN):
                        normalise(b, u)
                        for job, n in jobs(b, u):
                            if job[0] in "qk":
                                add_turned(b + 1, par ^ 1, job, n, b * UN + u)

                over_sequences(pool, body, lambda b, par: normalise(b, 0))

            @block.tensor
            def _(pe):
                pe.wait_ge(w_in, 16 * len(loads))

                def run(job, n, j, par):
                    kind, k = job
                    wait(pe, m_read, n)
                    if kind == "x":
                        wait(pe, xs_ready, j + 1)
                        for t in range(TT):
                            ins = nc.tensor.transpose(M[:, t * P:(t + 1) * P], xs[:, par, t, :], g.ident[:, :])
                    elif kind in "qk":
                        for s in range(2):
                            ins = nc.tensor.matmul(M[:, s * T:(s + 1) * T], wqk[2 * "qk".index(kind) + s][:, k, :],
                                                   xnT[:, :], start=True, stop=True)
                    elif kind == "v":
                        t, half = k // 2, k % 2
                        ins = nc.tensor.matmul(M[:, :], xnT[:, t * P:(t + 1) * P], wv[:, half * 512:(half + 1) * 512],
                                               start=True, stop=True)
                    else:
                        wait(pe, o_copied, (j - 2) * 4 + 2 * k + 2)
                        for p in range(NPAIR):
                            ins = nc.tensor.matmul(M[:, 0:P], osb[:, k, p, :], wo[:, p, :], start=p == 0,
                                                   stop=p == NPAIR - 1)
                    ins.then_inc(m_ready, 1)

                def transposes(b, u):
                    if not exists(b, u, LAG_T):
                        return
                    sq, v, _ = split(b, u, LAG_T)
                    n = sq * UN + v
                    wait(pe, norm_done, n + 1)
                    wait(pe, t_copied, n)
                    for kt in range(keys(v)):
                        for h in range(HC):
                            ins = nc.tensor.transpose(PT[:, kt, h * P:(h + 1) * P],
                                                      probs[:, v % PRING, h, kt * P:(kt + 1) * P], g.ident[:, :])
                    ins.then_inc(t_ready, 1)

                def scores(b, u, par):
                    if u == 0:
                        wait(pe, qk_ready, (b + 1) * NADD)
                    wait(pe, exp_done, UN * b + u - SRING + 1)
                    t, c, nk = u // NC, u % NC, keys(u) * P
                    out = s_view(u)
                    for i in range(HC // 2):
                        o2 = out[:, 2 * i:2 * i + 2, :]
                        nc.tensor.matmul(o2, qw[par][:, 2 * c + i, t * P:(t + 1) * P], kw[par][:, 2 * c + i, :, 0:nk],
                                         start=True, stop=True)
                        ins = nc.tensor.matmul(o2[:, :, t * P:(t + 1) * P], g.identb[:, :], g.maskb[:, :, :],
                                               start=False, stop=True, skip_group_check=True)
                    ins.then_inc(s_ready, 1)

                def values(b, u, par):
                    if not exists(b, u, LAG_V):
                        return
                    sq, v, shift = split(b, u, LAG_V)
                    n, c = sq * UN + v, v % NC
                    wait(pe, t_copied, n + 1)
                    if v == 0:
                        wait(pe, m_read, base(sq))
                    if c % 2 == 0:
                        wait(pe, o_copied, sq * 4 + v // 2)
                    vv, nk = vw[par ^ shift], keys(v)
                    for i in range(2):
                        for kt in range(nk):
                            for hh in range(2):
                                h = 2 * i + hh
                                ins = nc.tensor.matmul(O[DH * hh:DH * hh + DH, 2 * (c % 2) + i, :],
                                                       vv[:, kt, HC * c + h, :],
                                                       probsT[:, v % TRING, kt, h * P:(h + 1) * P],
                                                       start=kt == 0, stop=kt == nk - 1, tile_position=(0, DH * hh))
                    ins.then_inc(pv_done, 1)

                for n, job in enumerate(FIRST):
                    run(job, n, 0, 0)

                def body(b, par):
                    for u in range(UN):
                        todo = jobs(b, u)
                        for k, part in enumerate((lambda: transposes(b, u), lambda: scores(b, u, par),
                                                  lambda: values(b, u, par))):
                            part()
                            if k < len(todo):
                                run(*todo[k], b + 1, par ^ 1)

                def rest(b, par):
                    for u in range(LAG_V):
                        if u < LAG_T:
                            transposes(b, u)
                        values(b, u, par)
                    for k in range(TT):
                        run(("o", k), base(NB) + k, b + 1, par ^ 1)

                over_sequences(pe, body, rest)

            @block.scalar
            def _(act):
                def exponentials(b, u):
                    n, r, v = UN * b + u, u % PRING, s_view(u)
                    wait(act, max_ready, n + 1)
                    wait(act, t_ready, n - PRING + 1)
                    for h in range(HC):
                        ins = nc.scalar.activation(probs[:, r, h, 0:keys(u) * P], v[:, h, :], ACT.Exp,
                                                   bias=negmax[:, r, h:h + 1], accum_out=rowsum[:, r, h:h + 1])
                    ins.then_inc(exp_done, 1)

                def read(job, n, j, par):
                    kind, k = job
                    if kind == "x":
                        wait(act, m_ready, n + 1)
                        nc.scalar.activation(xnT[:, :], M[:, 0:T], ACT.Copy).then_inc(m_read, 1)
                    elif kind == "v":
                        wait(act, m_ready, n + 1)
                        wait(act, pv_done, UN * (j - 1))
                        t, half = k // 2, k % 2
                        nc.scalar.activation(vw[par][:, t, half * 8:(half + 1) * 8, :],
                                             M[:, :].rearrange("p (h d) -> p h d", h=8), ACT.Copy
                                             ).then_inc(m_read, 1)

                def o_copy(sq, group):
                    wait(act, pv_done, sq * UN + 2 * group + 2)
                    t, c2 = group // 2, group % 2
                    if not (isinstance(sq, int) and sq == 0):
                        act.wait_ge(m_read, base(sq) + OUT_PLACE[t] + 1)
                    nc.scalar.activation(osb[:, t, 4 * c2:4 * c2 + 4, :], O[:, :, :], ACT.Copy
                                         ).then_inc(o_copied, 1)

                for n, job in enumerate(FIRST):
                    read(job, n, 0, 0)

                def body(b, par):
                    for u in range(UN):
                        exponentials(b, u)
                        for job, n in jobs(b, u):
                            read(job, n, b + 1, par ^ 1)
                        if u in (1, 3) and exists(b, 0, 1):
                            o_copy(b - 1, 2 + u // 2)
                        if u in (5, 7):
                            o_copy(b, (u - 5) // 2)

                over_sequences(act, body, lambda b, par: [o_copy(b - 1, 2 + k) for k in range(2)])

            @block.vector
            def _(dve):
                halves_vector(dve, g, st, g.X, NT + 2 * PAD)
                moments_vector(dve, g, st, 1e-5, NT + 2 * PAD)
                dve.wait_ge(w_in, 16 * len(loads))

                def x_normalise(j, par):
                    if not (isinstance(j, int) and j < 2):
                        dve.wait_ge(m_ready, base(j - 2))
                    for t in range(TT):
                        tile = j * TT + t
                        ins = nc.vector.tensor_scalar(xs[:, par, t:t + 1, :], g.X[:, bass.ds(tile, 1), :],
                                                      g.mean[:, bass.ds(tile, 1)], g.rstd[:, bass.ds(tile, 1)],
                                                      ALU.subtract, ALU.mult)
                    ins.then_inc(xs_ready, 1)

                def read(job, n, j):
                    kind, k = job
                    if kind in "qk":
                        i = 2 * k + (kind == "k")
                        wait(dve, m_ready, n + 1)
                        wait(dve, qk_ready, j * NADD + adds(i - NTMP + 1))
                        nc.vector.tensor_tensor(tmp[:, i % NTMP, :], M[:, :], turn[kind == "k"][:, :], ALU.mult
                                                ).then_inc(m_read, 1)
                    elif kind == "o":
                        wait(dve, m_ready, n + 1)
                        dst = g.X[:, bass.ds((j - 2) * TT + k, 1), :]
                        nc.vector.tensor_tensor(dst, dst, M[:, 0:P].unsqueeze(1), ALU.add).then_inc(m_read, 1)

                def maxima(b, u):
                    n = UN * b + u
                    wait(dve, s_ready, n + 1)
                    wait(dve, exp_done, n - PRING + 1)
                    nc.vector.tensor_reduce(out=negmax[:, u % PRING, :], in_=s_view(u), axis=AX, op=ALU.max,
                                            negate=True).then_inc(max_ready, 1)

                def reciprocals(b, u):
                    if not exists(b, u, 1):
                        return
                    sq, v, _ = split(b, u, 1)
                    n, r = sq * UN + v, v % PRING
                    wait(dve, exp_done, n + 1)
                    wait(dve, norm_done, n - PRING + 1)
                    nc.vector.reciprocal(rinv[:, r, :], rowsum[:, r, :]).then_inc(rinv_ready, 1)

                def t_copy(b, u):
                    if not exists(b, u, LAG_T):
                        return
                    sq, v, _ = split(b, u, LAG_T)
                    n = sq * UN + v
                    wait(dve, t_ready, n + 1)
                    wait(dve, pv_done, n - TRING + 1)
                    nk = keys(v)
                    nc.vector.tensor_copy(probsT[:, v % TRING, 0:nk, :], PT[:, 0:nk, :]).then_inc(t_copied, 1)

                for j in range(2):
                    x_normalise(j, j)
                for n, job in enumerate(FIRST):
                    read(job, n, 0)

                def body(b, par):
                    for u in range(UN):
                        todo = jobs(b, u)
                        for k, part in enumerate((lambda: t_copy(b, u), lambda: maxima(b, u),
                                                  lambda: reciprocals(b, u))):
                            part()
                            if k < len(todo):
                                read(*todo[k], b + 1)
                        if u == 6:
                            x_normalise(b + 2, par)

                def rest(b, par):
                    reciprocals(b, 0)
                    for u in range(LAG_T):
                        t_copy(b, u)
                    for k in range(TT):
                        read(("o", k), base(NB) + k, b + 1)

                over_sequences(dve, body, rest)
        clear = list(st.sems)
        clear_semaphores(nc, clear)


def hyperbolic_attention_stage(nc, g, w, name):
    LAG_E, LAG_N, LAG_T, LAG_V = 2, 3, 5, 6
    NCOL = 3 * P + H + 1
    with ExitStack() as ctx:
        st = Scope(nc, ctx, name)
        sb, ps, sem = st.sb, st.ps, st.sem
        wall, ball, wo, bo = sb("wall", [P, NCOL]), sb("ball", [P, NCOL]), sb("wo", [P, NC, P]), sb("bo", [P, P])
        thr, safe, curv = sb("thr", [P, 1]), sb("safe", [P, 1]), sb("curv", [P, H])
        soft, one = sb("soft", [P, H]), sb("one", [P, 1])
        xs, xnT = sb("xs", [P, 2, TT, P]), sb("xnT", [P, T])
        F = [sb(f"F{i}", [P, TT, NCOL]) for i in range(2)]
        sg, oma, sal = sb("sg", [P, TT, H + 1]), sb("oma", [P, TT, H]), sb("sal", [P, TT, H])
        SA, SPK = sb("SA", [P, NT + 2 * PAD, H]), sb("SPK", [P, NT + 2 * PAD])
        sq, ops = sb("sq", [P, TT, 2 * P]), sb("ops", [P, TT, 3, P])
        n2, rn, rn2, z, gz, space = (sb(n, [P, TT, 2 * H]) for n in ("n2", "rn", "rn2", "z", "gz", "space"))
        resid, parts = sb("resid", [P, 2 * T]), sb("parts", [P, 2, 2, 3, 2 * T], BF16)
        KROWS = NBLK * 16
        qst = [[sb(f"qst{i}{k}", [KROWS, NPAIR, T], BF16) for k in range(2)] for i in range(2)]
        kst = [[sb(f"kst{i}{k}", [KROWS, NPAIR, 2, T], BF16) for k in range(2)] for i in range(2)]
        vp = [sb(f"vp{i}", [P, TT, H, 32]) for i in range(2)]
        DRING, WRING = 2, 4
        dd, ww = sb("dd", [P, DRING, HC * T]), sb("ww", [P, WRING, HC * T])
        probs, probsT = sb("probs", [P, PRING, HC, T]), sb("probsT", [P, TRING, TT, HC * P])
        rec = sb("rec", [P, PRING, HC])
        top, negtop = sb("top", [P, PRING, HC]), sb("negtop", [P, PRING, HC])
        rowsum, rinv = sb("rowsum", [P, PRING, HC]), sb("rinv", [P, PRING, HC])
        osb = sb("osb", [P, TT, NC, P])
        SE, SI = ps("SE", [P, HC * T]), ps("SI", [P, HC * T])
        PT, O, M = ps("PT", [P, TT, HC * P]), ps("O", [P, NC, P]), ps("M", [P, 512])
        moments_sems(st)
        w_in, setup, zeroed = sem("weights_in"), sem("setup"), sem("zeroed")
        xs_ready, m_ready, m_read = sem("xs_ready"), sem("job_ready"), sem("job_read")
        sig_ready, front, pool_front, hi_ready, parts_ready = (sem(n) for n in (
            "sigmoid_exp_ready", "front_steps", "pool_front_steps", "hi_ready", "parts_ready"))
        parts_out, st_in, v_ready = sem("parts_out"), [sem("stacks_in0"), sem("stacks_in1")], sem("v_ready")
        i_ready, d_ready, u_ready, root_ready, arg_ready, dist_ready = (sem(n) for n in (
            "inner_ready", "d_ready", "u_ready", "root_ready", "arg_ready", "dist_ready"))
        log_ready, acosh_ready, part_step = sem("log_ready"), sem("acosh_ready"), sem("middle_part_ready")
        e_ready, top_ready, neg_ready, exp_done = (sem(n) for n in ("e_ready", "top_ready", "neg_ready", "exp_done"))
        rec_ready, rinv_ready, norm_done, t_ready = (sem(n) for n in ("rec_ready", "rinv_ready", "norm_done", "t_ready"))
        t_copied, pv_done, o_copied, act_step = sem("t_copied"), sem("pv_done"), sem("o_copied"), sem("act_step")
        bo_added = sem("bias_added")
        scr = g.scratch2
        NIN = 2 * NBLK * 3

        FRONT = {1: [("x", 0)], 2: [("f", 0)], 3: [("f", 1)], 6: [("s", 0)], 7: [("s", 1)]}
        OUT = {4: ("o", 0), 7: ("o", 1)}
        FIRST = [j for u in sorted(FRONT) for j in FRONT[u]]
        NF, NJ = len(FIRST), len(FIRST) + len(OUT)

        def base(b):
            return 2 * NF if isinstance(b, int) and b == 0 else b * NJ + (3 * NF - NJ)

        def jobs(b, u):
            first = isinstance(b, int) and b == 0
            before = sum(len(FRONT.get(x, [])) + (x in OUT and not first) for x in range(u))
            todo = FRONT.get(u, []) + ([OUT[u]] if u in OUT and not first else [])
            return [(job, base(b) + before + k) for k, job in enumerate(todo)]

        def keys(u):
            return 1 if u // NC == 0 else TT

        def split(b, u, lag):
            return (b, u - lag, 0) if u >= lag else (b - 1, u - lag + UN, 1)

        def exists(b, u, lag):
            return not (isinstance(b, int) and not 0 <= UN * b + u - lag < UN * NB)

        def unit(b, u, lag):
            sq_, v, shift = split(b, u, lag)
            return sq_, v, sq_ * UN + v, keys(v) * P, shift

        loads = [(wall, w["wall"]), (ball, w["ball"]), (wo, w["wo"]), (bo, w["bo"]), (thr, w["thr"]),
                 (safe, w["qk_scale"]), (curv, w["log_k"])]
        C = [1.0]
        NSERIES = 7
        for k in range(1, NSERIES + 1):
            C.append(C[-1] / (2 * k * (2 * k + 1)))
        SMALL = float(np.float32(1.0 + 1e-6) - np.float32(1.0))
        SC = g.score_scale
        STEPS_SA, STEPS_A, STEPS = 6, 10, 10 + 7 + 1 + 2 * (NSERIES - 1) + 7

        with nc.Block() as block:
            @block.sync
            def _(sp):
                load_weights(sp, w_in, loads)
                sp.wait_ge(zeroed, 6)

                def counts(j, par):
                    v = (2 * j + 2, (j - par) * (8 * NIN), (j - 1) * UN, j * 32 + 32)
                    return v if isinstance(j, int) else tuple(sp.to_reg(x) for x in v)

                def bounce(par, first, n):
                    split_n, read_n, used_n, out_n = n
                    wait(sp, parts_ready, split_n)
                    wait(sp, st_in[par], read_n)
                    for kind in range(2):
                        sp.dma_start(scr[par, kind].rearrange("a p n -> p a n"), parts[:, par, kind, :, :]
                                     ).then_inc(parts_out, 16)
                    if not first:
                        sp.wait_ge(e_ready, used_n)
                    wait(sp, parts_out, out_n)
                    for kind in (1, 0):
                        for i in range(NBLK):
                            r = 16 * i
                            sp.dma_start(qst[par][kind][r:r + 16, :, :],
                                         scr[par, kind, QPART[i], :, 0:T].rearrange("(c r) t -> r c t", r=16)
                                         ).then_inc(st_in[par], 16)
                            for hh in range(2):
                                src = scr[par, kind, KPART[i], :, T:2 * T].rearrange("(c h d) t -> h d c t", h=2, d=8)
                                sp.dma_start(kst[par][kind][r + 8 * hh:r + 8 * hh + 8, :, hh, :], src[hh]
                                             ).then_inc(st_in[par], 16)

                bounce(0, True, counts(0, 0))
                bounce(1, True, counts(1, 1))
                bounce(0, False, counts(2, 0))
                with sp.Fori(0, (NB - 2) // 2) as i:
                    odd, even = counts(i * 2 + 3, 1), counts(i * 2 + 4, 0)
                    bounce(1, False, odd)
                    bounce(0, False, even)
                bounce(1, False, counts(NB + 1, 1))
                sp.wait_ge(parts_out, 32 * (NB + PAD))
                for i in range(2):
                    sp.wait_ge(st_in[i], 16 * NIN * (NB + PAD) // 2)

            @block.gpsimd
            def _(pool):
                for i in range(2):
                    for k in range(2):
                        nc.gpsimd.memset(kst[i][k][:, :, :, :], 0.0).then_inc(zeroed, 1)
                for i in range(2):
                    nc.gpsimd.memset(vp[i][:, :, :, :], 0.0).then_inc(zeroed, 1)
                moments_pool(pool, g, st)

                def to_power(out, in_, exponent, value):
                    wait(pool, front, value)
                    nc.gpsimd.tensor_tensor(out, in_, exponent, ALU.pow).then_inc(pool_front, 1)

                def front_powers(j, par, k):
                    flat = lambda x: x.rearrange("p t k -> p (t k)")
                    if k == 0:
                        to_power(SA[:, bass.ds(j * TT, TT), :], sal[:, :, :],
                                 g.half[:, 0:TT * H].rearrange("p (t k) -> p t k", t=TT), j * STEPS + STEPS_SA)
                    elif k == 1:
                        to_power(flat(rn[:, :, :]), flat(rn[:, :, :]), g.neghalf[:, 0:TT * 2 * H], j * STEPS + STEPS_A)
                    else:
                        out = ops[:, :, 1:3, :].rearrange("p t s (h d) -> p t (s h) d", d=8)[:, :, :, 0]
                        to_power(out, space[:, :, :], g.half[:, 0:TT * 2 * H].rearrange("p (t k) -> p t k", t=TT),
                                 (j + 1) * STEPS)

                def argument(b, u):
                    if not exists(b, u, 0):
                        return
                    n, nk = UN * b + u, keys(u) * P * HC
                    wait(pool, root_ready, n + 1)
                    x = ww[:, u % WRING, 0:nk]
                    nc.gpsimd.tensor_tensor(x, x, dd[:, u % DRING, 0:nk], ALU.add).then_inc(arg_ready, 1)

                def normalise(b, u):
                    if not exists(b, u, LAG_N):
                        return
                    sq_, v, n, nk, _ = unit(b, u, LAG_N)
                    r = v % PRING
                    wait(pool, rinv_ready, n + 1)
                    pr = probs[:, r, :, 0:nk]
                    nc.gpsimd.tensor_tensor(pr, pr, rinv[:, r, :].unsqueeze(2).broadcast_to([P, HC, nk]),
                                            ALU.mult).then_inc(norm_done, 1)

                for j in range(2):
                    for k in range(3):
                        front_powers(j, j, k)

                def body(b, par):
                    for u in range(UN):
                        normalise(b, u)
                        argument(b, u)
                        if u in (3, 4, 5):
                            front_powers(b + 2, par, u - 3)

                over_sequences(pool, body, lambda b, par: [normalise(b, u) for u in range(LAG_N)])

            @block.tensor
            def _(pe):
                pe.wait_ge(w_in, 16 * len(loads))

                def run(job, n, j, par):
                    kind, k = job
                    wait(pe, m_read, n)
                    if kind == "x":
                        wait(pe, xs_ready, j + 1)
                        for t in range(TT):
                            ins = nc.tensor.transpose(M[:, t * P:(t + 1) * P], xs[:, par, t, :], g.ident[:, :])
                    elif kind == "f":
                        ins = nc.tensor.matmul(M[:, 0:NCOL], xnT[:, k * P:(k + 1) * P], wall[:, :], start=True,
                                               stop=True)
                    elif kind == "s":
                        wait(pe, pool_front, 3 * j + 3)
                        for t in range(TT):
                            qop = ops[:, t, k, :]
                            kop = ops[:, t, 2, :] if k else F[par][:, t, P:2 * P]
                            nc.tensor.transpose(M[:, t * P:(t + 1) * P], qop, g.ident[:, :])
                            ins = nc.tensor.transpose(M[:, T + t * P:T + (t + 1) * P], kop, g.ident[:, :])
                    else:
                        wait(pe, o_copied, (j - 3) * TT + k + 1)
                        for c in range(NC):
                            ins = nc.tensor.matmul(M[:, 0:P], osb[:, k, c, :], wo[:, c, :], start=c == 0,
                                                   stop=c == NC - 1)
                    ins.then_inc(m_ready, 1)

                def transposes(b, u):
                    if not exists(b, u, LAG_T):
                        return
                    sq_, v, n, nk, _ = unit(b, u, LAG_T)
                    wait(pe, norm_done, n + 1)
                    wait(pe, t_copied, n)
                    for kt in range(nk // P):
                        for h in range(HC):
                            ins = nc.tensor.transpose(PT[:, kt, h * P:(h + 1) * P],
                                                      probs[:, v % PRING, h, kt * P:(kt + 1) * P], g.ident[:, :])
                    ins.then_inc(t_ready, 1)

                def products(out, par, kind, v, nk, mask):
                    t, c = v // NC, v % NC
                    out = out[:, 0:HC * nk].rearrange("p (h k) -> p h k", h=HC)
                    for i in range(HC // 2):
                        o2 = out[:, 2 * i:2 * i + 2, :]
                        ins = nc.tensor.matmul(o2, qst[par][kind][:, 2 * c + i, t * P:(t + 1) * P],
                                               kst[par][kind][:, 2 * c + i, :, 0:nk], start=True, stop=True)
                        if mask:
                            ins = nc.tensor.matmul(o2[:, :, t * P:(t + 1) * P], g.identb[:, :], g.maskb[:, :, :],
                                                   start=False, stop=True, skip_group_check=True)
                    return ins

                def inner(b, u, par):
                    if not exists(b, u, 0):
                        return
                    if u == 0:
                        wait(pe, st_in[par], (b - par) * (8 * NIN) + 16 * NIN)
                    wait(pe, d_ready, UN * b + u)
                    products(SI, par, 1, u, keys(u) * P, False).then_inc(i_ready, 1)

                def euclid(b, u, par):
                    if not exists(b, u, LAG_E):
                        return
                    sq_, v, n, nk, shift = unit(b, u, LAG_E)
                    wait(pe, top_ready, n)
                    products(SE, par ^ shift, 0, v, nk, True).then_inc(e_ready, 1)

                def values(b, u, par):
                    if not exists(b, u, LAG_V):
                        return
                    sq_, v, n, nk, shift = unit(b, u, LAG_V)
                    c, t = v % NC, v // NC
                    wait(pe, t_copied, n + 1)
                    if v == 0:
                        wait(pe, v_ready, sq_ + 1)
                    if c == 0:
                        wait(pe, o_copied, 2 * sq_ + t)
                    for kt in range(nk // P):
                        for h in range(HC):
                            ins = nc.tensor.matmul(O[32 * h:32 * h + 32, c, :], vp[par ^ shift][:, kt, HC * c + h, :],
                                                   probsT[:, v % TRING, kt, h * P:(h + 1) * P],
                                                   start=kt == 0, stop=kt == nk // P - 1, tile_position=(0, 32 * h))
                    ins.then_inc(pv_done, 1)

                for j in range(2):
                    for k, job in enumerate(FIRST):
                        run(job, j * NF + k, j, j)

                def body(b, par):
                    for u in range(UN):
                        transposes(b, u)
                        inner(b, u, par)
                        euclid(b, u, par)
                        values(b, u, par)
                        for job, n in jobs(b, u):
                            run(job, n, b + 2, par)

                def rest(b, par):
                    for u in range(LAG_V):
                        transposes(b, u)
                        euclid(b, u, par)
                        values(b, u, par)
                    for k in range(TT):
                        run(("o", k), base(NB) + k, b + 2, par)

                over_sequences(pe, body, rest)

            @block.scalar
            def _(act):
                act.wait_ge(w_in, 16 * len(loads))
                act.wait_ge(setup, 3)
                nc.scalar.activation(soft[:, :], soft[:, :], ACT.Exp).then_inc(act_step, 1)
                nc.scalar.activation(safe[:, :], safe[:, :], ACT.Exp, scale=-1.0).then_inc(act_step, 1)
                act.wait_ge(act_step, 1)
                nc.scalar.activation(soft[:, :], soft[:, :], ACT.Ln, bias=one[:, 0:1]).then_inc(act_step, 1)

                def read(job, n, j, par):
                    kind, k = job
                    if kind == "x":
                        wait(act, m_ready, n + 1)
                        nc.scalar.activation(xnT[:, :], M[:, 0:T], ACT.Copy).then_inc(m_read, 1)
                    elif kind == "s":
                        wait(act, m_ready, n + 1)
                        wait(act, parts_out, (j - 1) * 32)
                        nc.scalar.activation(parts[:, par, k, 0, :], M[:, :], ACT.Copy).then_inc(hi_ready, 1)

                def sigmoid_exp(j, par):
                    wait(act, front, j * STEPS + 2)
                    nc.scalar.activation(sg[:, :, :], F[par][:, :, 3 * P:], ACT.Exp, scale=-1.0
                                         ).then_inc(sig_ready, 1)

                def v_copy(j, par):
                    wait(act, front, j * STEPS + 2)
                    if isinstance(j, int) and j < 2:
                        wait(act, zeroed, 6)
                    wait(act, pv_done, UN * (j - 1))
                    nc.scalar.activation(vp[par][:, :, :, 0:8],
                                         F[par][:, :, 2 * P:3 * P].rearrange("p t (h d) -> p t h d", d=8), ACT.Copy
                                         ).then_inc(v_ready, 1)

                def root(b, u):
                    if not exists(b, u, 0):
                        return
                    n, nk = UN * b + u, keys(u) * P * HC
                    x = ww[:, u % WRING, 0:nk]
                    wait(act, u_ready, n + 1)
                    nc.scalar.activation(x, x, ACT.Ln).then_inc(log_ready, 1)
                    wait(act, log_ready, n + 1)
                    nc.scalar.activation(x, x, ACT.Exp, scale=0.5).then_inc(root_ready, 1)

                def distance(b, u):
                    if not exists(b, u, 1):
                        return
                    sq_, v, n, nk, _ = unit(b, u, 1)
                    x = ww[:, v % WRING, 0:HC * nk]
                    t, c = v // NC, v % NC
                    wait(act, arg_ready, n + 1)
                    nc.scalar.activation(x, x, ACT.Ln, bias=one[:, 0:1]).then_inc(acosh_ready, 1)
                    wait(act, acosh_ready, n + 1)
                    if v == 0:
                        wait(act, pool_front, 3 * sq_ + 1)
                    for h in range(HC):
                        y = x[:, h * nk:(h + 1) * nk]
                        sa = SA[:, bass.ds(sq_ * TT + t, 1), HC * c + h:HC * c + h + 1].rearrange("p a b -> p (a b)")
                        ins = nc.scalar.activation(y, y, ACT.Square, scale=sa)
                    ins.then_inc(dist_ready, 1)

                def exponentials(b, u):
                    if not exists(b, u, LAG_E):
                        return
                    sq_, v, n, nk, _ = unit(b, u, LAG_E)
                    r = v % PRING
                    wait(act, neg_ready, n + 1)
                    for h in range(HC):
                        y = probs[:, r, h, 0:nk]
                        ins = nc.scalar.activation(y, y, ACT.Exp, bias=negtop[:, r, h:h + 1],
                                                   accum_out=rowsum[:, r, h:h + 1])
                    ins.then_inc(exp_done, 1)

                def o_copy(sq_, t):
                    wait(act, pv_done, sq_ * UN + (t + 1) * NC)
                    if not (isinstance(sq_, int) and sq_ == 0):
                        act.wait_ge(m_read, base(sq_) + (4 if t == 0 else NJ))
                    nc.scalar.activation(osb[:, t, :, :], O[:, :, :], ACT.Copy).then_inc(o_copied, 1)

                for j in range(2):
                    for k, job in enumerate(FIRST):
                        if job == ("s", 0):
                            sigmoid_exp(j, j)
                        read(job, j * NF + k, j, j)
                v_copy(0, 0)

                def body(b, par):
                    for u in range(UN):
                        distance(b, u)
                        root(b, u)
                        exponentials(b, u)
                        for job, n in jobs(b, u):
                            read(job, n, b + 2, par)
                        if u == 3:
                            sigmoid_exp(b + 2, par)
                        if u == 1 and exists(b, 0, 1):
                            o_copy(b - 1, 0)
                        if u == 5 and exists(b, 0, 1):
                            o_copy(b - 1, 1)
                        if u == 6:
                            v_copy(b + 1, par ^ 1)

                def rest(b, par):
                    for u in range(LAG_V):
                        distance(b, u)
                        exponentials(b, u)
                        if u == 1:
                            o_copy(b - 1, 0)
                    o_copy(b - 1, 1)

                over_sequences(act, body, rest)

            @block.vector
            def _(dve):
                v_ = nc.vector
                halves_vector(dve, g, st, g.X, NT + 2 * PAD)
                moments_vector(dve, g, st, 1e-5, NT + 2 * PAD)
                dve.wait_ge(w_in, 16 * len(loads))
                c = Chain(dve, setup)
                c(v_.memset(one[:, :], 1.0))
                c(v_.tensor_scalar(soft[:, :], curv[:, :], -1.0, None, ALU.mult))
                c(v_.tensor_tensor(soft[:, :], soft[:, :], curv[:, :], ALU.min))
                c(v_.tensor_scalar(curv[:, :], curv[:, :], 0.0, None, ALU.max))
                dve.wait_ge(act_step, 3)
                c(v_.tensor_tensor(curv[:, :], curv[:, :], soft[:, :], ALU.add))
                c(v_.tensor_scalar(curv[:, :], curv[:, :], 1e-6, None, ALU.add))
                c(v_.reciprocal(curv[:, :], curv[:, :]))
                c(v_.tensor_scalar(safe[:, :], safe[:, :], 1.0, None, ALU.add))
                c(v_.reciprocal(safe[:, :], safe[:, :]))
                c(v_.tensor_scalar(safe[:, :], safe[:, :], 1.5, None, ALU.mult))

                def x_normalise(j, par):
                    if not (isinstance(j, int) and j < 2):
                        dve.wait_ge(m_ready, base(j - 2))
                    for t in range(TT):
                        tile = j * TT + t
                        ins = v_.tensor_scalar(xs[:, par, t:t + 1, :], g.X[:, bass.ds(tile, 1), :],
                                               g.mean[:, bass.ds(tile, 1)], g.rstd[:, bass.ds(tile, 1)],
                                               ALU.subtract, ALU.mult)
                    ins.then_inc(xs_ready, 1)

                def read(job, n, j, par):
                    kind, k = job
                    if kind == "f":
                        wait(dve, m_ready, n + 1)
                        wait(dve, v_ready, j - 1)
                        v_.tensor_tensor(F[par][:, k, :], M[:, 0:NCOL], ball[:, :], ALU.add).then_inc(m_read, 1)
                    elif kind == "s":
                        wait(dve, hi_ready, 2 * j + k + 1)
                        wait(dve, parts_ready, 2 * j + k)
                        v_.tensor_tensor(resid[:, :], M[:, :], parts[:, par, k, 0, :], ALU.subtract
                                         ).then_inc(m_read, 1)
                        wait(dve, m_read, n + 1)
                        v_.tensor_copy(parts[:, par, k, 1, :], resid[:, :]).then_inc(part_step, 1)
                        wait(dve, part_step, (2 * j + k) + 1)
                        v_.tensor_tensor(parts[:, par, k, 2, :], resid[:, :], parts[:, par, k, 1, :], ALU.subtract
                                         ).then_inc(parts_ready, 1)
                    elif kind == "o":
                        wait(dve, m_ready, n + 1)
                        dst = g.X[:, bass.ds((j - 3) * TT + k, 1), :]
                        v_.tensor_tensor(dst, dst, bo[:, :].unsqueeze(1), ALU.add).then_inc(bo_added, 1)
                        wait(dve, bo_added, (j - 3) * TT + k + 1)
                        v_.tensor_tensor(dst, dst, M[:, 0:P].unsqueeze(1), ALU.add).then_inc(m_read, 1)

                def front_operands(j, par, piece, n_f):
                    f = F[par]
                    fl = lambda x: x[:, :, :].rearrange("p t k -> p (t k)")
                    first = sq[:, :, :].rearrange("p t (k d) -> p (t k) d", d=8)[:, :, 0]
                    c = Chain(dve, front, j * STEPS + (0, STEPS_A)[piece])
                    if piece == 0:
                        wait(dve, m_read, n_f)
                        qk = f[:, :, 0:2 * P]
                        c(v_.tensor_tensor(sq[:, :, :], qk, qk, ALU.mult))
                        c(v_.tensor_reduce(out=fl(n2), in_=sq[:, :, :].rearrange("p t (k d) -> p (t k) d", d=8),
                                           axis=AX, op=ALU.add))
                        wait(dve, sig_ready, j + 1)
                        c(v_.tensor_scalar(sg[:, :, :], sg[:, :, :], 1.0, None, ALU.add))
                        c(v_.reciprocal(sg[:, :, :], sg[:, :, :]))
                        alpha = sg[:, :, 0:H]
                        c(v_.tensor_scalar(SPK[:, bass.ds(j * TT, TT)], sg[:, :, H], thr[:, 0:1], None, ALU.is_gt))
                        wait(dve, pool_front, 3 * j)
                        c(v_.tensor_tensor(sal[:, :, :], alpha,
                                           curv[:, :].unsqueeze(1).broadcast_to([P, TT, H]), ALU.mult))
                        c(v_.tensor_scalar(oma[:, :, :], alpha, -SC, SC, ALU.mult, ALU.add))
                        for t in range(TT):
                            c(v_.tensor_tensor(ops[:, t, 0, :].rearrange("p (h d) -> p h d", d=8),
                                               f[:, t, 0:P].rearrange("p (h d) -> p h d", d=8),
                                               oma[:, t, :].unsqueeze(2).broadcast_to([P, H, 8]), ALU.mult))
                        c(v_.tensor_scalar(fl(rn), fl(n2), 1e-24, None, ALU.max))
                        done = STEPS_A
                    else:
                        wait(dve, pool_front, 3 * j + 2)
                        c(v_.tensor_scalar(fl(rn), fl(rn), safe[:, 0:1], None, ALU.mult))
                        c(v_.tensor_tensor(fl(rn2), fl(rn), fl(rn), ALU.mult))
                        c(v_.scalar_tensor_tensor(out=fl(z), in0=first, scalar=-2.0, in1=fl(n2), op0=ALU.mult,
                                                  op1=ALU.add))
                        c(v_.tensor_tensor(fl(space), fl(n2), first, ALU.subtract))
                        c(v_.tensor_tensor(fl(z), fl(z), fl(rn2), ALU.mult))
                        c(v_.tensor_tensor(fl(space), fl(space), fl(rn2), ALU.mult))
                        c(v_.tensor_scalar(fl(z), fl(z), 1e-8, None, ALU.max))
                        c(v_.tensor_scalar(fl(gz), fl(z), C[NSERIES], C[NSERIES - 1], ALU.mult, ALU.add))
                        for k in range(NSERIES - 2, -1, -1):
                            c(v_.tensor_tensor(fl(gz), fl(gz), fl(z), ALU.mult))
                            c(v_.tensor_scalar(fl(gz), fl(gz), C[k], None, ALU.add))
                        c(v_.tensor_tensor(fl(rn), fl(rn), fl(gz), ALU.mult))
                        c(v_.tensor_tensor(fl(gz), fl(gz), fl(gz), ALU.mult))
                        c(v_.tensor_tensor(fl(space), fl(space), fl(gz), ALU.mult))
                        c(v_.tensor_scalar(fl(space), fl(space), 1.0, None, ALU.add))
                        c(v_.tensor_scalar(rn[:, :, 0:H], rn[:, :, 0:H], -1.0, None, ALU.mult))
                        for t in range(TT):
                            c(v_.tensor_tensor(ops[:, t, 1:3, :].rearrange("p s (h d) -> p (s h) d", d=8),
                                               f[:, t, 0:2 * P].rearrange("p (k d) -> p k d", d=8),
                                               rn[:, t, :].unsqueeze(2).broadcast_to([P, 2 * H, 8]), ALU.mult))
                        done = STEPS
                    if isinstance(j, int):
                        assert c.n == j * STEPS + done, (c.n, done)

                def excess(b, u):
                    if not exists(b, u, 0):
                        return
                    n, nk = UN * b + u, keys(u) * P * HC
                    d, x = dd[:, u % DRING, 0:nk], ww[:, u % WRING, 0:nk]
                    wait(dve, i_ready, n + 1)
                    wait(dve, arg_ready, n - DRING + 1)
                    v_.tensor_scalar(d, SI[:, 0:nk], 1.0, SMALL, ALU.subtract, ALU.max).then_inc(d_ready, 1)
                    wait(dve, d_ready, n + 1)
                    wait(dve, top_ready, n - WRING + 1)
                    v_.scalar_tensor_tensor(out=x, in0=d, scalar=2.0, in1=d, op0=ALU.add, op1=ALU.mult
                                            ).then_inc(u_ready, 1)

                def scores(b, u):
                    if exists(b, u, LAG_E):
                        _, ev, en, nk, _ = unit(b, u, LAG_E)
                        wait(dve, e_ready, en + 1)
                        wait(dve, dist_ready, en + 1)
                        wait(dve, t_ready, en - PRING + 1)
                        wait(dve, neg_ready, en - PRING + 1)
                    if exists(b, u, LAG_N):
                        sq_, v, n, _, _ = unit(b, u, LAG_N)
                        r = v % PRING
                        if not exists(b, u, LAG_E):
                            wait(dve, t_ready, n - PRING + 1)
                        wait(dve, exp_done, n + 1)
                        wait(dve, norm_done, n - PRING + 1)
                        v_.reciprocal(rec[:, r, :], rowsum[:, r, :]).then_inc(rec_ready, 1)
                        wait(dve, rec_ready, n + 1)
                        v_.tensor_scalar(rinv[:, r, :], rec[:, r, :], SPK[:, bass.ds(sq_ * TT + v // NC, 1)], None,
                                         ALU.mult).then_inc(rinv_ready, 1)
                    if exists(b, u, LAG_E):
                        r, x = ev % PRING, ww[:, ev % WRING, 0:HC * nk]
                        for h in range(HC):
                            part = slice(h * nk, (h + 1) * nk)
                            ins = v_.tensor_tensor_reduce(
                                out=probs[:, r, h, 0:nk], in0=SE[:, part], in1=x[:, part], scale=1.0, scalar=MASKED,
                                op0=ALU.subtract, op1=ALU.max, accum_out=top[:, r, h:h + 1])
                        ins.then_inc(top_ready, 1)
                        wait(dve, top_ready, en + 1)
                        v_.tensor_scalar(negtop[:, r, :], top[:, r, :], -1.0, None, ALU.mult).then_inc(neg_ready, 1)

                def t_copy(b, u):
                    if not exists(b, u, LAG_T):
                        return
                    _, v, n, nk, _ = unit(b, u, LAG_T)
                    wait(dve, t_ready, n + 1)
                    wait(dve, pv_done, n - TRING + 1)
                    nt = nk // P
                    v_.tensor_copy(probsT[:, v % TRING, 0:nt, :], PT[:, 0:nt, :]).then_inc(t_copied, 1)

                for j in range(2):
                    x_normalise(j, j)
                for j in range(2):
                    for k, job in enumerate(FIRST):
                        read(job, j * NF + k, j, j)
                        if job == ("f", 1):
                            for piece in range(2):
                                front_operands(j, j, piece, j * NF + k + 1)

                def body(b, par):
                    for u in range(UN):
                        excess(b, u)
                        t_copy(b, u)
                        scores(b, u)
                        for job, n in jobs(b, u):
                            read(job, n, b + 2, par)
                            if job == ("f", 1):
                                front_operands(b + 2, par, 0, n + 1)
                        if u == 0:
                            x_normalise(b + 2, par)
                        if u == 5:
                            front_operands(b + 2, par, 1, None)

                def rest(b, par):
                    for u in range(LAG_V):
                        t_copy(b, u)
                        scores(b, u)
                    for k in range(TT):
                        read(("o", k), base(NB) + k, b + 2, par)

                over_sequences(dve, body, rest)
        clear = list(st.sems)
        clear_semaphores(nc, clear)


def moe_stage(nc, g, w, name):
    E, G, EPG, HK = 8, 2, 4, 2
    with ExitStack() as ctx:
        st = Scope(nc, ctx, name)
        sb, ps, sem = st.sb, st.ps, st.sem
        wa, wb = sb("wa", [P, 2 * HK, P]), sb("wb", [P, 2 * HK, P])
        wso, w2 = sb("wso", [P, HK, P]), sb("w2", [P, HK, E * P])
        wg, bg = sb("wg", [P, G + E]), sb("bg", [P, G + E])
        n1, n2 = sb("n1", [P, P]), sb("n2", [P, P])
        XPT = sb("XPT", [P, NB * T])
        xs, xt = sb("xs", [P, 2, TT, P]), sb("xt", [P, 2, T])
        logits = sb("logits", [P, NT + 2 * PAD, G + E])
        gmax, gexp, gsum, gsel = sb("gmax", [P, NT]), sb("gexp", [P, NT, G]), sb("gsum", [P, NT]), sb("gsel", [P, NT, G])
        emax, esum = sb("emax", [P, NT * G]), sb("esum", [P, NT * G])
        prob, ahead, tie = sb("prob", [P, NT * G, EPG]), sb("ahead", [P, NT * G, EPG, EPG]), sb("tie", [P, NT * G, EPG, EPG])
        rank, earlier = sb("rank", [P, NT * G, EPG]), sb("earlier", [P, EPG, EPG])
        weight = sb("weight", [P, NT * E])
        gate, hid = sb("gate", [P, 2 * HK * T]), sb("hid", [P, 2, 2 * HK, T])
        acc = sb("acc", [P, 2, 2, P])
        GA, GB = ps("GA", [P, 2 * HK * T]), ps("GB", [P, 2 * HK * T])
        Y = [ps(f"Y{i}", [P, 4 * P]) for i in range(2)]
        SH, M = ps("SH", [P, 512]), ps("M", [P, 512])
        moments_sems(st)
        w_in, made = sem("weights_in"), sem("earlier_made")
        xs_ready, xT_ready, xt_ready, xp_ready, xpt_ready = (sem(n) for n in (
            "xs_ready", "xT_ready", "xt_ready", "xp_ready", "xpt_ready"))
        lg_ready, lg_used, gate_step, gate_act = (sem(n) for n in ("lg_ready", "lg_used", "gate_step", "gate_act"))
        ga_ready, gb_ready, silu_done, hid_ready = (sem(n) for n in ("ga_ready", "gb_ready", "silu_done", "hid_ready"))
        sh_ready, sh_used, y_ready, acc_step = (sem(n) for n in ("sh_ready", "sh_used", "y_ready", "acc_step"))
        add_step, x_done = sem("add_step"), sem("x_done")
        loads = [(wa, w["wa"]), (wb, w["wb"]), (wso, w["wso"]), (w2, w["w2"]), (wg, w["wg"]), (bg, w["bg"]),
                 (n1, w["n1"]), (n2, w["n2"])]
        NBN = NT

        with nc.Block() as block:
            @block.sync
            def _(sp):
                load_weights(sp, w_in, loads)

            @block.gpsimd
            def _(pool):
                c = Chain(pool, made)
                c(nc.gpsimd.memset(earlier[:, :, :], 1.0))
                c(nc.gpsimd.affine_select(out=earlier[:, :, :], in_=earlier[:, :, :], compare_op=ALU.is_gt, fill=0.0,
                                          base=0, pattern=[[1, EPG], [-1, EPG]], channel_multiplier=0))
                moments_pool(pool, g, st, 0)
                moments_pool(pool, g, st, 1)

            @block.tensor
            def _(pe):
                pe.wait_ge(w_in, 16 * len(loads))

                def gating(b, par):
                    if there(b, 0):
                        wait(pe, xs_ready, b + 1)
                        wait(pe, xpt_ready, b - 1)
                        xT = (GA, GB)[par]
                        for t in range(TT):
                            ins = nc.tensor.transpose(xT[:, t * P:(t + 1) * P], xs[:, par, t, :], g.ident[:, :])
                        ins.then_inc(xT_ready, 1)
                    if there(b, 1):
                        wait(pe, xt_ready, b)
                        wait(pe, lg_used, b - 1)
                        for t in range(TT):
                            ins = nc.tensor.matmul(M[:, t * 16:t * 16 + G + E], xt[:, par ^ 1, t * P:(t + 1) * P],
                                                   wg[:, :], start=True, stop=True)
                        ins.then_inc(lg_ready, 1)

                in_order(pe, gating, 1)

                def up(b, which, dst, used, done):
                    if not there(b, 0):
                        return
                    wait(pe, used, b)
                    for k in range(2 * HK):
                        ins = nc.tensor.matmul(dst[:, k * T:(k + 1) * T], which[:, k, :], XPT[:, bass.ds(b * T, T)],
                                               start=True, stop=True)
                    ins.then_inc(done, 1)

                def down(b, par, t):
                    wait(pe, sh_used, b * TT + t)
                    for kk in range(HK):
                        ins = nc.tensor.matmul(SH[:, 0:P], hid[:, par, kk, t * P:(t + 1) * P], wso[:, kk, :],
                                               start=kk == 0, stop=kk == HK - 1)
                    ins.then_inc(sh_ready, 1)
                    for half in range(2):
                        wait(pe, acc_step, (b * TT + t - 1) * (E + 1) + 4 * (half + 1))
                        for kk in range(HK):
                            ins = nc.tensor.matmul(Y[half][:, :], hid[:, par, HK + kk, t * P:(t + 1) * P],
                                                   w2[:, kk, half * 4 * P:(half + 1) * 4 * P],
                                                   start=kk == 0, stop=kk == HK - 1)
                        ins.then_inc(y_ready, 1)

                wait(pe, xpt_ready, NB)
                wait(pe, xp_ready, NB)

                def experts(b, par):
                    up(b, wa, GA, silu_done, ga_ready)
                    if there(b, 1):
                        wait(pe, hid_ready, b)
                        down(b - 1, par ^ 1, 0)
                    up(b, wb, GB, hid_ready, gb_ready)
                    if there(b, 1):
                        down(b - 1, par ^ 1, 1)

                in_order(pe, experts, 1)

            @block.scalar
            def _(act):
                def gating(b, par):
                    if there(b, 0):
                        wait(act, xT_ready, b + 1)
                        wait(act, lg_ready, b - 1)
                        xT = (GA, GB)[par]
                        nc.scalar.activation(xt[:, par, :], xT[:, 0:T], ACT.Copy).then_inc(xt_ready, 1)
                        nc.scalar.activation(XPT[:, bass.ds(b * T, T)], xT[:, 0:T], ACT.Copy).then_inc(xpt_ready, 1)
                        nc.scalar.activation(g.XP[:, bass.ds(b * TT, TT), :], xs[:, par, :, :], ACT.Copy
                                             ).then_inc(xp_ready, 1)

                in_order(act, gating, 0)
                act.wait_ge(gate_act, 1)
                nc.scalar.activation(gexp[:, :, :], gexp[:, :, :], ACT.Exp).then_inc(gate_act, 1)
                act.wait_ge(gate_act, 3)
                nc.scalar.activation(prob[:, :, :], prob[:, :, :], ACT.Exp).then_inc(gate_act, 1)

                def experts(b, par):
                    wait(act, ga_ready, b + 1)
                    wait(act, hid_ready, b)
                    nc.scalar.activation(gate[:, :], GA[:, :], ACT.Silu).then_inc(silu_done, 1)

                in_order(act, experts, 0)

            @block.vector
            def _(dve):
                halves_vector(dve, g, st, g.XP, NT)
                moments_vector(dve, g, st, 1e-6, NT, 0, rms=True)
                dve.wait_ge(w_in, 16 * len(loads))

                def gating(b, par):
                    if there(b, 0):
                        wait(dve, xT_ready, b - 1)
                        wait(dve, xp_ready, b - 1)
                        for t in range(TT):
                            tile = b * TT + t
                            ins = nc.vector.scalar_tensor_tensor(
                                out=xs[:, par, t:t + 1, :], in0=g.XP[:, bass.ds(tile, 1), :],
                                scalar=g.rstd[:, bass.ds(tile, 1)], in1=n1[:, :].unsqueeze(1),
                                op0=ALU.mult, op1=ALU.mult)
                        ins.then_inc(xs_ready, 1)
                    if there(b, 1):
                        wait(dve, lg_ready, b)
                        ins = nc.vector.tensor_tensor(
                            logits[:, bass.ds((b - 1) * TT, TT), :],
                            M[:, 0:32].rearrange("p (t k) -> p t k", t=TT)[:, :, 0:G + E],
                            bg[:, :].unsqueeze(1).broadcast_to([P, TT, G + E]), ALU.add)
                        ins.then_inc(lg_used, 1)

                in_order(dve, gating, 1)
                dve.wait_ge(lg_used, NB)
                c = Chain(dve, gate_step)
                v = nc.vector
                gl, el = logits[:, 0:NT, 0:G], logits[:, 0:NT, G:].rearrange("p n (g e) -> p n g e", g=G)
                flat = lambda x: x.rearrange("p (n g) e -> p n g e", g=G)
                pairs = lambda x: x.rearrange("p (n g) -> p n g", g=G)
                c(v.tensor_reduce(out=gmax[:, :], in_=gl, axis=AX, op=ALU.max))
                v.tensor_tensor(gexp[:, :, :], gl, gmax[:, :].unsqueeze(2).broadcast_to([P, NT, G]), ALU.subtract
                                ).then_inc(gate_act, 1)
                c(v.tensor_reduce(out=pairs(emax[:, :]), in_=el, axis=AX, op=ALU.max))
                dve.wait_ge(gate_act, 2)
                v.tensor_tensor(flat(prob[:, :, :]), el,
                                pairs(emax[:, :]).unsqueeze(3).broadcast_to([P, NT, G, EPG]), ALU.subtract
                                ).then_inc(gate_act, 1)
                c(v.tensor_reduce(out=gsum[:, :], in_=gexp[:, :, :], axis=AX, op=ALU.add))
                c(v.reciprocal(gsum[:, :], gsum[:, :]))
                c(v.tensor_tensor(gsel[:, :, 0], gexp[:, :, 0], gexp[:, :, 1], ALU.is_ge))
                c(v.tensor_scalar(gsel[:, :, 1], gsel[:, :, 0], -1.0, 1.0, ALU.mult, ALU.add))
                c(v.tensor_tensor(gexp[:, :, :], gexp[:, :, :], gsel[:, :, :], ALU.mult))
                c(v.tensor_tensor(gexp[:, :, :], gexp[:, :, :], gsum[:, :].unsqueeze(2).broadcast_to([P, NT, G]),
                                  ALU.mult))
                dve.wait_ge(gate_act, 4)
                c(v.tensor_reduce(out=esum[:, :], in_=prob[:, :, :], axis=AX, op=ALU.add))
                c(v.reciprocal(esum[:, :], esum[:, :]))
                c(v.tensor_tensor(esum[:, :], esum[:, :], gexp[:, :, :].rearrange("p n g -> p (n g)"), ALU.mult))
                c(v.tensor_tensor(prob[:, :, :], prob[:, :, :], esum[:, :].unsqueeze(2).broadcast_to([P, NT * G, EPG]),
                                  ALU.mult))
                full = [P, NT * G, EPG, EPG]
                mine_, other = prob[:, :, :].unsqueeze(3).broadcast_to(full), prob[:, :, :].unsqueeze(2).broadcast_to(full)
                c(v.tensor_tensor(ahead[:, :, :, :], other, mine_, ALU.is_gt))
                c(v.tensor_tensor(tie[:, :, :, :], other, mine_, ALU.is_equal))
                dve.wait_ge(made, 2)
                c(v.tensor_tensor(tie[:, :, :, :], tie[:, :, :, :],
                                  earlier[:, :, :].unsqueeze(1).broadcast_to(full), ALU.mult))
                c(v.tensor_tensor(ahead[:, :, :, :], ahead[:, :, :, :], tie[:, :, :, :], ALU.add))
                c(v.tensor_reduce(out=rank[:, :, :], in_=ahead[:, :, :, :], axis=AX, op=ALU.add))
                c(v.scalar_tensor_tensor(out=weight[:, :].rearrange("p (n e) -> p n e", e=EPG), in0=rank[:, :, :],
                                         scalar=2.0, in1=prob[:, :, :], op0=ALU.is_lt, op1=ALU.mult))
                dve.wait_ge(xp_ready, NB)

                def combine(b, t):
                    tile = b * TT + t
                    a = acc[:, t, :, :]
                    n = tile * 9
                    wait(dve, sh_ready, tile + 1)
                    v.tensor_tensor(a[:, 0:1, :], g.XP[:, bass.ds(tile, 1), :], SH[:, 0:P].unsqueeze(1), ALU.add
                                    ).then_inc(sh_used, 1)
                    for e in range(E):
                        if e % 4 == 0:
                            wait(dve, y_ready, tile * 2 + e // 4 + 1)
                        src = Y[e // 4][:, (e % 4) * P:(e % 4 + 1) * P]
                        we = weight[:, bass.ds(tile * E + e, 1)]
                        k = e % 2
                        if e == 0:
                            wait(dve, sh_used, tile + 1)
                        elif e >= 2:
                            wait(dve, acc_step, n + e - 1)
                        if e == 1:
                            ins = v.tensor_scalar(a[:, 1, :], src, we, None, ALU.mult)
                        else:
                            ins = v.scalar_tensor_tensor(out=a[:, k, :], in0=src, scalar=we, in1=a[:, k, :],
                                                         op0=ALU.mult, op1=ALU.add)
                        ins.then_inc(acc_step, 1)
                    wait(dve, acc_step, n + E)
                    v.tensor_tensor(g.XP[:, bass.ds(tile, 1), :], a[:, 0:1, :], a[:, 1:2, :], ALU.add
                                    ).then_inc(acc_step, 1)
                    wait(dve, acc_step, n + 9)
                    v.bn_stats(g.bn6[:, bass.ds(tile * 6, 6)], g.XP[:, bass.ds(tile, 1), :]).then_inc(st.bn_done, 1)

                def experts(b, par):
                    if there(b, 1):
                        combine(b - 1, 0)
                    if there(b, 0):
                        wait(dve, gb_ready, b + 1)
                        wait(dve, silu_done, b + 1)
                        v.tensor_tensor(hid[:, par, :, :], gate[:, :].rearrange("p (k t) -> p k t", t=T),
                                        GB[:, :].rearrange("p (k t) -> p k t", t=T), ALU.mult).then_inc(hid_ready, 1)
                    if there(b, 1):
                        combine(b - 1, 1)

                in_order(dve, experts, 1)
                moments_vector(dve, g, st, 1e-6, 2 * NT, 1, rms=True)
                with dve.Fori(0, NT // 2) as i:
                    for k in range(2):
                        tile = i * 2 + k
                        row, out = g.XP[:, bass.ds(tile, 1), :], g.X[:, bass.ds(tile, 1), :]
                        v.scalar_tensor_tensor(out=row, in0=row, scalar=g.rstd[:, bass.ds(tile, 1)],
                                               in1=n2[:, :].unsqueeze(1), op0=ALU.mult, op1=ALU.mult
                                               ).then_inc(add_step, 1)
                    for k in range(2):
                        tile = i * 2 + k
                        row, out = g.XP[:, bass.ds(tile, 1), :], g.X[:, bass.ds(tile, 1), :]
                        wait(dve, add_step, tile + 1)
                        v.tensor_tensor(out, out, row, ALU.add).then_inc(x_done, 1)
        clear = list(st.sems)
        clear_semaphores(nc, clear)


def qlora_stage(nc, g, w, name):
    NBLOCK, R = 3, 32
    with ExitStack() as ctx:
        st = Scope(nc, ctx, name)
        sb, ps, sem = st.sb, st.ps, st.sem
        NL = 2 * NBLOCK
        qw, scl = sb("qw", [P, NL, P], I32), sb("scl", [P, NL, P])
        la, lb = sb("la", [R, NL, P]), sb("lb", [R, NL, P])
        wt = sb("wt", [P, NL, P])
        b1, b2 = sb("b1", [P, NBLOCK, P]), sb("b2", [P, NBLOCK])
        gam, bet = sb("gam", [P, NBLOCK]), sb("bet", [P, NBLOCK])
        HT = sb("HT", [P, NB * T])
        zs, yT, hT = sb("zs", [P, 2, TT, P]), sb("yT", [P, 2, T]), sb("hT", [P, 2, T])
        ZT = [ps(f"ZT{i}", [P, 512]) for i in range(2)]
        H2 = [ps(f"H2{i}", [P, 512]) for i in range(2)]
        Y1 = [ps(f"Y1{i}", [P, 512]) for i in range(2)]
        moments_sems(st)
        w_in, deq, lora_ready, w_ready = sem("weights_in"), sem("dequantised"), sem("lora_ready"), sem("weights_ready")
        zs_ready, zT_ready, act_done, h2_ready, h_ready, ht_copied, y1_ready, y1_used = (sem(n) for n in (
            "zs_ready", "zT_ready", "act_done", "h2_ready", "h_ready", "ht_copied", "y1_ready", "y1_used"))
        loads = [(qw, w["qw"]), (scl, w["scl"]), (la, w["la"]), (lb, w["lb"]), (b1, w["b1"]), (b2, w["b2"]),
                 (gam, w["gam"]), (bet, w["bet"])]
        ROUNDS = range(NBLOCK + 1)

        with nc.Block() as block:
            @block.sync
            def _(sp):
                load_weights(sp, w_in, loads)

            @block.gpsimd
            def _(pool):
                for r in ROUNDS:
                    moments_pool(pool, g, st, r)

            @block.tensor
            def _(pe):
                pe.wait_ge(w_in, 16 * len(loads))
                lo = [ZT[0], H2[0]]
                for i in range(NL):
                    ins = nc.tensor.matmul(lo[i // 4][:, (i % 4) * P:(i % 4 + 1) * P], la[:, i, :], lb[:, i, :],
                                           start=True, stop=True)
                ins.then_inc(lora_ready, 1)
                pe.wait_ge(w_ready, 2)
                for r in ROUNDS:
                    def step(b, par, r=r):
                        n = r * NB + b
                        if there(b, 0):
                            wait(pe, zs_ready, n + 1)
                            wait(pe, act_done, n - 1)
                            for t in range(TT):
                                ins = nc.tensor.transpose(ZT[par][:, t * P:(t + 1) * P], zs[:, par, t, :],
                                                          g.ident[:, :])
                            ins.then_inc(zT_ready, 1)
                        if there(b, 1) and r > 0:
                            wait(pe, act_done, n)
                            wait(pe, h_ready, n - 2)
                            nc.tensor.matmul(H2[par ^ 1][:, 0:T], wt[:, 2 * r - 1, :], yT[:, par ^ 1, :],
                                             start=True, stop=True).then_inc(h2_ready, 1)
                        if there(b, 2):
                            wait(pe, h_ready, n - 1)
                            wait(pe, y1_used, n - 2)
                            for t in range(TT):
                                if r < NBLOCK:
                                    ins = nc.tensor.matmul(Y1[par][:, t * P:(t + 1) * P],
                                                           hT[:, par, t * P:(t + 1) * P], wt[:, 2 * r, :],
                                                           start=True, stop=True)
                                else:
                                    ins = nc.tensor.transpose(Y1[par][:, t * P:(t + 1) * P],
                                                              hT[:, par, t * P:(t + 1) * P], g.ident[:, :])
                            ins.then_inc(y1_ready, 1)
                    in_order(pe, step, 2)

            @block.scalar
            def _(act):
                act.wait_ge(w_in, 16 * len(loads))
                for r in ROUNDS:
                    def step(b, par, r=r):
                        n = r * NB + b
                        if there(b, 0):
                            wait(act, zT_ready, n + 1)
                            if r == 0:
                                wait(act, y1_ready, n - 1)
                                nc.scalar.activation(hT[:, par, :], ZT[par][:, 0:T], ACT.Copy).then_inc(h_ready, 1)
                                nc.scalar.activation(HT[:, bass.ds(b * T, T)], ZT[par][:, 0:T], ACT.Copy
                                                     ).then_inc(act_done, 1)
                            else:
                                wait(act, h2_ready, n - NB - 1)
                                nc.scalar.activation(yT[:, par, :], ZT[par][:, 0:T], ACT.Gelu,
                                                     scale=gam[:, r - 1:r], bias=bet[:, r - 1:r]
                                                     ).then_inc(act_done, 1)
                        if there(b, 1) and 0 < r:
                            wait(act, h_ready, n)
                            nc.scalar.activation(HT[:, bass.ds((b - 1) * T, T)], hT[:, par ^ 1, :], ACT.Copy
                                                 ).then_inc(ht_copied, 1)
                    in_order(act, step, 1)

            @block.vector
            def _(dve):
                v = nc.vector
                dve.wait_ge(w_in, 16 * len(loads))
                c = Chain(dve, deq)
                c(v.tensor_copy(wt[:, :, :], qw[:, :, :]))
                c(v.tensor_scalar(wt[:, :, :], wt[:, :, :], 1.0 / 7.5, -1.0, ALU.mult, ALU.add))
                c(v.tensor_tensor(wt[:, :, :], wt[:, :, :], scl[:, :, :], ALU.mult))
                dve.wait_ge(lora_ready, 1)
                v.tensor_tensor(wt[:, 0:4, :], wt[:, 0:4, :], ZT[0][:, :].rearrange("p (l o) -> p l o", l=4), ALU.add
                                ).then_inc(w_ready, 1)
                v.tensor_tensor(wt[:, 4:6, :], wt[:, 4:6, :], H2[0][:, 0:2 * P].rearrange("p (l o) -> p l o", l=2),
                                ALU.add).then_inc(w_ready, 1)
                halves_vector(dve, g, st, g.X, NT)
                for r in ROUNDS:
                    moments_vector(dve, g, st, 1e-5, (r + 1) * NT, r)

                    def step(b, par, r=r):
                        n = r * NB + b
                        if there(b, 0):
                            wait(dve, zT_ready, n - 1)
                            for t in range(TT):
                                tile = b * TT + t
                                src = (g.X if r == 0 else g.XP)[:, bass.ds(tile, 1), :]
                                ins = v.tensor_scalar(zs[:, par, t:t + 1, :], src, g.mean[:, bass.ds(tile, 1)],
                                                      g.rstd[:, bass.ds(tile, 1)], ALU.subtract, ALU.mult)
                            ins.then_inc(zs_ready, 1)
                        if there(b, 1) and r > 0:
                            wait(dve, h2_ready, n - NB)
                            wait(dve, y1_ready, n - 2)
                            wait(dve, ht_copied, n - NB - 2)
                            if r == 1:
                                wait(dve, act_done, NB)
                            v.scalar_tensor_tensor(out=hT[:, par ^ 1, :], in0=H2[par ^ 1][:, 0:T],
                                                   scalar=b2[:, r - 1:r], in1=HT[:, bass.ds((b - 1) * T, T)],
                                                   op0=ALU.add, op1=ALU.add).then_inc(h_ready, 1)
                        if there(b, 2):
                            wait(dve, y1_ready, n - 1)
                            y = Y1[par][:, 0:T].rearrange("p (t o) -> p t o", t=TT)
                            if r < NBLOCK:
                                dst = g.XP[:, bass.ds((b - 2) * TT, TT), :]
                                v.tensor_tensor(dst, y, b1[:, r:r + 1, :].broadcast_to([P, TT, P]), ALU.add
                                                ).then_inc(y1_used, 1)
                                wait(dve, y1_used, n - 1)
                                for t in range(TT):
                                    tile = (b - 2) * TT + t
                                    v.bn_stats(g.bn6[:, bass.ds(tile * 6, 6)], g.XP[:, bass.ds(tile, 1), :]
                                               ).then_inc(st.bn_done, 1)
                            else:
                                dst = g.X[:, bass.ds((b - 2) * TT, TT), :]
                                v.tensor_tensor(dst, dst, y, ALU.add).then_inc(y1_used, 1)
                    in_order(dve, step, 2)
        clear = list(st.sems)
        clear_semaphores(nc, clear)


def store_stage(nc, g, out):
    with ExitStack() as ctx:
        st = Scope(nc, ctx, "store")
        x_out = st.sem("x_out")
        with nc.Block() as block:
            @block.sync
            def _(sp):
                ov = out.rearrange("(n p) d -> p n d", p=P)
                for k in range(4):
                    sp.dma_start(ov[:, k * 8:(k + 1) * 8, :], g.X[:, k * 8:(k + 1) * 8, :]).then_inc(x_out, 16)
                sp.wait_ge(x_out, 64)


class Globals:
    pass


def build_program(nc, a, out, stages):
    g = Globals()
    g.nc = nc
    g.score_scale = float(np.float32(1.0) / np.sqrt(np.float32(8.0)))
    with ExitStack() as ctx:
        def sb(name, shape, dt=F32):
            return ctx.enter_context(nc.sbuf_tensor(name, shape, dt))
        ntp = NT + 2 * PAD
        g.X = sb("X", [P, ntp, P])
        g.XP = sb("XP", [P, ntp, P])
        g.bn6, g.mean, g.gap, g.rstd = sb("bn6", [P, ntp * 6]), sb("mean", [P, ntp]), sb("gap", [P, ntp]), sb("rstd", [P, ntp])
        g.neghalf, g.half = sb("neghalf", [P, TT * 2 * H]), sb("half", [P, TT * 2 * H])
        g.ident, g.identb = sb("ident", [P, P]), sb("identb", [P, P], BF16)
        g.maskb = sb("maskb", [P, 2, P], BF16)
        g.scratch, g.scratch2 = a["scratch"], a["scratch2"]
        load_stage(nc, a["x"], g)
        of = lambda prefix: {k[4:]: v for k, v in a.items() if k.startswith(prefix)}
        for n, s in enumerate(stages):
            name = f"s{n}"
            if s == "L0a":
                hyperbolic_attention_stage(nc, g, of("l0a_"), name)
            if s == "L0b":
                attention_stage(nc, g, of("l0b_"), causal=True, name=name)
            if s == "F":
                attention_stage(nc, g, of("ffn_"), causal=False, rope=True, moe=True, name=name)
            if s == "L1a":
                wide_attention_stage(nc, g, of("l1a_"), name)
            if s == "MOE":
                moe_stage(nc, g, of("moe_"), name)
            if s == "L1b":
                attention_stage(nc, g, of("l1b_"), causal=True, bias=True, name=name)
            if s == "Q":
                qlora_stage(nc, g, of("qlo_"), name)
        store_stage(nc, g, out)


def pad_heads(wo):
    p = np.zeros((HC, 32, NC, P), np.float32)
    p[:, 0:8] = wo.reshape(NC, HC, 8, P).transpose(1, 2, 0, 3)
    return p.reshape(P, NC, P)


def rope_tables(scale):
    inv = (np.float32(1.0) / np.float32(10000.0) ** (np.arange(0, 8, 2, dtype=np.float32) / np.float32(8)))
    ang = np.arange(T, dtype=np.float32)[:, None] * inv.astype(np.float32)[None, :]
    cos, sin = np.cos(ang).T, np.sin(ang).T
    f = np.arange(P)
    c = cos[(f % 8) // 2]
    s = sin[(f % 8) // 2] * np.where(f % 2 == 0, -1, 1)[:, None]
    both = lambda m: np.stack([m * scale, m], axis=1).astype(np.float32)
    return both(c), both(s)


def half_rope():
    inv = np.float32(1.0) / np.float32(6000.0) ** (np.arange(0, 32, 2, dtype=np.float32) / np.float32(32))
    ang = (np.arange(T, dtype=np.float32)[:, None] * inv.astype(np.float32)[None, :]).T
    cos, sin = np.ones((64, T), np.float32), np.zeros((64, T), np.float32)
    cos[0:16], cos[16:32] = np.cos(ang), np.cos(ang)
    sin[0:16], sin[16:32] = -np.sin(ang), np.sin(ang)
    return np.tile(np.concatenate([cos, sin], axis=1), (2, 1)).astype(np.float32)


def rows(v):
    return np.ascontiguousarray(np.broadcast_to(v.reshape(1, -1), (P, v.size)))


def layouts(inp):
    a = {"x": inp["L0_attn_a_x"].reshape(NB * T, P)}
    one = lambda n: inp["L0_attn_a_" + n]
    a["l0a_wall"] = np.concatenate([one("Wqkv"), one("Walpha"), one("Wimp")], axis=0).T
    a["l0a_ball"] = rows(np.concatenate([one("bqkv"), one("balpha"), one("bimp")]))
    a["l0a_wo"], a["l0a_bo"] = pad_heads(one("Wout").T), rows(one("bout"))
    a["l0a_thr"], a["l0a_qk_scale"], a["l0a_log_k"] = (rows(one(n)) for n in ("spike_threshold", "qk_scale", "log_k"))
    w = inp["L0_attn_b_Wqkv"]
    a["l0b_wq"], a["l0b_wk"], a["l0b_wv"] = w[0:P].T, w[P:2 * P].T, w[2 * P:].T
    a["l0b_wo"] = pad_heads(inp["L0_attn_b_Wout"].T)
    w, b = inp["L1_attn_b_Wqkv"].transpose(1, 0, 2), inp["L1_attn_b_bqkv"]
    for k, n in enumerate("qkv"):
        a["l1b_w" + n] = w[:, :, 8 * k:8 * k + 8].reshape(P, P)
        bb = b[:, 8 * k:8 * k + 8].reshape(P)
        a["l1b_b" + n] = rows(bb) if n == "v" else bb.reshape(P, 1)
    a["l1b_wo"] = pad_heads(inp["L1_attn_b_Wout"])
    a["l1b_bo"] = rows(inp["L1_attn_b_bout"])
    swap = np.arange(P) ^ 1
    a["ffn_wq"], a["ffn_wqs"] = inp["L0_ffn_Wq"], inp["L0_ffn_Wq"][:, swap]
    a["ffn_wkcT"], a["ffn_wvcT"] = inp["L0_ffn_Wk_c"].T, inp["L0_ffn_Wv_c"].T
    a["ffn_wk"], a["ffn_wks"], a["ffn_wv"] = inp["L0_ffn_Wk"], inp["L0_ffn_Wk"][:, swap], inp["L0_ffn_Wv"]
    a["ffn_wo"] = pad_heads(inp["L0_ffn_Wo"])
    a["ffn_cosT"], a["ffn_sinT"] = rope_tables(np.float32(1.0) / np.sqrt(np.float32(8.0)))
    w = inp["L1_attn_a_W_qkv"]
    half = np.arange(64)
    half[0:16], half[16:32] = np.arange(16, 32), np.arange(16)
    for n, m in (("wq", w[0]), ("wqs", w[0][:, half]), ("wk", w[1]), ("wks", w[1][:, half])):
        a["l1a_" + n] = m.reshape(NPAIR, P, P).transpose(2, 0, 1)
    a["l1a_wv"] = w[2].reshape(H * 64, P).T
    a["l1a_wo"] = inp["L1_attn_a_W_o"].T.reshape(NPAIR, P, P).transpose(1, 0, 2)
    turn = half_rope()
    a["l1a_turn_q"], a["l1a_turn_k"] = turn * np.float32(0.125), turn
    ins, w1 = inp["L0_ffn_W_shared_in"], inp["L0_ffn_W1_shared"]
    a["moe_wa"] = np.concatenate([ins[:, 0:256], w1[:, 0:256]], axis=1).reshape(P, 4, P)
    a["moe_wb"] = np.concatenate([ins[:, 256:], w1[:, 256:]], axis=1).reshape(P, 4, P)
    a["moe_wso"] = inp["L0_ffn_W_shared_out"].reshape(2, P, P).transpose(1, 0, 2)
    a["moe_w2"] = inp["L0_ffn_W2_experts"].reshape(8, 2, P, P).transpose(2, 1, 0, 3).reshape(P, 2, 8 * P)
    a["moe_wg"] = np.concatenate([inp["L0_ffn_Wg_gate"], inp["L0_ffn_We_gate"]], axis=1)
    a["moe_bg"] = rows(np.concatenate([inp["L0_ffn_group_bias"], inp["L0_ffn_expert_bias"]]))
    a["moe_n1"], a["moe_n2"] = rows(inp["L0_ffn_norm1_w"]), rows(inp["L0_ffn_norm2_w"])
    a["qlo_qw"] = inp["L1_ffn_qweights"].transpose(2, 0, 1)
    a["qlo_scl"] = np.repeat(inp["L1_ffn_scales"], P // inp["L1_ffn_scales"].shape[2], axis=2).transpose(2, 0, 1)
    a["qlo_la"] = inp["L1_ffn_lora_a"].transpose(1, 0, 2)
    a["qlo_lb"] = inp["L1_ffn_lora_b"].transpose(2, 0, 1)
    a["qlo_b1"] = rows(inp["L1_ffn_biases"][0::2].reshape(-1)).reshape(P, 3, P)
    a["qlo_b2"] = inp["L1_ffn_biases"][1::2].T
    a["qlo_gam"], a["qlo_bet"] = inp["L1_ffn_ln_gamma"].T, inp["L1_ffn_ln_beta"].T
    return {k: np.ascontiguousarray(v) for k, v in a.items()}


STAGES = ("L0a", "F", "MOE", "L0b", "F", "MOE", "L1a", "Q", "L1b", "Q")


def kernel(**inputs):
    from concourse import bacc
    from concourse.bass_utils import run_bass_kernel_spmd

    arrays = layouts({k: np.asarray(v) for k, v in inputs.items()})
    nc = bacc.Bacc("TRN2", target_bir_lowering=False, num_devices=1)
    a = {k: nc.dram_tensor(k, v.shape, mybir.dt.from_np(v.dtype), kind="ExternalInput").ap()
         for k, v in arrays.items()}
    a["scratch"] = nc.dram_tensor("scratch", (2, 3, P, 2 * T), BF16, kind="Internal").ap()
    a["scratch2"] = nc.dram_tensor("scratch2", (2, 2, 3, P, 2 * T), BF16, kind="Internal").ap()
    out = nc.dram_tensor("out", (NB * T, P), F32, kind="ExternalOutput").ap()
    build_program(nc, a, out, STAGES)
    r = run_bass_kernel_spmd(nc, [arrays], core_ids=[0])
    return r.results[0]["out"].reshape(NB, T, P)
```

```python
from contextlib import ExitStack

import numpy as np

import concourse.bass as bass
from concourse import mybir

F32 = mybir.dt.float32
BF16 = mybir.dt.bfloat16
I32 = mybir.dt.int32
ALU = mybir.AluOpType
ACT = mybir.ActivationFunctionType
AX = mybir.AxisListType.X

P = 128
NB, T = 16, 256
TT = T // P
NT = NB * TT
PAD = 2
H = 16
HC = 4
NC = H // HC
UN = TT * NC
NPAIR = H // 2
LAG_T, LAG_V = 3, 4
PRING, SRING, TRING = 4, 2, 2
QPART = (0, 0, 1, 0, 2, 1)
KPART = (0, 1, 0, 2, 0, 1)
NBLK = len(QPART)
MASKED = -3.0e38


def wait(eng, sem, value):
    if isinstance(value, int) and value <= 0:
        return
    eng.wait_ge(sem, value)


def over_sequences(eng, body, epilogue=None):
    body(0, 0)
    with eng.Fori(0, (NB - 2) // 2) as i:
        body(i * 2 + 1, 1)
        body(i * 2 + 2, 0)
    body(NB - 1, (NB - 1) % 2)
    if epilogue is not None:
        epilogue(NB, NB % 2)


def clear_semaphores(nc, sems):
    with nc.Block() as block:
        @block.gpsimd
        def _(pool):
            for s in sems:
                pool.sem_clear(s)


class Scope:

    def __init__(self, nc, ctx, stage):
        self.nc, self.ctx, self.stage, self.sems = nc, ctx, stage, []

    def sb(self, name, shape, dt=F32):
        return self.ctx.enter_context(self.nc.sbuf_tensor(f"{self.stage}_{name}", shape, dt))

    def ps(self, name, shape, dt=F32):
        return self.ctx.enter_context(self.nc.psum_tensor(f"{self.stage}_{name}", shape, dt))

    def sem(self, name):
        s = self.ctx.enter_context(self.nc.semaphore(f"{self.stage}_{name}"))
        self.sems.append(s)
        return s


class Chain:

    def __init__(self, eng, sem, start=0):
        self.eng, self.sem, self.n = eng, sem, start

    def __call__(self, ins):
        self.n = self.n + 1
        ins.then_inc(self.sem, 1)
        self.eng.wait_ge(self.sem, self.n)


def load_stage(nc, x, g):
    with ExitStack() as ctx:
        st = Scope(nc, ctx, "load")
        x_in, made = st.sem("x_in"), st.sem("constants_made")
        with nc.Block() as block:
            @block.sync
            def _(sp):
                xv = x.rearrange("(n p) d -> p n d", p=P)
                for k in range(4):
                    sp.dma_start(g.X[:, k * 8:(k + 1) * 8, :], xv[:, k * 8:(k + 1) * 8, :]).then_inc(x_in, 16)
                sp.wait_ge(x_in, 64)

            @block.gpsimd
            def _(pool):
                c = Chain(pool, made)
                c(pool.memset(g.ident[:, :], 0.0))
                c(pool.affine_select(out=g.ident[:, :], in_=g.ident[:, :], compare_op=ALU.not_equal, fill=1.0,
                                     base=0, pattern=[[-1, P]], channel_multiplier=1))
                c(pool.tensor_copy(g.identb[:, :], g.ident[:, :]))
                c(pool.memset(g.maskb[:, :, :], 0.0))
                c(pool.affine_select(out=g.maskb[:, :, :], in_=g.maskb[:, :, :], compare_op=ALU.is_ge, fill=MASKED,
                                     base=0, pattern=[[0, 2], [-1, P]], channel_multiplier=1))
                c(pool.memset(g.neghalf[:, :], -0.5))
                c(pool.memset(g.half[:, :], 0.5))
                c(pool.memset(g.X[:, NT:, :], 0.0))
                c(pool.memset(g.bn6[:, :], 0.0))
        clear = list(st.sems)
        clear_semaphores(nc, clear)


def moments_sems(st):
    st.bn_done, st.moment_step = st.sem("bn_done"), st.sem("moment_step")
    st.var_ready, st.rstd_ready, st.mean_ready = st.sem("var_ready"), st.sem("rstd_ready"), st.sem("mean_ready")


def halves_vector(dve, g, st, src, ntiles):
    with dve.Fori(0, ntiles // 2) as i:
        for k in range(2):
            g.nc.vector.bn_stats(g.bn6[:, bass.ds(i * 12 + 6 * k, 6)], src[:, bass.ds(i * 2 + k, 1), :]
                                 ).then_inc(st.bn_done, 1)


def moments_vector(dve, g, st, eps, bn_count, turn=0, rms=False):
    nc = g.nc
    six = g.bn6[:, :].rearrange("p (n k) -> p n k", k=6)
    mean_e, sq_e, mean_o, sq_o = six[:, :, 1], six[:, :, 2], six[:, :, 4], six[:, :, 5]
    dve.wait_ge(st.bn_done, bn_count)
    step = Chain(dve, st.moment_step, 5 * turn)
    nc.vector.tensor_tensor(g.mean[:, :], mean_e, mean_o, ALU.mult if rms else ALU.add).then_inc(st.moment_step, 1)
    nc.vector.tensor_tensor(g.rstd[:, :], sq_e, sq_o, ALU.add).then_inc(st.moment_step, 1)
    step.n = step.n + 2
    step(nc.vector.tensor_tensor(g.gap[:, :], mean_e, mean_o, ALU.subtract))
    nc.vector.tensor_scalar(g.rstd[:, :], g.rstd[:, :], 1.0 / P, eps, ALU.mult, ALU.add).then_inc(st.moment_step, 1)
    step.n = step.n + 1
    step(nc.vector.tensor_tensor(g.gap[:, :], g.gap[:, :], g.gap[:, :], ALU.mult))
    if rms:
        nc.vector.scalar_tensor_tensor(out=g.mean[:, :], in0=g.gap[:, :], scalar=0.5, in1=g.mean[:, :],
                                       op0=ALU.mult, op1=ALU.add).then_inc(st.mean_ready, 1)
        dve.wait_ge(st.mean_ready, turn + 1)
        nc.vector.tensor_tensor(g.rstd[:, :], g.rstd[:, :], g.mean[:, :], ALU.add).then_inc(st.var_ready, 1)
    else:
        nc.vector.tensor_scalar(g.mean[:, :], g.mean[:, :], 0.5, None, ALU.mult).then_inc(st.mean_ready, 1)
        nc.vector.scalar_tensor_tensor(out=g.rstd[:, :], in0=g.gap[:, :], scalar=0.25, in1=g.rstd[:, :],
                                       op0=ALU.mult, op1=ALU.add).then_inc(st.var_ready, 1)
        dve.wait_ge(st.mean_ready, turn + 1)
    dve.wait_ge(st.rstd_ready, turn + 1)


def moments_pool(pool, g, st, turn=0):
    pool.wait_ge(st.var_ready, turn + 1)
    g.nc.gpsimd.tensor_tensor(g.rstd[:, :], g.rstd[:, :], g.neghalf[:, 0:NT + 2 * PAD], ALU.pow).then_inc(st.rstd_ready, 1)


def load_weights(sp, sem, pairs):
    for dst, src in pairs:
        sp.dma_start(dst[tuple(slice(None) for _ in dst.shape)], src).then_inc(sem, 16)
    sp.wait_ge(sem, 16 * len(pairs))


def in_order(eng, body, lag, head=2):
    for b in range(head):
        body(b, b % 2)
    with eng.Fori(0, (NB - head) // 2) as i:
        body(i * 2 + head, 0)
        body(i * 2 + (head + 1), 1)
    for k in range(lag):
        body(NB + k, k % 2)


def there(b, lag):
    return not isinstance(b, int) or 0 <= b - lag < NB


class Jobs:

    def __init__(self, order, first):
        self.order, self.first = order, first
        self.start = len(first) + sum(j[4] >= 0 for j in order)

    def number(self, b, i):
        if isinstance(b, int) and b == 0:
            return len(self.first) + sum(j[4] >= 0 for j in self.order[:i])
        if isinstance(b, int) and b == NB:
            return self.start + (NB - 1) * len(self.order) + sum(j[4] < 0 for j in self.order[:i])
        return b * len(self.order) + (self.start - len(self.order) + i)

    def at(self, b, slot, place):
        out = []
        for i, (s, p, kind, k, of) in enumerate(self.order):
            if (s, p) != (slot, place):
                continue
            if isinstance(b, int) and (b + of < 0 or (b == NB and of >= 0)):
                continue
            out.append((kind, k, b + of, of % 2, self.number(b, i)))
        return out

    def after(self, b, kind, k):
        i = [(j[2], j[3]) for j in self.order].index((kind, k))
        if isinstance(b, int) and (b < 0 or b + self.order[i][4] < 0):
            return 0
        return self.number(b, i) + 1


def before_first(order, nseq):
    return [(kind, k, j) for j in range(nseq) for kind, k in order]


def attention_stage(nc, g, w, *, causal, rope=False, bias=False, moe=False, name):
    LAG_T, LAG_V = 3, 4
    with ExitStack() as ctx:
        st = Scope(nc, ctx, name)
        sb, ps, sem = st.sb, st.ps, st.sem
        wq, wk, wv, wo = sb("wq", [P, P]), sb("wk", [P, P]), sb("wv", [P, P]), sb("wo", [P, P])
        if rope:
            wqs, wks = sb("wqs", [P, P]), sb("wks", [P, P])
            wkcT, wvcT = sb("wkcT", [32, P]), sb("wvcT", [32, P])
            wk2, wks2, wv2 = sb("wk2", [32, P]), sb("wks2", [32, P]), sb("wv2", [32, P])
            cosT, sinT = sb("cosT", [P, 2, T]), sb("sinT", [P, 2, T])
            roc, ros, qkf = sb("roc", [P, 2 * T]), sb("ros", [P, 2 * T]), sb("qkf", [P, 2 * T])
        if bias:
            bq, bk, bv = sb("bq", [P, 1]), sb("bk", [P, 1]), sb("bv", [P, P])
            bo = sb("bo", [P, P])
        xs, xc = sb("xs", [P, 2, TT, P]), sb("xc", [P, TT, P])
        xnT = sb("xnT", [P, 2, T])
        resid, zero = sb("resid", [P, 2 * T]), sb("zero", [P, 1])
        parts = sb("parts", [P, 2, 3, 2 * T], BF16)
        KROWS = NBLK * 16
        qst = [sb(f"qst{i}", [KROWS, NPAIR, T], BF16) for i in range(2)]
        kst = [sb(f"kst{i}", [KROWS, NPAIR, 2, T], BF16) for i in range(2)]
        vp = [sb(f"vp{i}", [P, TT, H, 32]) for i in range(2)]
        probs = sb("probs", [P, PRING, HC, T])
        probsT = sb("probsT", [P, TRING, TT, HC * P])
        negmax = sb("negmax", [P, PRING, HC])
        osb = sb("osb", [P, TT, NC, P])
        rinv, y, yT = sb("rinv", [P, H]), sb("y", [P, P]), sb("yT", [P, P])
        S = [ps(f"S{i}", [P, HC * T]) for i in range(SRING)]
        PT = [ps(f"PT{k}", [P, HC * P]) for k in range(TT)]
        O = ps("O", [P, NC, P])
        M = ps("M", [P, 512])
        moments_sems(st)
        w_in, zeroed = sem("weights_in"), sem("zeroed")
        wc_ready, wc_copied = sem("weights_multiplied"), sem("weights_copied")
        m_ready, m_read = sem("job_ready"), sem("job_read")
        centred, xs_ready, xp_ready = sem("centred"), sem("xs_ready"), sem("xp_ready")
        qk_summed, hi_ready, res_ready = sem("rotated_sum_ready"), sem("hi_ready"), sem("residue_ready")
        mid_ready, parts_ready = sem("middle_ready"), sem("parts_ready")
        parts_out, st_in = sem("parts_out"), [sem("stacks_in0"), sem("stacks_in1")]
        s_ready, max_ready, exp_done = sem("s_ready"), sem("max_ready"), sem("exp_done")
        t_ready, t_copied = sem("t_ready"), [sem("t_copied0"), sem("t_copied1")]
        pv_done, o_copied, rinv_ready, bo_added = sem("pv_done"), sem("o_copied"), sem("rinv_ready"), sem("bo_added")
        scr = g.scratch
        NIN = NBLK * 3

        front = [("x", 0), ("qk", 0)] + ([("swapped", 0)] if rope else [])
        order = [(0, 1, "u", 0, -1), (1, 1, "w", 0, -1), (2, 0, "x", 0, 2), (2, 2, "o", 0, -1), (3, 1, "qk", 0, 2)]
        order += [(3, 2, "swapped", 0, 2)] if rope else []
        order += [(4, 1, "u", 1, -1), (5, 1, "w", 1, -1), (6, 0, "v", 0, 1), (6, 2, "o", 1, -1)]
        jobs = Jobs(order, before_first(front, 2) + [("v", 0, 0)])

        def keys(u):
            return 1 if causal and u // NC == 0 else TT

        def split(b, u, lag):
            return (b, u - lag, 0) if u >= lag else (b - 1, u - lag + UN, 1)

        def exists(b, u, lag):
            return not (isinstance(b, int) and not 0 <= UN * b + u - lag < UN * NB)

        def tiles_before(b, u, kt=None):
            kts = range(TT) if kt is None else (kt,)
            count = lambda units: sum(k < keys(v) for v in units for k in kts)
            return b * count(range(UN)) + count(range(u))

        def s_view(u):
            n = keys(u) * P
            return S[u % SRING][:, 0:HC * n].rearrange("p (h k) -> p h k", h=HC)

        wloads = [(wq, w["wq"]), (wo, w["wo"])]
        if rope:
            wloads += [(wqs, w["wqs"]), (wkcT, w["wkcT"]), (wvcT, w["wvcT"]), (wk2, w["wk"]), (wks2, w["wks"]),
                       (wv2, w["wv"]), (cosT, w["cosT"]), (sinT, w["sinT"])]
        else:
            wloads += [(wk, w["wk"]), (wv, w["wv"])]
        if bias:
            wloads += [(bq, w["bq"]), (bk, w["bk"]), (bv, w["bv"]), (bo, w["bo"])]
        WIN = 16 * len(wloads)

        with nc.Block() as block:
            @block.sync
            def _(sp):
                load_weights(sp, w_in, wloads)
                sp.wait_ge(zeroed, 3)

                def counts(j, par):
                    v = (j + 1, (j - par) * (8 * NIN), j * UN - UN, j * 16 + 16)
                    return v if isinstance(j, int) else tuple(sp.to_reg(x) for x in v)

                def bounce(par, first, n):
                    split_n, read_n, used_n, out_n = n
                    wait(sp, parts_ready, split_n)
                    wait(sp, st_in[par], read_n)
                    sp.dma_start(scr[par].rearrange("a p n -> p a n"), parts[:, par, :, :]).then_inc(parts_out, 16)
                    if not first:
                        sp.wait_ge(s_ready, used_n)
                    wait(sp, parts_out, out_n)
                    for i in range(NBLK):
                        r = 16 * i
                        sp.dma_start(qst[par][r:r + 16, :, :],
                                     scr[par, QPART[i], :, 0:T].rearrange("(c r) t -> r c t", r=16)
                                     ).then_inc(st_in[par], 16)
                        for hh in range(2):
                            src = scr[par, KPART[i], :, T:2 * T].rearrange("(c h d) t -> h d c t", h=2, d=8)
                            sp.dma_start(kst[par][r + 8 * hh:r + 8 * hh + 8, :, hh, :], src[hh]
                                         ).then_inc(st_in[par], 16)

                bounce(0, True, counts(0, 0))
                bounce(1, True, counts(1, 1))
                bounce(0, False, counts(2, 0))
                with sp.Fori(0, (NB - 2) // 2) as i:
                    odd, even = counts(i * 2 + 3, 1), counts(i * 2 + 4, 0)
                    bounce(1, False, odd)
                    bounce(0, False, even)
                bounce(1, False, counts(NB + 1, 1))
                sp.wait_ge(parts_out, 16 * (NB + PAD))
                for i in range(2):
                    sp.wait_ge(st_in[i], 16 * NIN * (NB + PAD) // 2)

            @block.gpsimd
            def _(pool):
                tt = nc.gpsimd.tensor_tensor
                nc.gpsimd.memset(zero[:, :], 0.0).then_inc(zeroed, 1)
                moments_pool(pool, g, st)
                pool.wait_ge(st.mean_ready, 1)
                pool.wait_ge(st.rstd_ready, 1)

                def x_normalise(j, par):
                    tiles = bass.ds(j * TT, TT)
                    spread = lambda x: x[:, tiles].unsqueeze(2).broadcast_to([P, TT, P])
                    wait(pool, xs_ready, j)
                    if moe:
                        wait(pool, xp_ready, j)
                    tt(xc[:, :, :], g.X[:, tiles, :], spread(g.mean), ALU.subtract).then_inc(centred, 1)
                    wait(pool, centred, j + 1)
                    tt(xs[:, par, :, :], xc[:, :, :], spread(g.rstd), ALU.mult).then_inc(xs_ready, 1)
                    if moe:
                        tt(g.XP[:, tiles, :], xc[:, :, :], spread(g.rstd), ALU.mult).then_inc(xp_ready, 1)

                def split_parts(j, par):
                    if rope:
                        wait(pool, m_read, last_read(j))
                        wait(pool, res_ready, j)
                        tt(qkf[:, :], roc[:, :], ros[:, :], ALU.add).then_inc(qk_summed, 1)
                        wait(pool, hi_ready, j + 1)
                        wait(pool, parts_ready, j)
                        tt(resid[:, :], qkf[:, :], parts[:, par, 0, :], ALU.subtract).then_inc(res_ready, 1)
                        wait(pool, res_ready, j + 1)
                    else:
                        wait(pool, m_read, last_read(j))
                    tt(parts[:, par, 1, :], resid[:, :], zero[:, 0:1].broadcast_to([P, 2 * T]), ALU.add
                       ).then_inc(mid_ready, 1)
                    wait(pool, mid_ready, j + 1)
                    tt(parts[:, par, 2, :], resid[:, :], parts[:, par, 1, :], ALU.subtract).then_inc(parts_ready, 1)

                def last_read(j):
                    if isinstance(j, int) and j < 2:
                        return len(front) * (j + 1)
                    return jobs.after(j - 2, *front[-1])

                x_normalise(0, 0)
                x_normalise(1, 1)
                for i in range(2):
                    nc.gpsimd.memset(kst[i][:, :, :, :], 0.0).then_inc(zeroed, 1)
                for i in range(2):
                    c = Chain(pool, zeroed, 3 + 2 * i)
                    c(nc.gpsimd.memset(vp[i][:, :, :, :], 0.0))
                    c(nc.gpsimd.memset(vp[i][:, :, :, 8:9], 1.0))
                for j in range(2):
                    split_parts(j, j)

                def body(b, par):
                    x_normalise(b + 2, par)
                    split_parts(b + 2, par)

                over_sequences(pool, body)

            @block.tensor
            def _(pe):
                pe.wait_ge(w_in, WIN)
                if rope:
                    for k, (a, c) in enumerate(((wkcT, wk2), (wkcT, wks2), (wvcT, wv2))):
                        ins = nc.tensor.matmul(M[:, k * P:(k + 1) * P], a[:, :], c[:, :], start=True, stop=True)
                    ins.then_inc(wc_ready, 1)
                pe.wait_ge(wc_copied, 1)

                def run(kind, k, j, par, n):
                    wait(pe, m_read, n)
                    if kind == "x":
                        wait(pe, xs_ready, j + 1)
                        for t in range(TT):
                            ins = nc.tensor.transpose(M[:, t * P:(t + 1) * P], xs[:, par, t, :], g.ident[:, :])
                    elif kind in ("qk", "swapped"):
                        a, c = (wq, wk) if kind == "qk" else (wqs, wks)
                        nc.tensor.matmul(M[:, 0:T], a[:, :], xnT[:, par, :], start=True, stop=True)
                        ins = nc.tensor.matmul(M[:, T:2 * T], c[:, :], xnT[:, par, :], start=True, stop=True)
                    elif kind == "v":
                        for t in range(TT):
                            ins = nc.tensor.matmul(M[:, t * P:(t + 1) * P], xnT[:, par, t * P:(t + 1) * P], wv[:, :],
                                                   start=True, stop=True)
                    elif kind == "u":
                        wait(pe, o_copied, j * TT + k + 1)
                        for c in range(NC):
                            ins = nc.tensor.transpose(M[:, c * P:(c + 1) * P], osb[:, k, c, :], g.ident[:, :])
                    elif kind == "w":
                        ins = nc.tensor.transpose(M[:, 0:P], y[:, :], g.ident[:, :])
                    else:
                        ins = nc.tensor.matmul(M[:, 0:P], yT[:, :], wo[:, :], start=True, stop=True)
                    ins.then_inc(m_ready, 1)

                def transposes(b, u):
                    if not exists(b, u, LAG_T):
                        return
                    sq, v, _ = split(b, u, LAG_T)
                    wait(pe, exp_done, sq * UN + v + 1)
                    for kt in range(keys(v)):
                        wait(pe, t_copied[kt], tiles_before(sq, v, kt))
                        for h in range(HC):
                            ins = nc.tensor.transpose(PT[kt][:, h * P:(h + 1) * P],
                                                      probs[:, v % PRING, h, kt * P:(kt + 1) * P], g.ident[:, :])
                        ins.then_inc(t_ready, 1)

                def scores(b, u, par):
                    if not exists(b, u, 0):
                        return
                    if u == 0:
                        wait(pe, st_in[par], (b - par) * (8 * NIN) + 16 * NIN)
                    wait(pe, exp_done, UN * b + u - SRING + 1)
                    t, c, nk = u // NC, u % NC, keys(u) * P
                    out = s_view(u)
                    for i in range(HC // 2):
                        o2 = out[:, 2 * i:2 * i + 2, :]
                        ins = nc.tensor.matmul(o2, qst[par][:, 2 * c + i, t * P:(t + 1) * P],
                                               kst[par][:, 2 * c + i, :, 0:nk], start=True, stop=True)
                        if causal:
                            ins = nc.tensor.matmul(o2[:, :, t * P:(t + 1) * P], g.identb[:, :], g.maskb[:, :, :],
                                                   start=False, stop=True, skip_group_check=True)
                    ins.then_inc(s_ready, 1)

                def values(b, u, par):
                    if not exists(b, u, LAG_V):
                        return
                    sq, v, shift = split(b, u, LAG_V)
                    c, t, nk = v % NC, v // NC, keys(v)
                    if v == 0:
                        wait(pe, m_read, values_read(sq))
                    if c == 0:
                        wait(pe, o_copied, TT * sq + t)
                    for kt in range(nk):
                        wait(pe, t_copied[kt], tiles_before(sq, v, kt) + 1)
                        for h in range(HC):
                            ins = nc.tensor.matmul(O[32 * h:32 * h + 32, c, :], vp[par ^ shift][:, kt, HC * c + h, :],
                                                   probsT[:, v % TRING, kt, h * P:(h + 1) * P],
                                                   start=kt == 0, stop=kt == nk - 1, tile_position=(0, 32 * h))
                    ins.then_inc(pv_done, 1)

                def values_read(sq):
                    return len(jobs.first) if isinstance(sq, int) and sq == 0 else jobs.after(sq - 1, "v", 0)

                for n, (kind, k, j) in enumerate(jobs.first):
                    run(kind, k, j, j, n)

                def body(b, par):
                    for u in range(UN):
                        for place, part in enumerate((lambda: scores(b, u, par), lambda: transposes(b, u),
                                                      lambda: values(b, u, par))):
                            part()
                            for kind, k, j, shift, n in jobs.at(b, u, place):
                                run(kind, k, j, par ^ shift, n)

                over_sequences(pe, body, body)

            @block.scalar
            def _(act):
                if rope:
                    act.wait_ge(wc_ready, 1)
                    for k, dst in enumerate((wk, wks, wv)):
                        ins = nc.scalar.activation(dst[:, :], M[:, k * P:(k + 1) * P], ACT.Copy)
                    ins.then_inc(wc_copied, 1)
                else:
                    act.wait_ge(w_in, WIN)
                    if bias:
                        nc.scalar.activation(bq[:, :], bq[:, :], ACT.Copy, scale=g.score_scale).then_inc(wc_ready, 1)
                    nc.scalar.activation(wq[:, :], wq[:, :], ACT.Copy, scale=g.score_scale).then_inc(wc_copied, 1)
                    if bias:
                        act.wait_ge(wc_ready, 1)

                def exponentials(b, u):
                    if not exists(b, u, 0):
                        return
                    n, r, v = UN * b + u, u % PRING, s_view(u)
                    wait(act, max_ready, n + 1)
                    if exists(b, u, PRING):
                        sq, old, _ = split(b, u, PRING)
                        wait(act, t_ready, tiles_before(sq, old) + keys(old))
                    for h in range(HC):
                        ins = nc.scalar.activation(probs[:, r, h, 0:keys(u) * P], v[:, h, :], ACT.Exp,
                                                   bias=negmax[:, r, h:h + 1])
                    ins.then_inc(exp_done, 1)

                def t_copy(b, u):
                    if not exists(b, u, LAG_T):
                        return
                    sq, v, _ = split(b, u, LAG_T)
                    if keys(v) > 1:
                        wait(act, t_ready, tiles_before(sq, v) + 2)
                        wait(act, pv_done, sq * UN + v - TRING + 1)
                        nc.scalar.activation(probsT[:, v % TRING, 1, :], PT[1][:, :], ACT.Copy
                                             ).then_inc(t_copied[1], 1)

                def read(kind, k, j, par, n):
                    if kind == "x":
                        wait(act, m_ready, n + 1)
                        nc.scalar.activation(xnT[:, par, :], M[:, 0:T], ACT.Copy).then_inc(m_read, 1)
                    elif kind == "qk" and not rope:
                        wait(act, m_ready, n + 1)
                        wait(act, parts_out, (j - 1) * 16)
                        if bias:
                            for half, bb in enumerate((bq, bk)):
                                part = slice(half * T, (half + 1) * T)
                                ins = nc.scalar.activation(parts[:, par, 0, part], M[:, part], ACT.Identity,
                                                           bias=bb[:, 0:1])
                        else:
                            ins = nc.scalar.activation(parts[:, par, 0, :], M[:, :], ACT.Copy)
                        ins.then_inc(hi_ready, 1)
                    elif kind == "v" and not bias:
                        wait(act, m_ready, n + 1)
                        if isinstance(j, int) and j < 2:
                            wait(act, zeroed, 7)
                        wait(act, pv_done, UN * (j - 1))
                        nc.scalar.activation(vp[par][:, :, :, 0:8],
                                             M[:, 0:T].rearrange("p (t h d) -> p t h d", t=TT, h=H), ACT.Copy
                                             ).then_inc(m_read, 1)
                    elif kind == "w":
                        wait(act, m_ready, n + 1)
                        nc.scalar.activation(yT[:, :], M[:, 0:P], ACT.Copy).then_inc(m_read, 1)

                def high_part(j, par):
                    wait(act, qk_summed, j + 1)
                    wait(act, parts_out, (j - 1) * 16)
                    nc.scalar.activation(parts[:, par, 0, :], qkf[:, :], ACT.Copy).then_inc(hi_ready, 1)

                def o_copy(sq, t, before):
                    if isinstance(sq, int) and not 0 <= sq < NB:
                        return
                    wait(act, pv_done, sq * UN + (t + 1) * NC)
                    wait(act, m_ready, before)
                    nc.scalar.activation(osb[:, t, :, :], O[:, :, :], ACT.Copy).then_inc(o_copied, 1)

                for n, (kind, k, j) in enumerate(jobs.first):
                    read(kind, k, j, j, n)
                    if kind == "swapped":
                        high_part(j, j)

                def body(b, par):
                    for u in range(UN):
                        for place, part in enumerate((lambda: t_copy(b, u), lambda: None, lambda: exponentials(b, u))):
                            part()
                            for kind, k, j, shift, n in jobs.at(b, u, place):
                                read(kind, k, j, par ^ shift, n)
                        if u == 3:
                            o_copy(b - 1, 1, jobs.after(b - 1, "u", 1))
                        if u == 5 and rope and not (isinstance(b, int) and b == NB):
                            high_part(b + 2, par)
                        if u == 7:
                            o_copy(b, 0, jobs.after(b, "u", 0))

                over_sequences(act, body, body)

            @block.vector
            def _(dve):
                v_ = nc.vector
                halves_vector(dve, g, st, g.X, NT + 2 * PAD)
                moments_vector(dve, g, st, 1e-5, NT + 2 * PAD)
                dve.wait_ge(w_in, WIN)
                if bias:
                    dve.wait_ge(wc_ready, 1)

                def read(kind, k, j, par, n):
                    if kind == "qk" and rope:
                        wait(dve, m_ready, n + 1)
                        wait(dve, qk_summed, j)
                        v_.tensor_tensor(roc[:, :], M[:, :], cosT[:, :, :].rearrange("p a t -> p (a t)"), ALU.mult
                                         ).then_inc(m_read, 1)
                    elif kind == "swapped":
                        wait(dve, m_ready, n + 1)
                        v_.tensor_tensor(ros[:, :], M[:, :], sinT[:, :, :].rearrange("p a t -> p (a t)"), ALU.mult
                                         ).then_inc(m_read, 1)
                    elif kind == "qk":
                        wait(dve, hi_ready, j + 1)
                        wait(dve, parts_ready, j)
                        if bias:
                            for half, bb in enumerate((bq, bk)):
                                part = slice(half * T, (half + 1) * T)
                                ins = v_.scalar_tensor_tensor(out=resid[:, part], in0=M[:, part], scalar=bb[:, 0:1],
                                                              in1=parts[:, par, 0, part], op0=ALU.add,
                                                              op1=ALU.subtract)
                        else:
                            ins = v_.tensor_tensor(resid[:, :], M[:, :], parts[:, par, 0, :], ALU.subtract)
                        ins.then_inc(m_read, 1)
                    elif kind == "v" and bias:
                        wait(dve, m_ready, n + 1)
                        if isinstance(j, int) and j < 2:
                            wait(dve, zeroed, 7)
                        wait(dve, pv_done, UN * (j - 1))
                        bvb = bv[:, :].rearrange("p (h d) -> p h d", h=H)
                        for t in range(TT):
                            ins = v_.tensor_tensor(vp[par][:, t, :, 0:8],
                                                   M[:, t * P:(t + 1) * P].rearrange("p (h d) -> p h d", h=H),
                                                   bvb, ALU.add)
                        ins.then_inc(m_read, 1)
                    elif kind == "u":
                        wait(dve, m_ready, n + 1)
                        heads = M[:, :].rearrange("p (h d) -> p h d", d=32)
                        v_.reciprocal(rinv[:, :], heads[:, :, 8]).then_inc(rinv_ready, 1)
                        wait(dve, rinv_ready, j * TT + k + 1)
                        v_.tensor_tensor(y[:, :].rearrange("p (h d) -> p h d", d=8), heads[:, :, 0:8],
                                         rinv[:, :].unsqueeze(2).broadcast_to([P, H, 8]), ALU.mult
                                         ).then_inc(m_read, 1)
                    elif kind == "o":
                        wait(dve, m_ready, n + 1)
                        dst = (g.XP if moe else g.X)[:, bass.ds(j * TT + k, 1), :]
                        if moe:
                            wait(dve, xp_ready, j + 1)
                        if bias:
                            v_.tensor_tensor(dst, dst, bo[:, :].unsqueeze(1), ALU.add).then_inc(bo_added, 1)
                            wait(dve, bo_added, j * TT + k + 1)
                        v_.tensor_tensor(dst, dst, M[:, 0:P].unsqueeze(1), ALU.add).then_inc(m_read, 1)

                def maxima(b, u):
                    if not exists(b, u, 0):
                        return
                    n = UN * b + u
                    wait(dve, s_ready, n + 1)
                    wait(dve, exp_done, n - PRING + 1)
                    v_.tensor_reduce(out=negmax[:, u % PRING, :], in_=s_view(u), axis=AX, op=ALU.max,
                                     negate=True).then_inc(max_ready, 1)

                def t_copy(b, u):
                    if not exists(b, u, LAG_T):
                        return
                    sq, v, _ = split(b, u, LAG_T)
                    wait(dve, t_ready, tiles_before(sq, v) + 1)
                    wait(dve, pv_done, sq * UN + v - TRING + 1)
                    v_.tensor_copy(probsT[:, v % TRING, 0, :], PT[0][:, :]).then_inc(t_copied[0], 1)

                for n, (kind, k, j) in enumerate(jobs.first):
                    read(kind, k, j, j, n)

                def body(b, par):
                    for u in range(UN):
                        for place, part in enumerate((lambda: maxima(b, u), lambda: t_copy(b, u), lambda: None)):
                            part()
                            for kind, k, j, shift, n in jobs.at(b, u, place):
                                read(kind, k, j, par ^ shift, n)

                over_sequences(dve, body, body)
        clear = list(st.sems)
        clear_semaphores(nc, clear)


def wide_attention_stage(nc, g, w, name):
    DH, LAG_T, LAG_V = 64, 3, 4
    with ExitStack() as ctx:
        st = Scope(nc, ctx, name)
        sb, ps, sem = st.sb, st.ps, st.sem
        wqk = [sb(f"w{n}", [P, NPAIR, P]) for n in ("q", "qs", "k", "ks")]
        wv, wo = sb("wv", [P, H * DH]), sb("wo", [P, NPAIR, P])
        turn = [sb("turn_q", [P, 2 * T]), sb("turn_k", [P, 2 * T])]
        xs, xnT = sb("xs", [P, 2, TT, P]), sb("xnT", [P, T])
        NTMP = 4
        tmp = sb("tmp", [P, NTMP, 2 * T])
        qw = [sb(f"qw{i}", [P, NPAIR, T]) for i in range(2)]
        kw = [sb(f"kw{i}", [P, NPAIR, 2, T]) for i in range(2)]
        vw = [sb(f"vw{i}", [P, TT, H, DH]) for i in range(2)]
        probs, probsT = sb("probs", [P, PRING, HC, T]), sb("probsT", [P, TRING, TT, HC * P])
        negmax, rowsum, rinv = sb("negmax", [P, PRING, HC]), sb("rowsum", [P, PRING, HC]), sb("rinv", [P, PRING, HC])
        osb, yT = sb("osb", [P, NPAIR, T]), sb("yT", [P, T])
        S = [ps(f"S{i}", [P, HC * T]) for i in range(SRING)]
        PT, O, banks = ps("PT", [P, HC * P]), ps("O", [P, 4, P]), [ps(f"M{i}", [P, 512]) for i in range(2)]
        moments_sems(st)
        w_in, kw_zeroed = sem("weights_in"), sem("kw_zeroed")
        xs_ready, m_ready, qk_ready = sem("xs_ready"), sem("job_ready"), sem("qk_ready")
        m_read = [sem("even_job_read"), sem("odd_job_read")]
        s_ready, max_ready, exp_done = sem("s_ready"), sem("max_ready"), sem("exp_done")
        rinv_ready, norm_done, t_ready = sem("rinv_ready"), sem("norm_done"), sem("t_ready")
        t_copied, pv_done, o_copied = [sem("t_copied0"), sem("t_copied1")], sem("pv_done"), sem("o_copied")

        FRONT = [("x", 0), ("x", 1)] + [(n, p) for p in range(NPAIR) for n in "qk"] + [("v", i) for i in range(4)]
        todo = [(kind, k, 1) for kind, k in FRONT]
        todo[12:12] = [("o", 0, -1)]
        todo[16:16] = [("r", 0, -1)]
        PLACES = 3
        jobs = Jobs([(i // PLACES, i % PLACES, *job) for i, job in enumerate(todo)], before_first(FRONT, 1))
        assert jobs.start % 2 == 0 and len(todo) % 2 == 0

        def numbered(b, u, place):
            out = []
            for kind, k, j, shift, n in jobs.at(b, u, place):
                i = [(x[2], x[3]) for x in jobs.order].index((kind, k))
                if isinstance(n, int):
                    out.append((kind, k, j, shift, n, n % 2, n // 2))
                else:
                    const = jobs.start - len(jobs.order) + i
                    out.append((kind, k, j, shift, n, const % 2, b * (len(jobs.order) // 2) + const // 2))
            return out

        NADD = 3 * NPAIR

        def adds(k):
            return 3 * (k // 2) + k % 2

        def keys(u):
            return 1 if u // NC == 0 else TT

        def split(b, u, lag):
            return (b, u - lag, 0) if u >= lag else (b - 1, u - lag + UN, 1)

        def exists(b, u, lag):
            return not (isinstance(b, int) and not 0 <= UN * b + u - lag < UN * NB)

        def tiles_before(b, u, kt=None):
            kts = range(TT) if kt is None else (kt,)
            count = lambda units: sum(k < keys(v) for v in units for k in kts)
            return b * count(range(UN)) + count(range(u))

        def s_view(u):
            n = keys(u) * P
            return S[u % SRING][:, 0:HC * n].rearrange("p (h k) -> p h k", h=HC)

        loads = list(zip(wqk, (w["wq"], w["wqs"], w["wk"], w["wks"]))) + [
            (wv, w["wv"]), (wo, w["wo"]), (turn[0], w["turn_q"]), (turn[1], w["turn_k"])]

        with nc.Block() as block:
            @block.sync
            def _(sp):
                load_weights(sp, w_in, loads)

            @block.gpsimd
            def _(pool):
                for i in range(2):
                    nc.gpsimd.memset(kw[i][:, :, :, :], 0.0).then_inc(kw_zeroed, 1)
                moments_pool(pool, g, st)
                pool.wait_ge(kw_zeroed, 2)

                def add_turned(j, par, kind, p, bank, before, normalised):
                    k = 2 * p + (kind == "k")
                    wait(pool, m_read[bank], before + 1)
                    a, c = tmp[:, k % NTMP, 0:T], tmp[:, k % NTMP, T:2 * T]
                    wait(pool, s_ready, UN * (j - 1))
                    if kind == "q":
                        wait(pool, qk_ready, j * NADD + adds(k))
                        nc.gpsimd.tensor_tensor(qw[par][:, p, :], a, c, ALU.add).then_inc(qk_ready, 1)
                    else:
                        wait(pool, norm_done, normalised)
                        for hh in range(2):
                            wait(pool, qk_ready, j * NADD + adds(k) + hh)
                            r = slice(DH * hh, DH * hh + DH)
                            nc.gpsimd.tensor_tensor(kw[par][r, p, hh, :], a[r, :], c[r, :], ALU.add
                                                    ).then_inc(qk_ready, 1)

                def normalise(b, u):
                    if not exists(b, u, 1):
                        return
                    sq, v, _ = split(b, u, 1)
                    r, nk = v % PRING, keys(v) * P
                    added = sum(x[2] in "qk" for x in jobs.order if x[0] < u)
                    if exists(b, u, 0):
                        wait(pool, qk_ready, (b + 1) * NADD + adds(added))
                    else:
                        wait(pool, qk_ready, (b + 1) * NADD)
                    wait(pool, rinv_ready, sq * UN + v + 1)
                    pr = probs[:, r, :, 0:nk]
                    nc.gpsimd.tensor_tensor(pr, pr, rinv[:, r, :].unsqueeze(2).broadcast_to([P, HC, nk]),
                                            ALU.mult).then_inc(norm_done, 1)

                for n, (kind, k, j) in enumerate(jobs.first):
                    if kind in "qk":
                        add_turned(0, 0, kind, k, n % 2, n // 2, 0)

                def body(b, par):
                    for u in range(UN):
                        normalise(b, u)
                        for place in range(PLACES):
                            for kind, k, j, shift, n, bank, before in numbered(b, u, place):
                                if kind in "qk":
                                    add_turned(j, par ^ shift, kind, k, bank, before, b * UN + u)

                over_sequences(pool, body, body)

            @block.tensor
            def _(pe):
                pe.wait_ge(w_in, 16 * len(loads))

                def run(kind, k, j, par, n, bank, before):
                    M = banks[bank]
                    wait(pe, m_read[bank], before)
                    if (kind, k) in (("q", 0), ("r", 0)):
                        wait(pe, m_read[bank ^ 1], before + 1 if bank else before)
                    if kind == "x":
                        wait(pe, xs_ready, j + 1)
                        ins = nc.tensor.transpose(M[:, 0:P], xs[:, par, k, :], g.ident[:, :])
                    elif kind in "qk":
                        for s in range(2):
                            ins = nc.tensor.matmul(M[:, s * T:(s + 1) * T], wqk[2 * "qk".index(kind) + s][:, k, :],
                                                   xnT[:, :], start=True, stop=True)
                    elif kind == "v":
                        t, half = k // 2, k % 2
                        ins = nc.tensor.matmul(M[:, :], xnT[:, t * P:(t + 1) * P], wv[:, half * 512:(half + 1) * 512],
                                               start=True, stop=True)
                    elif kind == "o":
                        wait(pe, o_copied, j * 4 + 4)
                        for p in range(NPAIR):
                            ins = nc.tensor.matmul(M[:, 0:T], wo[:, p, :], osb[:, p, :], start=p == 0,
                                                   stop=p == NPAIR - 1)
                    else:
                        for t in range(TT):
                            ins = nc.tensor.transpose(M[:, t * P:(t + 1) * P], yT[:, t * P:(t + 1) * P],
                                                      g.ident[:, :])
                    ins.then_inc(m_ready, 1)

                def transposes(b, u, kt):
                    if not exists(b, u, LAG_T):
                        return
                    sq, v, _ = split(b, u, LAG_T)
                    if kt >= keys(v):
                        return
                    if kt == 0:
                        wait(pe, norm_done, sq * UN + v + 1)
                    wait(pe, t_copied[0], tiles_before(sq, v, 0) + kt)
                    wait(pe, t_copied[1], tiles_before(sq, v, 1))
                    for h in range(HC):
                        ins = nc.tensor.transpose(PT[:, h * P:(h + 1) * P],
                                                  probs[:, v % PRING, h, kt * P:(kt + 1) * P], g.ident[:, :])
                    ins.then_inc(t_ready, 1)

                def scores(b, u, par):
                    if not exists(b, u, 0):
                        return
                    if u == 0:
                        wait(pe, qk_ready, (b + 1) * NADD)
                    wait(pe, exp_done, UN * b + u - SRING + 1)
                    t, c, nk = u // NC, u % NC, keys(u) * P
                    out = s_view(u)
                    for i in range(HC // 2):
                        o2 = out[:, 2 * i:2 * i + 2, :]
                        nc.tensor.matmul(o2, qw[par][:, 2 * c + i, t * P:(t + 1) * P], kw[par][:, 2 * c + i, :, 0:nk],
                                         start=True, stop=True)
                        ins = nc.tensor.matmul(o2[:, :, t * P:(t + 1) * P], g.identb[:, :], g.maskb[:, :, :],
                                               start=False, stop=True, skip_group_check=True)
                    ins.then_inc(s_ready, 1)

                def values(b, u, par):
                    if not exists(b, u, LAG_V):
                        return
                    sq, v, shift = split(b, u, LAG_V)
                    n, c = sq * UN + v, v % NC
                    for kt in range(keys(v)):
                        wait(pe, t_copied[kt], tiles_before(sq, v, kt) + 1)
                    if v == 0:
                        half = len(jobs.first) // 2
                        for bank in range(2):
                            wait(pe, m_read[bank], half if isinstance(sq, int) and sq == 0 else
                                 (jobs.start // 2 - len(jobs.order) // 2) + sq * (len(jobs.order) // 2))
                    if c % 2 == 0:
                        wait(pe, o_copied, sq * 4 + v // 2)
                    vv, nk = vw[par ^ shift], keys(v)
                    for i in range(2):
                        for kt in range(nk):
                            for hh in range(2):
                                h = 2 * i + hh
                                ins = nc.tensor.matmul(O[DH * hh:DH * hh + DH, 2 * (c % 2) + i, :],
                                                       vv[:, kt, HC * c + h, :],
                                                       probsT[:, v % TRING, kt, h * P:(h + 1) * P],
                                                       start=kt == 0, stop=kt == nk - 1, tile_position=(0, DH * hh))
                    ins.then_inc(pv_done, 1)

                for n, (kind, k, j) in enumerate(jobs.first):
                    run(kind, k, j, j, n, n % 2, n // 2)

                def body(b, par):
                    for u in range(UN):
                        for place, part in enumerate((
                                lambda: transposes(b, u, 0), lambda: scores(b, u, par), lambda: transposes(b, u, 1))):
                            part()
                            for kind, k, j, shift, n, bank, before in numbered(b, u, place):
                                run(kind, k, j, par ^ shift, n, bank, before)
                        values(b, u, par)

                over_sequences(pe, body, body)

            @block.scalar
            def _(act):
                def exponentials(b, u):
                    if not exists(b, u, 0):
                        return
                    n, r, v = UN * b + u, u % PRING, s_view(u)
                    wait(act, max_ready, n + 1)
                    if exists(b, u, PRING):
                        sq, old, _ = split(b, u, PRING)
                        wait(act, t_ready, tiles_before(sq, old) + keys(old))
                    for h in range(HC):
                        ins = nc.scalar.activation(probs[:, r, h, 0:keys(u) * P], v[:, h, :], ACT.Exp,
                                                   bias=negmax[:, r, h:h + 1], accum_out=rowsum[:, r, h:h + 1])
                    ins.then_inc(exp_done, 1)

                def t_copy(b, u):
                    if not exists(b, u, LAG_T):
                        return
                    sq, v, _ = split(b, u, LAG_T)
                    if keys(v) > 1:
                        wait(act, t_ready, tiles_before(sq, v) + 2)
                        wait(act, pv_done, sq * UN + v - TRING + 1)
                        nc.scalar.activation(probsT[:, v % TRING, 1, :], PT[:, :], ACT.Copy).then_inc(t_copied[1], 1)

                def read(kind, k, j, par, n, bank):
                    M = banks[bank]
                    if kind == "x":
                        wait(act, m_ready, n + 1)
                        nc.scalar.activation(xnT[:, k * P:(k + 1) * P], M[:, 0:P], ACT.Copy
                                             ).then_inc(m_read[bank], 1)
                    elif kind == "v":
                        wait(act, m_ready, n + 1)
                        wait(act, pv_done, UN * (j - 1))
                        t, half = k // 2, k % 2
                        nc.scalar.activation(vw[par][:, t, half * 8:(half + 1) * 8, :],
                                             M[:, :].rearrange("p (h d) -> p h d", h=8), ACT.Copy
                                             ).then_inc(m_read[bank], 1)
                    elif kind == "o":
                        wait(act, m_ready, n + 1)
                        nc.scalar.activation(yT[:, :], M[:, 0:T], ACT.Copy).then_inc(m_read[bank], 1)

                def o_copy(sq, group):
                    if isinstance(sq, int) and not 0 <= sq < NB:
                        return
                    t, c2 = group // 2, group % 2
                    wait(act, pv_done, sq * UN + 2 * group + 2)
                    wait(act, m_ready, jobs.after(sq, "o", 0))
                    nc.scalar.activation(osb[:, 4 * c2:4 * c2 + 4, t * P:(t + 1) * P], O[:, :, :], ACT.Copy
                                         ).then_inc(o_copied, 1)

                for n, (kind, k, j) in enumerate(jobs.first):
                    read(kind, k, j, j, n, n % 2)

                def body(b, par):
                    for u in range(UN):
                        for place, part in enumerate((lambda: None, lambda: exponentials(b, u), lambda: t_copy(b, u))):
                            part()
                            for kind, k, j, shift, n, bank, before in numbered(b, u, place):
                                read(kind, k, j, par ^ shift, n, bank)
                        if u in (1, 3):
                            o_copy(b - 1, 2 + u // 2)
                        if u in (5, 7):
                            o_copy(b, (u - 5) // 2)

                over_sequences(act, body, body)

            @block.vector
            def _(dve):
                halves_vector(dve, g, st, g.X, NT + 2 * PAD)
                moments_vector(dve, g, st, 1e-5, NT + 2 * PAD)
                dve.wait_ge(w_in, 16 * len(loads))

                def x_normalise(j, par):
                    if not (isinstance(j, int) and j < 2):
                        wait(dve, m_ready, 2 if isinstance(j, int) and j == 2 else jobs.after(j - 3, "x", 1))
                    for t in range(TT):
                        tile = j * TT + t
                        ins = nc.vector.tensor_scalar(xs[:, par, t:t + 1, :], g.X[:, bass.ds(tile, 1), :],
                                                      g.mean[:, bass.ds(tile, 1)], g.rstd[:, bass.ds(tile, 1)],
                                                      ALU.subtract, ALU.mult)
                    ins.then_inc(xs_ready, 1)

                def read(kind, k, j, n, bank):
                    M = banks[bank]
                    if kind in "qk":
                        i = 2 * k + (kind == "k")
                        wait(dve, m_ready, n + 1)
                        wait(dve, qk_ready, j * NADD + adds(i - NTMP + 1))
                        nc.vector.tensor_tensor(tmp[:, i % NTMP, :], M[:, :], turn[kind == "k"][:, :], ALU.mult
                                                ).then_inc(m_read[bank], 1)
                    elif kind == "r":
                        wait(dve, m_ready, n + 1)
                        dst = g.X[:, bass.ds(j * TT, TT), :]
                        nc.vector.tensor_tensor(dst, dst, M[:, 0:T].rearrange("p (t o) -> p t o", t=TT), ALU.add
                                                ).then_inc(m_read[bank], 1)

                def maxima(b, u):
                    if not exists(b, u, 0):
                        return
                    n = UN * b + u
                    wait(dve, s_ready, n + 1)
                    wait(dve, exp_done, n - PRING + 1)
                    nc.vector.tensor_reduce(out=negmax[:, u % PRING, :], in_=s_view(u), axis=AX, op=ALU.max,
                                            negate=True).then_inc(max_ready, 1)

                def reciprocals(b, u):
                    if not exists(b, u, 1):
                        return
                    sq, v, _ = split(b, u, 1)
                    n, r = sq * UN + v, v % PRING
                    wait(dve, exp_done, n + 1)
                    wait(dve, norm_done, n - PRING + 1)
                    nc.vector.reciprocal(rinv[:, r, :], rowsum[:, r, :]).then_inc(rinv_ready, 1)

                def t_copy(b, u):
                    if not exists(b, u, LAG_T):
                        return
                    sq, v, _ = split(b, u, LAG_T)
                    wait(dve, t_ready, tiles_before(sq, v) + 1)
                    wait(dve, pv_done, sq * UN + v - TRING + 1)
                    nc.vector.tensor_copy(probsT[:, v % TRING, 0, :], PT[:, :]).then_inc(t_copied[0], 1)

                for j in range(2):
                    x_normalise(j, j)
                for n, (kind, k, j) in enumerate(jobs.first):
                    read(kind, k, 0, n, n % 2)

                def body(b, par):
                    for u in range(UN):
                        for place, part in enumerate((lambda: t_copy(b, u), lambda: maxima(b, u),
                                                      lambda: reciprocals(b, u))):
                            part()
                            for kind, k, j, shift, n, bank, before in numbered(b, u, place):
                                read(kind, k, j, n, bank)
                        if u == 6 and exists(b, u, 0):
                            x_normalise(b + 2, par)

                over_sequences(dve, body, body)
        clear = list(st.sems)
        clear_semaphores(nc, clear)


def hyperbolic_attention_stage(nc, g, w, name):
    LAG_D, LAG_E, LAG_T, LAG_V = 2, 3, 5, 6
    NCOL = 3 * P + H + 1
    with ExitStack() as ctx:
        st = Scope(nc, ctx, name)
        sb, ps, sem = st.sb, st.ps, st.sem
        wall, ball, wo, bo = sb("wall", [P, NCOL]), sb("ball", [P, NCOL]), sb("wo", [P, P]), sb("bo", [P, P])
        thr, safe, curv = sb("thr", [P, 1]), sb("safe", [P, 1]), sb("curv", [P, H])
        soft, one = sb("soft", [P, H]), sb("one", [P, 1])
        xs, xc, xnT = sb("xs", [P, 2, TT, P]), sb("xc", [P, TT, P]), sb("xnT", [P, T])
        F = [sb(f"F{i}", [P, TT, NCOL]) for i in range(2)]
        sg, oma, sal = sb("sg", [P, TT, H + 1]), sb("oma", [P, TT, H]), sb("sal", [P, TT, H])
        SA, SPK = sb("SA", [P, NT + 2 * PAD, H]), sb("SPK", [P, NT + 2 * PAD])
        sq, ops = sb("sq", [P, TT, 2 * P]), sb("ops", [P, TT, 3, P])
        n2, rn, rn2, z, gz = (sb(n, [P, TT, 2 * H]) for n in ("n2", "rn", "rn2", "z", "gz"))
        squares, roots, work = ([sb(f"{n}{i}", [P, TT, width]) for i, width in enumerate((3 * H, 2 * H))]
                                for n in ("squares", "roots", "root_work"))
        zero, resid, parts = sb("zero", [P, 1]), sb("resid", [P, 2, 2 * T]), sb("parts", [P, 2, 2, 3, 2 * T], BF16)
        KROWS = NBLK * 16
        qst = [[sb(f"qst{i}{k}", [KROWS, NPAIR, T], BF16) for k in range(2)] for i in range(2)]
        kst = [[sb(f"kst{i}{k}", [KROWS, NPAIR, 2, T], BF16) for k in range(2)] for i in range(2)]
        vp = [sb(f"vp{i}", [P, TT, H, 32]) for i in range(2)]
        DRING, WRING = 2, 4
        dd, ww = sb("dd", [P, DRING, HC * T]), sb("ww", [P, WRING, HC * T])
        probs, probsT = sb("probs", [P, PRING, HC, T]), sb("probsT", [P, TRING, TT, HC * P])
        top, negtop = sb("top", [P, PRING, HC]), sb("negtop", [P, PRING, HC])
        rec, rinv, y, yT = sb("rec", [P, H]), sb("rinv", [P, H]), sb("y", [P, P]), sb("yT", [P, P])
        osb = sb("osb", [P, TT, NC, P])
        SE, SI = ps("SE", [P, HC * T]), ps("SI", [P, HC * T])
        PT, O, M = [ps(f"PT{k}", [P, HC * P]) for k in range(TT)], ps("O", [P, NC, P]), ps("M", [P, 512])
        moments_sems(st)
        w_in, setup, zeroed = sem("weights_in"), sem("setup"), sem("zeroed")
        centred, xs_ready, m_ready, m_read = sem("centred"), sem("xs_ready"), sem("job_ready"), sem("job_read")
        sig_ready, front, logs_ready, roots_ready, hi_ready, parts_ready = (sem(n) for n in (
            "sigmoid_exp_ready", "front_steps", "root_logs_ready", "roots_ready", "hi_ready", "parts_ready"))
        parts_out, st_in, v_ready = sem("parts_out"), [sem("stacks_in0"), sem("stacks_in1")], sem("v_ready")
        i_ready, d_ready, u_ready, root_ready, arg_ready, dist_ready = (sem(n) for n in (
            "inner_ready", "d_ready", "u_ready", "root_ready", "arg_ready", "dist_ready"))
        log_ready, acosh_ready, part_step = sem("log_ready"), sem("acosh_ready"), sem("middle_part_ready")
        e_ready, top_ready, neg_ready, exp_done = (sem(n) for n in ("e_ready", "top_ready", "neg_ready", "exp_done"))
        rec_ready, rinv_ready, t_ready = sem("rec_ready"), sem("rinv_ready"), sem("t_ready")
        t_copied, pv_done, o_copied, act_step = [sem("t_copied0"), sem("t_copied1")], sem("pv_done"), sem("o_copied"), sem("act_step")
        bo_added = sem("bias_added")
        scr = g.scratch2
        NIN = 2 * NBLK * 3

        early, late = [("x", 0), ("f", 0), ("f", 1)], [("s", 0), ("s", 1)]
        jobs = Jobs([(0, 1, "x", 0, 2), (1, 0, "s", 0, 1), (1, 2, "s", 1, 1), (2, 1, "f", 0, 2), (2, 2, "u", 0, -1),
                     (3, 1, "f", 1, 2), (3, 2, "w", 0, -1), (4, 1, "o", 0, -1), (6, 1, "u", 1, -1),
                     (7, 0, "w", 1, -1), (7, 2, "o", 1, -1)],
                    before_first(early + late, 1) + [(kind, k, 1) for kind, k in early])

        def after_front(j, kind, k):
            first = [(x[0], x[1], x[2]) for x in jobs.first]
            if isinstance(j, int) and (kind, k, j) in first:
                return first.index((kind, k, j)) + 1
            return jobs.after(j - (1 if kind == "s" else 2), kind, k)

        def keys(u):
            return 1 if u // NC == 0 else TT

        def split(b, u, lag):
            return (b, u - lag, 0) if u >= lag else (b - 1, u - lag + UN, 1)

        def exists(b, u, lag):
            return not (isinstance(b, int) and not 0 <= UN * b + u - lag < UN * NB)

        def unit(b, u, lag):
            sq_, v, shift = split(b, u, lag)
            return sq_, v, sq_ * UN + v, keys(v) * P, shift

        def tiles_before(b, u, kt=None):
            kts = range(TT) if kt is None else (kt,)
            count = lambda units: sum(k < keys(v) for v in units for k in kts)
            return b * count(range(UN)) + count(range(u))

        loads = [(wall, w["wall"]), (ball, w["ball"]), (wo, w["wo"]), (bo, w["bo"]), (thr, w["thr"]),
                 (safe, w["qk_scale"]), (curv, w["log_k"])]
        C = [1.0]
        NSERIES = 6
        for k in range(1, NSERIES + 1):
            C.append(C[-1] / (2 * k * (2 * k + 1)))
        SMALL = float(np.float32(1.0 + 1e-6) - np.float32(1.0))
        SC = g.score_scale
        STEPS_N, STEPS_A, STEPS_SA, STEPS_R, STEPS_Z, STEPS_S = 2, 9, 14, 16, 16 + 5 + 4, 16 + 5 + NSERIES + 1 + 6
        STEPS = STEPS_S + 5

        with nc.Block() as block:
            @block.sync
            def _(sp):
                load_weights(sp, w_in, loads)
                sp.wait_ge(zeroed, 5)

                def counts(j, par):
                    v = (2 * j + 2, (j - par) * (8 * NIN), (j - 1) * UN, j * 32 + 32)
                    return v if isinstance(j, int) else tuple(sp.to_reg(x) for x in v)

                def bounce(par, first, n):
                    split_n, read_n, used_n, out_n = n
                    wait(sp, parts_ready, split_n)
                    wait(sp, st_in[par], read_n)
                    for kind in range(2):
                        sp.dma_start(scr[par, kind].rearrange("a p n -> p a n"), parts[:, par, kind, :, :]
                                     ).then_inc(parts_out, 16)
                    if not first:
                        sp.wait_ge(e_ready, used_n)
                    wait(sp, parts_out, out_n)
                    for kind in (1, 0):
                        for i in range(NBLK):
                            r = 16 * i
                            sp.dma_start(qst[par][kind][r:r + 16, :, :],
                                         scr[par, kind, QPART[i], :, 0:T].rearrange("(c r) t -> r c t", r=16)
                                         ).then_inc(st_in[par], 16)
                            for hh in range(2):
                                src = scr[par, kind, KPART[i], :, T:2 * T].rearrange("(c h d) t -> h d c t", h=2, d=8)
                                sp.dma_start(kst[par][kind][r + 8 * hh:r + 8 * hh + 8, :, hh, :], src[hh]
                                             ).then_inc(st_in[par], 16)

                bounce(0, True, counts(0, 0))
                bounce(1, True, counts(1, 1))
                bounce(0, False, counts(2, 0))
                with sp.Fori(0, (NB - 2) // 2) as i:
                    odd, even = counts(i * 2 + 3, 1), counts(i * 2 + 4, 0)
                    bounce(1, False, odd)
                    bounce(0, False, even)
                sp.wait_ge(parts_out, 32 * (NB + 1))
                for i in range(2):
                    sp.wait_ge(st_in[i], 16 * NIN * (NB // 2 + 1 - i))

            @block.gpsimd
            def _(pool):
                tt = nc.gpsimd.tensor_tensor
                nc.gpsimd.memset(zero[:, :], 0.0).then_inc(zeroed, 1)
                moments_pool(pool, g, st)
                pool.wait_ge(st.mean_ready, 1)
                pool.wait_ge(st.rstd_ready, 1)

                def x_normalise(j, par):
                    tiles = bass.ds(j * TT, TT)
                    spread = lambda x: x[:, tiles].unsqueeze(2).broadcast_to([P, TT, P])
                    wait(pool, xs_ready, j)
                    tt(xc[:, :, :], g.X[:, tiles, :], spread(g.mean), ALU.subtract).then_inc(centred, 1)
                    wait(pool, centred, j + 1)
                    tt(xs[:, par, :, :], xc[:, :, :], spread(g.rstd), ALU.mult).then_inc(xs_ready, 1)

                def split_parts(j, par, k):
                    wait(pool, m_read, after_front(j, "s", k))
                    tt(parts[:, par, k, 1, :], resid[:, k, :], zero[:, 0:1].broadcast_to([P, 2 * T]), ALU.add
                       ).then_inc(part_step, 1)
                    wait(pool, part_step, 2 * j + k + 1)
                    tt(parts[:, par, k, 2, :], resid[:, k, :], parts[:, par, k, 1, :], ALU.subtract
                       ).then_inc(parts_ready, 1)

                x_normalise(0, 0)
                x_normalise(1, 1)
                for i in range(2):
                    for k in range(2):
                        nc.gpsimd.memset(kst[i][k][:, :, :, :], 0.0).then_inc(zeroed, 1)
                for i in range(2):
                    c = Chain(pool, zeroed, 5 + 2 * i)
                    c(nc.gpsimd.memset(vp[i][:, :, :, :], 0.0))
                    c(nc.gpsimd.memset(vp[i][:, :, :, 8:9], 1.0))

                def argument(b, u):
                    if not exists(b, u, 0):
                        return
                    n, nk = UN * b + u, keys(u) * P * HC
                    wait(pool, root_ready, n + 1)
                    x = ww[:, u % WRING, 0:nk]
                    nc.gpsimd.tensor_tensor(x, x, dd[:, u % DRING, 0:nk], ALU.add).then_inc(arg_ready, 1)

                for k in range(2):
                    split_parts(0, 0, k)

                def body(b, par):
                    for u in range(UN):
                        last = isinstance(b, int) and b == NB
                        if u == 0 and not last:
                            x_normalise(b + 2, par)
                        argument(b, u)
                        if u in (1, 2) and not last:
                            split_parts(b + 1, par ^ 1, u - 1)

                over_sequences(pool, body, body)

            @block.tensor
            def _(pe):
                pe.wait_ge(w_in, 16 * len(loads))

                def run(kind, k, j, par, n):
                    wait(pe, m_read, n)
                    if kind == "x":
                        wait(pe, xs_ready, j + 1)
                        for t in range(TT):
                            ins = nc.tensor.transpose(M[:, t * P:(t + 1) * P], xs[:, par, t, :], g.ident[:, :])
                    elif kind == "f":
                        ins = nc.tensor.matmul(M[:, 0:NCOL], xnT[:, k * P:(k + 1) * P], wall[:, :], start=True,
                                               stop=True)
                    elif kind == "s":
                        wait(pe, front, (j + 1) * STEPS)
                        for t in range(TT):
                            qop = ops[:, t, k, :]
                            kop = ops[:, t, 2, :] if k else F[par][:, t, P:2 * P]
                            nc.tensor.transpose(M[:, t * P:(t + 1) * P], qop, g.ident[:, :])
                            ins = nc.tensor.transpose(M[:, T + t * P:T + (t + 1) * P], kop, g.ident[:, :])
                    elif kind == "u":
                        wait(pe, o_copied, j * TT + k + 1)
                        for c in range(NC):
                            ins = nc.tensor.transpose(M[:, c * P:(c + 1) * P], osb[:, k, c, :], g.ident[:, :])
                    elif kind == "w":
                        ins = nc.tensor.transpose(M[:, 0:P], y[:, :], g.ident[:, :])
                    else:
                        ins = nc.tensor.matmul(M[:, 0:P], yT[:, :], wo[:, :], start=True, stop=True)
                    ins.then_inc(m_ready, 1)

                def transposes(b, u):
                    if not exists(b, u, LAG_T):
                        return
                    sq_, v, n, nk, _ = unit(b, u, LAG_T)
                    wait(pe, exp_done, n + 1)
                    for kt in range(nk // P):
                        wait(pe, t_copied[kt], tiles_before(sq_, v, kt))
                        for h in range(HC):
                            ins = nc.tensor.transpose(PT[kt][:, h * P:(h + 1) * P],
                                                      probs[:, v % PRING, h, kt * P:(kt + 1) * P], g.ident[:, :])
                        ins.then_inc(t_ready, 1)

                def products(out, par, kind, v, nk, mask):
                    t, c = v // NC, v % NC
                    out = out[:, 0:HC * nk].rearrange("p (h k) -> p h k", h=HC)
                    for i in range(HC // 2):
                        o2 = out[:, 2 * i:2 * i + 2, :]
                        ins = nc.tensor.matmul(o2, qst[par][kind][:, 2 * c + i, t * P:(t + 1) * P],
                                               kst[par][kind][:, 2 * c + i, :, 0:nk], start=True, stop=True)
                        if mask:
                            ins = nc.tensor.matmul(o2[:, :, t * P:(t + 1) * P], g.identb[:, :], g.maskb[:, :, :],
                                                   start=False, stop=True, skip_group_check=True)
                    return ins

                def inner(b, u, par):
                    if not exists(b, u, 0):
                        return
                    if u == 0:
                        wait(pe, st_in[par], (b - par) * (8 * NIN) + 16 * NIN)
                    wait(pe, d_ready, UN * b + u)
                    products(SI, par, 1, u, keys(u) * P, False).then_inc(i_ready, 1)

                def euclid(b, u, par):
                    if not exists(b, u, LAG_E):
                        return
                    sq_, v, n, nk, shift = unit(b, u, LAG_E)
                    wait(pe, top_ready, n)
                    products(SE, par ^ shift, 0, v, nk, True).then_inc(e_ready, 1)

                def values(b, u, par):
                    if not exists(b, u, LAG_V):
                        return
                    sq_, v, n, nk, shift = unit(b, u, LAG_V)
                    c, t = v % NC, v // NC
                    for kt in range(nk // P):
                        wait(pe, t_copied[kt], tiles_before(sq_, v, kt) + 1)
                    if v == 0:
                        wait(pe, v_ready, sq_ + 1)
                    if c == 0:
                        wait(pe, o_copied, 2 * sq_ + t)
                    for kt in range(nk // P):
                        for h in range(HC):
                            ins = nc.tensor.matmul(O[32 * h:32 * h + 32, c, :], vp[par ^ shift][:, kt, HC * c + h, :],
                                                   probsT[:, v % TRING, kt, h * P:(h + 1) * P],
                                                   start=kt == 0, stop=kt == nk // P - 1, tile_position=(0, 32 * h))
                    ins.then_inc(pv_done, 1)

                for n, (kind, k, j) in enumerate(jobs.first):
                    run(kind, k, j, j, n)

                def body(b, par):
                    for u in range(UN):
                        for place, part in enumerate((
                                lambda: [transposes(b, u), inner(b, u, par)], lambda: euclid(b, u, par),
                                lambda: values(b, u, par))):
                            part()
                            for kind, k, j, shift, n in jobs.at(b, u, place):
                                run(kind, k, j, par ^ shift, n)

                over_sequences(pe, body, body)

            @block.scalar
            def _(act):
                nc.scalar.preload_act_table_set("natural_log_exp_and_others")
                act.wait_ge(w_in, 16 * len(loads))
                act.wait_ge(setup, 3)
                nc.scalar.activation(soft[:, :], soft[:, :], ACT.Exp).then_inc(act_step, 1)
                nc.scalar.activation(safe[:, :], safe[:, :], ACT.Exp, scale=-1.0).then_inc(act_step, 1)
                act.wait_ge(act_step, 1)
                nc.scalar.activation(soft[:, :], soft[:, :], ACT.Ln, bias=one[:, 0:1]).then_inc(act_step, 1)

                def read(kind, k, j, par, n):
                    if kind == "x":
                        wait(act, m_ready, n + 1)
                        nc.scalar.activation(xnT[:, :], M[:, 0:T], ACT.Copy).then_inc(m_read, 1)
                    elif kind == "s":
                        wait(act, m_ready, n + 1)
                        wait(act, parts_out, (j - 1) * 32)
                        nc.scalar.activation(parts[:, par, k, 0, :], M[:, :], ACT.Copy).then_inc(hi_ready, 1)
                    elif kind == "w":
                        wait(act, m_ready, n + 1)
                        nc.scalar.activation(yT[:, :], M[:, 0:P], ACT.Copy).then_inc(m_read, 1)

                def sigmoid_exp(j, par):
                    wait(act, front, j * STEPS + STEPS_N)
                    nc.scalar.activation(sg[:, :, :], F[par][:, :, 3 * P:], ACT.Exp, scale=-1.0
                                         ).then_inc(sig_ready, 1)

                def inverse_roots(j, i):
                    wait(act, front, j * STEPS + (STEPS_A, STEPS_S)[i])
                    nc.scalar.activation(roots[i][:, :, :], squares[i][:, :, :], ACT.Ln).then_inc(logs_ready, 1)
                    wait(act, logs_ready, 2 * j + i + 1)
                    nc.scalar.activation(roots[i][:, :, :], roots[i][:, :, :], ACT.Exp, scale=-0.5
                                         ).then_inc(roots_ready, 1)

                def v_copy(j, par):
                    wait(act, front, j * STEPS + STEPS_N)
                    if isinstance(j, int) and j < 2:
                        wait(act, zeroed, 9)
                    wait(act, pv_done, UN * (j - 1))
                    nc.scalar.activation(vp[par][:, :, :, 0:8],
                                         F[par][:, :, 2 * P:3 * P].rearrange("p t (h d) -> p t h d", d=8), ACT.Copy
                                         ).then_inc(v_ready, 1)

                def root(b, u):
                    if not exists(b, u, 0):
                        return
                    n, nk = UN * b + u, keys(u) * P * HC
                    x = ww[:, u % WRING, 0:nk]
                    wait(act, u_ready, n + 1)
                    nc.scalar.activation(x, x, ACT.Ln).then_inc(log_ready, 1)
                    wait(act, log_ready, n + 1)
                    nc.scalar.activation(x, x, ACT.Exp, scale=0.5).then_inc(root_ready, 1)

                def distance(b, u):
                    if not exists(b, u, LAG_D):
                        return
                    sq_, v, n, nk, _ = unit(b, u, LAG_D)
                    x = ww[:, v % WRING, 0:HC * nk]
                    t, c = v // NC, v % NC
                    wait(act, arg_ready, n + 1)
                    nc.scalar.activation(x, x, ACT.Ln, bias=one[:, 0:1]).then_inc(acosh_ready, 1)
                    wait(act, acosh_ready, n + 1)
                    if v == 0:
                        wait(act, front, sq_ * STEPS + STEPS_SA)
                    for h in range(HC):
                        y = x[:, h * nk:(h + 1) * nk]
                        sa = SA[:, bass.ds(sq_ * TT + t, 1), HC * c + h:HC * c + h + 1].rearrange("p a b -> p (a b)")
                        ins = nc.scalar.activation(y, y, ACT.Square, scale=sa)
                    ins.then_inc(dist_ready, 1)

                def exponentials(b, u):
                    if not exists(b, u, LAG_E):
                        return
                    sq_, v, n, nk, _ = unit(b, u, LAG_E)
                    r = v % PRING
                    wait(act, neg_ready, n + 1)
                    for h in range(HC):
                        y = probs[:, r, h, 0:nk]
                        ins = nc.scalar.activation(y, y, ACT.Exp, bias=negtop[:, r, h:h + 1])
                    ins.then_inc(exp_done, 1)

                def o_copy(sq_, t):
                    if isinstance(sq_, int) and sq_ < 0:
                        return
                    wait(act, pv_done, sq_ * UN + (t + 1) * NC)
                    wait(act, m_ready, jobs.after(sq_, "u", t))
                    nc.scalar.activation(osb[:, t, :, :], O[:, :, :], ACT.Copy).then_inc(o_copied, 1)

                for n, (kind, k, j) in enumerate(jobs.first):
                    read(kind, k, j, j, n)
                    if (kind, k) == ("f", 1):
                        sigmoid_exp(j, j)
                        inverse_roots(j, 0)
                        inverse_roots(j, 1)
                v_copy(0, 0)

                def body(b, par):
                    last = isinstance(b, int) and b == NB
                    for u in range(UN):
                        for place, part in enumerate((lambda: distance(b, u), lambda: root(b, u),
                                                      lambda: exponentials(b, u))):
                            part()
                            for kind, k, j, shift, n in jobs.at(b, u, place):
                                read(kind, k, j, par ^ shift, n)
                        if u == 1:
                            o_copy(b - 1, 0)
                        if u == 3 and not last:
                            sigmoid_exp(b + 2, par)
                        if u in (4, 7) and not last:
                            inverse_roots(b + 2, u // 7)
                        if u == 5:
                            o_copy(b - 1, 1)
                        if u == 6 and not last:
                            v_copy(b + 1, par ^ 1)

                over_sequences(act, body, body)

            @block.vector
            def _(dve):
                v_ = nc.vector
                halves_vector(dve, g, st, g.X, NT + 2 * PAD)
                moments_vector(dve, g, st, 1e-5, NT + 2 * PAD)
                dve.wait_ge(w_in, 16 * len(loads))
                c = Chain(dve, setup)
                c(v_.memset(one[:, :], 1.0))
                c(v_.tensor_scalar(soft[:, :], curv[:, :], -1.0, None, ALU.mult))
                c(v_.tensor_tensor(soft[:, :], soft[:, :], curv[:, :], ALU.min))
                c(v_.tensor_scalar(curv[:, :], curv[:, :], 0.0, None, ALU.max))
                dve.wait_ge(act_step, 3)
                c(v_.tensor_tensor(curv[:, :], curv[:, :], soft[:, :], ALU.add))
                c(v_.tensor_scalar(curv[:, :], curv[:, :], 1e-6, None, ALU.add))
                c(v_.reciprocal(curv[:, :], curv[:, :]))
                c(v_.tensor_scalar(safe[:, :], safe[:, :], 1.0, None, ALU.add))
                c(v_.reciprocal(safe[:, :], safe[:, :]))
                c(v_.tensor_scalar(safe[:, :], safe[:, :], 1.5, None, ALU.mult))

                def read(kind, k, j, par, n):
                    if kind == "f":
                        wait(dve, m_ready, n + 1)
                        wait(dve, v_ready, j - 1)
                        v_.tensor_tensor(F[par][:, k, :], M[:, 0:NCOL], ball[:, :], ALU.add).then_inc(m_read, 1)
                    elif kind == "s":
                        wait(dve, hi_ready, 2 * j + k + 1)
                        wait(dve, parts_ready, 2 * j + k - 1)
                        v_.tensor_tensor(resid[:, k, :], M[:, :], parts[:, par, k, 0, :], ALU.subtract
                                         ).then_inc(m_read, 1)
                    elif kind == "u":
                        wait(dve, m_ready, n + 1)
                        heads = M[:, :].rearrange("p (h d) -> p h d", d=32)
                        v_.reciprocal(rec[:, :], heads[:, :, 8]).then_inc(rec_ready, 1)
                        wait(dve, rec_ready, j * TT + k + 1)
                        v_.tensor_scalar(rinv[:, :], rec[:, :], SPK[:, bass.ds(j * TT + k, 1)], None, ALU.mult
                                         ).then_inc(rinv_ready, 1)
                        wait(dve, rinv_ready, j * TT + k + 1)
                        v_.tensor_tensor(y[:, :].rearrange("p (h d) -> p h d", d=8), heads[:, :, 0:8],
                                         rinv[:, :].unsqueeze(2).broadcast_to([P, H, 8]), ALU.mult
                                         ).then_inc(m_read, 1)
                    elif kind == "o":
                        wait(dve, m_ready, n + 1)
                        dst = g.X[:, bass.ds(j * TT + k, 1), :]
                        v_.tensor_tensor(dst, dst, bo[:, :].unsqueeze(1), ALU.add).then_inc(bo_added, 1)
                        wait(dve, bo_added, j * TT + k + 1)
                        v_.tensor_tensor(dst, dst, M[:, 0:P].unsqueeze(1), ALU.add).then_inc(m_read, 1)

                def front_operands(j, par, piece):
                    f = F[par]
                    fl = lambda x: x[:, :, :].rearrange("p t k -> p (t k)")
                    space = squares[1]
                    first = sq[:, :, :].rearrange("p t (k d) -> p (t k) d", d=8)[:, :, 0]
                    c = Chain(dve, front, j * STEPS + (0, STEPS_N, STEPS_A, STEPS_R, STEPS_Z, STEPS_S)[piece])

                    def refine(i):
                        x, y_, a = squares[i][:, :, :], roots[i][:, :, :], work[i][:, :, :]
                        wait(dve, roots_ready, 2 * j + i + 1)
                        c(v_.tensor_tensor(a, y_, y_, ALU.mult))
                        c(v_.tensor_tensor(a, a, x, ALU.mult))
                        c(v_.tensor_scalar(a, a, -0.5, 1.5, ALU.mult, ALU.add))
                        c(v_.tensor_tensor(y_, y_, a, ALU.mult))

                    if piece == 0:
                        wait(dve, m_read, after_front(j, "f", 1))
                        qk = f[:, :, 0:2 * P]
                        c(v_.tensor_tensor(sq[:, :, :], qk, qk, ALU.mult))
                        c(v_.tensor_reduce(out=fl(n2), in_=sq[:, :, :].rearrange("p t (k d) -> p (t k) d", d=8),
                                           axis=AX, op=ALU.add))
                        done = STEPS_N
                    elif piece == 1:
                        wait(dve, sig_ready, j + 1)
                        c(v_.tensor_scalar(sg[:, :, :], sg[:, :, :], 1.0, None, ALU.add))
                        c(v_.reciprocal(sg[:, :, :], sg[:, :, :]))
                        alpha = sg[:, :, 0:H]
                        c(v_.tensor_scalar(SPK[:, bass.ds(j * TT, TT)], sg[:, :, H], thr[:, 0:1], None, ALU.is_gt))
                        c(v_.tensor_tensor(sal[:, :, :], alpha,
                                           curv[:, :].unsqueeze(1).broadcast_to([P, TT, H]), ALU.mult))
                        c(v_.tensor_scalar(oma[:, :, :], alpha, -SC, SC, ALU.mult, ALU.add))
                        for t in range(TT):
                            v_.tensor_tensor(ops[:, t, 0, :].rearrange("p (h d) -> p h d", d=8),
                                             f[:, t, 0:P].rearrange("p (h d) -> p h d", d=8),
                                             oma[:, t, :].unsqueeze(2).broadcast_to([P, H, 8]), ALU.mult)
                        c(v_.tensor_scalar(squares[0][:, :, 0:H], sal[:, :, :], 1e-30, None, ALU.max))
                        c(v_.tensor_scalar(squares[0][:, :, H:], n2[:, :, :], 1e-24, None, ALU.max))
                        done = STEPS_A
                    elif piece == 2:
                        refine(0)
                        c(v_.tensor_tensor(SA[:, bass.ds(j * TT, TT), :], sal[:, :, :], roots[0][:, :, 0:H], ALU.mult))
                        c(v_.tensor_scalar(rn[:, :, :], roots[0][:, :, H:], safe[:, 0:1], None, ALU.mult))
                        c(v_.tensor_tensor(fl(rn2), fl(rn), fl(rn), ALU.mult))
                        done = STEPS_R
                    elif piece == 3:
                        c(v_.scalar_tensor_tensor(out=fl(z), in0=first, scalar=-2.0, in1=fl(n2), op0=ALU.mult,
                                                  op1=ALU.add))
                        c(v_.tensor_tensor(fl(space), fl(n2), first, ALU.subtract))
                        c(v_.tensor_tensor(fl(z), fl(z), fl(rn2), ALU.mult))
                        c(v_.tensor_tensor(fl(space), fl(space), fl(rn2), ALU.mult))
                        c(v_.tensor_scalar(fl(z), fl(z), 1e-8, None, ALU.max))
                        c(v_.tensor_scalar(fl(gz), fl(z), C[NSERIES], None, ALU.mult))
                        for k in range(NSERIES - 1, NSERIES - 4, -1):
                            c(v_.scalar_tensor_tensor(out=fl(gz), in0=fl(gz), scalar=C[k], in1=fl(z), op0=ALU.add,
                                                      op1=ALU.mult))
                        done = STEPS_Z
                    elif piece == 4:
                        for k in range(NSERIES - 4, 0, -1):
                            c(v_.scalar_tensor_tensor(out=fl(gz), in0=fl(gz), scalar=C[k], in1=fl(z), op0=ALU.add,
                                                      op1=ALU.mult))
                        c(v_.tensor_scalar(fl(gz), fl(gz), C[0], None, ALU.add))
                        c(v_.tensor_tensor(fl(rn), fl(rn), fl(gz), ALU.mult))
                        c(v_.tensor_tensor(fl(gz), fl(gz), fl(gz), ALU.mult))
                        c(v_.tensor_tensor(fl(space), fl(space), fl(gz), ALU.mult))
                        c(v_.tensor_scalar(fl(space), fl(space), 1.0, None, ALU.add))
                        c(v_.tensor_scalar(rn[:, :, 0:H], rn[:, :, 0:H], -1.0, None, ALU.mult))
                        for t in range(TT):
                            ins = v_.tensor_tensor(ops[:, t, 1:3, :].rearrange("p s (h d) -> p (s h) d", d=8),
                                                   f[:, t, 0:2 * P].rearrange("p (k d) -> p k d", d=8),
                                                   rn[:, t, :].unsqueeze(2).broadcast_to([P, 2 * H, 8]), ALU.mult)
                        c(ins)
                        done = STEPS_S
                    else:
                        refine(1)
                        out = ops[:, :, 1:3, :].rearrange("p t s (h d) -> p t (s h) d", d=8)[:, :, :, 0]
                        c(v_.tensor_tensor(out, space[:, :, :], roots[1][:, :, :], ALU.mult))
                        done = STEPS
                    if isinstance(j, int):
                        assert c.n == j * STEPS + done, (c.n, done)

                def excess(b, u):
                    if not exists(b, u, 0):
                        return
                    n, nk = UN * b + u, keys(u) * P * HC
                    d, x = dd[:, u % DRING, 0:nk], ww[:, u % WRING, 0:nk]
                    wait(dve, i_ready, n + 1)
                    wait(dve, arg_ready, n - DRING + 1)
                    v_.tensor_scalar(d, SI[:, 0:nk], 1.0, SMALL, ALU.subtract, ALU.max).then_inc(d_ready, 1)
                    wait(dve, d_ready, n + 1)
                    wait(dve, top_ready, n - WRING + 1)
                    v_.scalar_tensor_tensor(out=x, in0=d, scalar=2.0, in1=d, op0=ALU.add, op1=ALU.mult
                                            ).then_inc(u_ready, 1)

                def scores(b, u):
                    if exists(b, u, LAG_E):
                        _, ev, en, nk, _ = unit(b, u, LAG_E)
                        r, x = ev % PRING, ww[:, ev % WRING, 0:HC * nk]
                        for h in range(HC):
                            part = slice(h * nk, (h + 1) * nk)
                            ins = v_.tensor_tensor_reduce(
                                out=probs[:, r, h, 0:nk], in0=SE[:, part], in1=x[:, part], scale=1.0, scalar=MASKED,
                                op0=ALU.subtract, op1=ALU.max, accum_out=top[:, r, h:h + 1])
                        ins.then_inc(top_ready, 1)
                        wait(dve, top_ready, en + 1)
                        v_.tensor_scalar(negtop[:, r, :], top[:, r, :], -1.0, None, ALU.mult).then_inc(neg_ready, 1)

                def score_waits(b, u):
                    if not exists(b, u, LAG_E):
                        return
                    _, _, n, _, _ = unit(b, u, LAG_E)
                    wait(dve, e_ready, n + 1)
                    wait(dve, dist_ready, n + 1)
                    if exists(b, u, LAG_E + PRING):
                        old_sq, old, _, _, _ = unit(b, u, LAG_E + PRING)
                        wait(dve, t_ready, tiles_before(old_sq, old) + keys(old))

                def t_copy(b, u):
                    if not exists(b, u, LAG_T):
                        return score_waits(b, u)
                    sq_, v, n, nk, _ = unit(b, u, LAG_T)
                    for kt in range(nk // P):
                        wait(dve, t_ready, tiles_before(sq_, v) + kt + 1)
                        wait(dve, pv_done, n - TRING + 1)
                        if kt == nk // P - 1:
                            score_waits(b, u)
                        v_.tensor_copy(probsT[:, v % TRING, kt, :], PT[kt][:, :]).then_inc(t_copied[kt], 1)

                for n, (kind, k, j) in enumerate(jobs.first):
                    read(kind, k, j, j, n)
                    if (kind, k) == ("f", 1):
                        for piece in range(6 - j):
                            front_operands(j, j, piece)

                def body(b, par):
                    last = isinstance(b, int) and b == NB
                    for u in range(UN):
                        for place, part in enumerate((lambda: [excess(b, u), t_copy(b, u)], lambda: scores(b, u),
                                                      lambda: None)):
                            part()
                            for kind, k, j, shift, n in jobs.at(b, u, place):
                                read(kind, k, j, par ^ shift, n)
                        if u == 0 and not last:
                            front_operands(b + 1, par ^ 1, 5)
                        if u in (3, 4, 5, 6, 7) and not last:
                            front_operands(b + 2, par, u - 3)

                over_sequences(dve, body, body)
        clear = list(st.sems)
        clear_semaphores(nc, clear)


def moe_stage(nc, g, w, name):
    E, G, EPG, HK = 8, 2, 4, 2
    with ExitStack() as ctx:
        st = Scope(nc, ctx, name)
        sb, ps, sem = st.sb, st.ps, st.sem
        wa, wb = sb("wa", [P, 2 * HK, P]), sb("wb", [P, 2 * HK, P])
        wso, w2 = sb("wso", [P, HK, P]), sb("w2", [P, HK, E * P])
        wg, bg = sb("wg", [P, G + E]), sb("bg", [P, G + E])
        n1, n2 = sb("n1", [P, P]), sb("n2", [P, P])
        XPT = sb("XPT", [P, NB * T])
        xs, xt = sb("xs", [P, 2, TT, P]), sb("xt", [P, 2, T])
        logits = sb("logits", [P, NT + 2 * PAD, G + E])
        gmax, gexp, gsum, gsel = sb("gmax", [P, NT]), sb("gexp", [P, NT, G]), sb("gsum", [P, NT]), sb("gsel", [P, NT, G])
        emax, esum = sb("emax", [P, NT * G]), sb("esum", [P, NT * G])
        prob, ahead, tie = sb("prob", [P, NT * G, EPG]), sb("ahead", [P, NT * G, EPG, EPG]), sb("tie", [P, NT * G, EPG, EPG])
        rank, earlier = sb("rank", [P, NT * G, EPG]), sb("earlier", [P, EPG, EPG])
        weight = sb("weight", [P, NT * E])
        gate, hid = sb("gate", [P, 2 * HK * T]), sb("hid", [P, 2, 2 * HK, T])
        acc = sb("acc", [P, 2, 2, P])
        GA, GB = ps("GA", [P, 2 * HK * T]), ps("GB", [P, 2 * HK * T])
        Y = [ps(f"Y{i}", [P, 4 * P]) for i in range(2)]
        SH, M = ps("SH", [P, 512]), ps("M", [P, 512])
        moments_sems(st)
        w_in, made = sem("weights_in"), sem("earlier_made")
        xs_ready, xT_ready, xt_ready, xp_ready, xpt_ready = (sem(n) for n in (
            "xs_ready", "xT_ready", "xt_ready", "xp_ready", "xpt_ready"))
        lg_ready, lg_used, gate_step, gate_act = (sem(n) for n in ("lg_ready", "lg_used", "gate_step", "gate_act"))
        ga_ready, gb_ready, silu_done, hid_ready = (sem(n) for n in ("ga_ready", "gb_ready", "silu_done", "hid_ready"))
        sh_ready, sh_used, y_ready, acc_step = (sem(n) for n in ("sh_ready", "sh_used", "y_ready", "acc_step"))
        add_step, x_done = sem("add_step"), sem("x_done")
        loads = [(wa, w["wa"]), (wb, w["wb"]), (wso, w["wso"]), (w2, w["w2"]), (wg, w["wg"]), (bg, w["bg"]),
                 (n1, w["n1"]), (n2, w["n2"])]
        NBN = NT

        with nc.Block() as block:
            @block.sync
            def _(sp):
                load_weights(sp, w_in, loads)

            @block.gpsimd
            def _(pool):
                c = Chain(pool, made)
                c(nc.gpsimd.memset(earlier[:, :, :], 1.0))
                c(nc.gpsimd.affine_select(out=earlier[:, :, :], in_=earlier[:, :, :], compare_op=ALU.is_gt, fill=0.0,
                                          base=0, pattern=[[1, EPG], [-1, EPG]], channel_multiplier=0))
                moments_pool(pool, g, st, 0)
                moments_pool(pool, g, st, 1)

            @block.tensor
            def _(pe):
                pe.wait_ge(w_in, 16 * len(loads))

                def gating(b, par):
                    if there(b, 0):
                        wait(pe, xs_ready, b + 1)
                        wait(pe, xpt_ready, b - 1)
                        xT = (GA, GB)[par]
                        for t in range(TT):
                            ins = nc.tensor.transpose(xT[:, t * P:(t + 1) * P], xs[:, par, t, :], g.ident[:, :])
                        ins.then_inc(xT_ready, 1)
                    if there(b, 1):
                        wait(pe, xt_ready, b)
                        wait(pe, lg_used, b - 1)
                        for t in range(TT):
                            ins = nc.tensor.matmul(M[:, t * 16:t * 16 + G + E], xt[:, par ^ 1, t * P:(t + 1) * P],
                                                   wg[:, :], start=True, stop=True)
                        ins.then_inc(lg_ready, 1)

                in_order(pe, gating, 1)

                def up(b, which, dst, used, done):
                    if not there(b, 0):
                        return
                    wait(pe, used, b)
                    for k in range(2 * HK):
                        ins = nc.tensor.matmul(dst[:, k * T:(k + 1) * T], which[:, k, :], XPT[:, bass.ds(b * T, T)],
                                               start=True, stop=True)
                    ins.then_inc(done, 1)

                def down(b, par, t):
                    wait(pe, sh_used, b * TT + t)
                    for kk in range(HK):
                        ins = nc.tensor.matmul(SH[:, 0:P], hid[:, par, kk, t * P:(t + 1) * P], wso[:, kk, :],
                                               start=kk == 0, stop=kk == HK - 1)
                    ins.then_inc(sh_ready, 1)
                    for half in range(2):
                        wait(pe, acc_step, (b * TT + t - 1) * (E + 1) + 4 * (half + 1))
                        for kk in range(HK):
                            ins = nc.tensor.matmul(Y[half][:, :], hid[:, par, HK + kk, t * P:(t + 1) * P],
                                                   w2[:, kk, half * 4 * P:(half + 1) * 4 * P],
                                                   start=kk == 0, stop=kk == HK - 1)
                        ins.then_inc(y_ready, 1)

                wait(pe, xpt_ready, NB)
                wait(pe, xp_ready, NB)

                def experts(b, par):
                    up(b, wa, GA, silu_done, ga_ready)
                    if there(b, 1):
                        wait(pe, hid_ready, b)
                        down(b - 1, par ^ 1, 0)
                    up(b, wb, GB, hid_ready, gb_ready)
                    if there(b, 1):
                        down(b - 1, par ^ 1, 1)

                in_order(pe, experts, 1)

            @block.scalar
            def _(act):
                def gating(b, par):
                    if there(b, 0):
                        wait(act, xT_ready, b + 1)
                        wait(act, lg_ready, b - 1)
                        xT = (GA, GB)[par]
                        nc.scalar.activation(xt[:, par, :], xT[:, 0:T], ACT.Copy).then_inc(xt_ready, 1)
                        nc.scalar.activation(XPT[:, bass.ds(b * T, T)], xT[:, 0:T], ACT.Copy).then_inc(xpt_ready, 1)
                        nc.scalar.activation(g.XP[:, bass.ds(b * TT, TT), :], xs[:, par, :, :], ACT.Copy
                                             ).then_inc(xp_ready, 1)

                in_order(act, gating, 0)
                act.wait_ge(gate_act, 1)
                nc.scalar.activation(gexp[:, :, :], gexp[:, :, :], ACT.Exp).then_inc(gate_act, 1)
                act.wait_ge(gate_act, 3)
                nc.scalar.activation(prob[:, :, :], prob[:, :, :], ACT.Exp).then_inc(gate_act, 1)

                def experts(b, par):
                    wait(act, ga_ready, b + 1)
                    wait(act, hid_ready, b)
                    nc.scalar.activation(gate[:, :], GA[:, :], ACT.Silu).then_inc(silu_done, 1)

                in_order(act, experts, 0)

            @block.vector
            def _(dve):
                halves_vector(dve, g, st, g.XP, NT)
                moments_vector(dve, g, st, 1e-6, NT, 0, rms=True)
                dve.wait_ge(w_in, 16 * len(loads))

                def gating(b, par):
                    if there(b, 0):
                        wait(dve, xT_ready, b - 1)
                        wait(dve, xp_ready, b - 1)
                        for t in range(TT):
                            tile = b * TT + t
                            ins = nc.vector.scalar_tensor_tensor(
                                out=xs[:, par, t:t + 1, :], in0=g.XP[:, bass.ds(tile, 1), :],
                                scalar=g.rstd[:, bass.ds(tile, 1)], in1=n1[:, :].unsqueeze(1),
                                op0=ALU.mult, op1=ALU.mult)
                        ins.then_inc(xs_ready, 1)
                    if there(b, 1):
                        wait(dve, lg_ready, b)
                        ins = nc.vector.tensor_tensor(
                            logits[:, bass.ds((b - 1) * TT, TT), :],
                            M[:, 0:32].rearrange("p (t k) -> p t k", t=TT)[:, :, 0:G + E],
                            bg[:, :].unsqueeze(1).broadcast_to([P, TT, G + E]), ALU.add)
                        ins.then_inc(lg_used, 1)

                in_order(dve, gating, 1)
                dve.wait_ge(lg_used, NB)
                c = Chain(dve, gate_step)
                v = nc.vector
                gl, el = logits[:, 0:NT, 0:G], logits[:, 0:NT, G:].rearrange("p n (g e) -> p n g e", g=G)
                flat = lambda x: x.rearrange("p (n g) e -> p n g e", g=G)
                pairs = lambda x: x.rearrange("p (n g) -> p n g", g=G)
                c(v.tensor_reduce(out=gmax[:, :], in_=gl, axis=AX, op=ALU.max))
                v.tensor_tensor(gexp[:, :, :], gl, gmax[:, :].unsqueeze(2).broadcast_to([P, NT, G]), ALU.subtract
                                ).then_inc(gate_act, 1)
                c(v.tensor_reduce(out=pairs(emax[:, :]), in_=el, axis=AX, op=ALU.max))
                dve.wait_ge(gate_act, 2)
                v.tensor_tensor(flat(prob[:, :, :]), el,
                                pairs(emax[:, :]).unsqueeze(3).broadcast_to([P, NT, G, EPG]), ALU.subtract
                                ).then_inc(gate_act, 1)
                c(v.tensor_reduce(out=gsum[:, :], in_=gexp[:, :, :], axis=AX, op=ALU.add))
                c(v.reciprocal(gsum[:, :], gsum[:, :]))
                c(v.tensor_tensor(gsel[:, :, 0], gexp[:, :, 0], gexp[:, :, 1], ALU.is_ge))
                c(v.tensor_scalar(gsel[:, :, 1], gsel[:, :, 0], -1.0, 1.0, ALU.mult, ALU.add))
                c(v.tensor_tensor(gexp[:, :, :], gexp[:, :, :], gsel[:, :, :], ALU.mult))
                c(v.tensor_tensor(gexp[:, :, :], gexp[:, :, :], gsum[:, :].unsqueeze(2).broadcast_to([P, NT, G]),
                                  ALU.mult))
                dve.wait_ge(gate_act, 4)
                c(v.tensor_reduce(out=esum[:, :], in_=prob[:, :, :], axis=AX, op=ALU.add))
                c(v.reciprocal(esum[:, :], esum[:, :]))
                c(v.tensor_tensor(esum[:, :], esum[:, :], gexp[:, :, :].rearrange("p n g -> p (n g)"), ALU.mult))
                c(v.tensor_tensor(prob[:, :, :], prob[:, :, :], esum[:, :].unsqueeze(2).broadcast_to([P, NT * G, EPG]),
                                  ALU.mult))
                full = [P, NT * G, EPG, EPG]
                mine_, other = prob[:, :, :].unsqueeze(3).broadcast_to(full), prob[:, :, :].unsqueeze(2).broadcast_to(full)
                c(v.tensor_tensor(ahead[:, :, :, :], other, mine_, ALU.is_gt))
                c(v.tensor_tensor(tie[:, :, :, :], other, mine_, ALU.is_equal))
                dve.wait_ge(made, 2)
                c(v.tensor_tensor(tie[:, :, :, :], tie[:, :, :, :],
                                  earlier[:, :, :].unsqueeze(1).broadcast_to(full), ALU.mult))
                c(v.tensor_tensor(ahead[:, :, :, :], ahead[:, :, :, :], tie[:, :, :, :], ALU.add))
                c(v.tensor_reduce(out=rank[:, :, :], in_=ahead[:, :, :, :], axis=AX, op=ALU.add))
                c(v.scalar_tensor_tensor(out=weight[:, :].rearrange("p (n e) -> p n e", e=EPG), in0=rank[:, :, :],
                                         scalar=2.0, in1=prob[:, :, :], op0=ALU.is_lt, op1=ALU.mult))
                dve.wait_ge(xp_ready, NB)

                def combine(b, t):
                    tile = b * TT + t
                    a = acc[:, t, :, :]
                    n = tile * 9
                    wait(dve, sh_ready, tile + 1)
                    v.tensor_tensor(a[:, 0:1, :], g.XP[:, bass.ds(tile, 1), :], SH[:, 0:P].unsqueeze(1), ALU.add
                                    ).then_inc(sh_used, 1)
                    for e in range(E):
                        if e % 4 == 0:
                            wait(dve, y_ready, tile * 2 + e // 4 + 1)
                        src = Y[e // 4][:, (e % 4) * P:(e % 4 + 1) * P]
                        we = weight[:, bass.ds(tile * E + e, 1)]
                        k = e % 2
                        if e == 0:
                            wait(dve, sh_used, tile + 1)
                        elif e >= 2:
                            wait(dve, acc_step, n + e - 1)
                        if e == 1:
                            ins = v.tensor_scalar(a[:, 1, :], src, we, None, ALU.mult)
                        else:
                            ins = v.scalar_tensor_tensor(out=a[:, k, :], in0=src, scalar=we, in1=a[:, k, :],
                                                         op0=ALU.mult, op1=ALU.add)
                        ins.then_inc(acc_step, 1)
                    wait(dve, acc_step, n + E)
                    v.tensor_tensor(g.XP[:, bass.ds(tile, 1), :], a[:, 0:1, :], a[:, 1:2, :], ALU.add
                                    ).then_inc(acc_step, 1)
                    wait(dve, acc_step, n + 9)
                    v.bn_stats(g.bn6[:, bass.ds(tile * 6, 6)], g.XP[:, bass.ds(tile, 1), :]).then_inc(st.bn_done, 1)

                def experts(b, par):
                    if there(b, 1):
                        combine(b - 1, 0)
                    if there(b, 0):
                        wait(dve, gb_ready, b + 1)
                        wait(dve, silu_done, b + 1)
                        v.tensor_tensor(hid[:, par, :, :], gate[:, :].rearrange("p (k t) -> p k t", t=T),
                                        GB[:, :].rearrange("p (k t) -> p k t", t=T), ALU.mult).then_inc(hid_ready, 1)
                    if there(b, 1):
                        combine(b - 1, 1)

                in_order(dve, experts, 1)
                moments_vector(dve, g, st, 1e-6, 2 * NT, 1, rms=True)
                with dve.Fori(0, NT // 2) as i:
                    for k in range(2):
                        tile = i * 2 + k
                        row, out = g.XP[:, bass.ds(tile, 1), :], g.X[:, bass.ds(tile, 1), :]
                        v.scalar_tensor_tensor(out=row, in0=row, scalar=g.rstd[:, bass.ds(tile, 1)],
                                               in1=n2[:, :].unsqueeze(1), op0=ALU.mult, op1=ALU.mult
                                               ).then_inc(add_step, 1)
                    for k in range(2):
                        tile = i * 2 + k
                        row, out = g.XP[:, bass.ds(tile, 1), :], g.X[:, bass.ds(tile, 1), :]
                        wait(dve, add_step, tile + 1)
                        v.tensor_tensor(out, out, row, ALU.add).then_inc(x_done, 1)
        clear = list(st.sems)
        clear_semaphores(nc, clear)


def qlora_stage(nc, g, w, name):
    NBLOCK, R = 3, 32
    with ExitStack() as ctx:
        st = Scope(nc, ctx, name)
        sb, ps, sem = st.sb, st.ps, st.sem
        NL = 2 * NBLOCK
        qw, scl = sb("qw", [P, NL, P], I32), sb("scl", [P, NL, P])
        la, lb = sb("la", [R, NL, P]), sb("lb", [R, NL, P])
        wt = sb("wt", [P, NL, P])
        b1, b2 = sb("b1", [P, NBLOCK, P]), sb("b2", [P, NBLOCK])
        gam, bet = sb("gam", [P, NBLOCK]), sb("bet", [P, NBLOCK])
        HT = sb("HT", [P, NB * T])
        zs, yT, hT = sb("zs", [P, 2, TT, P]), sb("yT", [P, 2, T]), sb("hT", [P, 2, T])
        ZT = [ps(f"ZT{i}", [P, 512]) for i in range(2)]
        H2 = [ps(f"H2{i}", [P, 512]) for i in range(2)]
        Y1 = [ps(f"Y1{i}", [P, 512]) for i in range(2)]
        moments_sems(st)
        w_in, deq, lora_ready, w_ready = sem("weights_in"), sem("dequantised"), sem("lora_ready"), sem("weights_ready")
        zs_ready, zT_ready, act_done, h2_ready, h_ready, ht_copied, y1_ready, y1_used = (sem(n) for n in (
            "zs_ready", "zT_ready", "act_done", "h2_ready", "h_ready", "ht_copied", "y1_ready", "y1_used"))
        loads = [(qw, w["qw"]), (scl, w["scl"]), (la, w["la"]), (lb, w["lb"]), (b1, w["b1"]), (b2, w["b2"]),
                 (gam, w["gam"]), (bet, w["bet"])]
        ROUNDS = range(NBLOCK + 1)

        with nc.Block() as block:
            @block.sync
            def _(sp):
                load_weights(sp, w_in, loads)

            @block.gpsimd
            def _(pool):
                for r in ROUNDS:
                    moments_pool(pool, g, st, r)

            @block.tensor
            def _(pe):
                pe.wait_ge(w_in, 16 * len(loads))
                lo = [ZT[0], H2[0]]
                for i in range(NL):
                    ins = nc.tensor.matmul(lo[i // 4][:, (i % 4) * P:(i % 4 + 1) * P], la[:, i, :], lb[:, i, :],
                                           start=True, stop=True)
                ins.then_inc(lora_ready, 1)
                pe.wait_ge(w_ready, 2)
                for r in ROUNDS:
                    def step(b, par, r=r):
                        n = r * NB + b
                        if there(b, 0):
                            wait(pe, zs_ready, n + 1)
                            wait(pe, act_done, n - 1)
                            for t in range(TT):
                                ins = nc.tensor.transpose(ZT[par][:, t * P:(t + 1) * P], zs[:, par, t, :],
                                                          g.ident[:, :])
                            ins.then_inc(zT_ready, 1)
                        if there(b, 1) and r > 0:
                            wait(pe, act_done, n)
                            wait(pe, h_ready, n - 2)
                            nc.tensor.matmul(H2[par ^ 1][:, 0:T], wt[:, 2 * r - 1, :], yT[:, par ^ 1, :],
                                             start=True, stop=True).then_inc(h2_ready, 1)
                        if there(b, 2):
                            wait(pe, h_ready, n - 1)
                            wait(pe, y1_used, n - 3)
                            for t in range(TT):
                                if r < NBLOCK:
                                    ins = nc.tensor.matmul(Y1[par][:, t * P:(t + 1) * P],
                                                           hT[:, par, t * P:(t + 1) * P], wt[:, 2 * r, :],
                                                           start=True, stop=True)
                                else:
                                    ins = nc.tensor.transpose(Y1[par][:, t * P:(t + 1) * P],
                                                              hT[:, par, t * P:(t + 1) * P], g.ident[:, :])
                            ins.then_inc(y1_ready, 1)
                    in_order(pe, step, 2, 4)

            @block.scalar
            def _(act):
                act.wait_ge(w_in, 16 * len(loads))
                for r in ROUNDS:
                    def step(b, par, r=r):
                        n = r * NB + b
                        if there(b, 0):
                            wait(act, zT_ready, n + 1)
                            if r == 0:
                                wait(act, y1_ready, n - 1)
                                nc.scalar.activation(hT[:, par, :], ZT[par][:, 0:T], ACT.Copy).then_inc(h_ready, 1)
                                nc.scalar.activation(HT[:, bass.ds(b * T, T)], ZT[par][:, 0:T], ACT.Copy
                                                     ).then_inc(act_done, 1)
                            else:
                                wait(act, h2_ready, n - NB - 1)
                                nc.scalar.activation(yT[:, par, :], ZT[par][:, 0:T], ACT.Gelu,
                                                     scale=gam[:, r - 1:r], bias=bet[:, r - 1:r]
                                                     ).then_inc(act_done, 1)
                        if there(b, 1) and 0 < r:
                            wait(act, h_ready, n)
                            nc.scalar.activation(HT[:, bass.ds((b - 1) * T, T)], hT[:, par ^ 1, :], ACT.Copy
                                                 ).then_inc(ht_copied, 1)
                    in_order(act, step, 1)

            @block.vector
            def _(dve):
                v = nc.vector
                dve.wait_ge(w_in, 16 * len(loads))
                c = Chain(dve, deq)
                c(v.tensor_copy(wt[:, :, :], qw[:, :, :]))
                c(v.tensor_scalar(wt[:, :, :], wt[:, :, :], 1.0 / 7.5, -1.0, ALU.mult, ALU.add))
                c(v.tensor_tensor(wt[:, :, :], wt[:, :, :], scl[:, :, :], ALU.mult))
                dve.wait_ge(lora_ready, 1)
                v.tensor_tensor(wt[:, 0:4, :], wt[:, 0:4, :], ZT[0][:, :].rearrange("p (l o) -> p l o", l=4), ALU.add
                                ).then_inc(w_ready, 1)
                v.tensor_tensor(wt[:, 4:6, :], wt[:, 4:6, :], H2[0][:, 0:2 * P].rearrange("p (l o) -> p l o", l=2),
                                ALU.add).then_inc(w_ready, 1)
                halves_vector(dve, g, st, g.X, NT)
                for r in ROUNDS:
                    moments_vector(dve, g, st, 1e-5, (r + 1) * NT, r)

                    def step(b, par, r=r):
                        n = r * NB + b
                        if there(b, 0):
                            wait(dve, zT_ready, n - 1)
                            for t in range(TT):
                                tile = b * TT + t
                                src = (g.X if r == 0 else g.XP)[:, bass.ds(tile, 1), :]
                                ins = v.tensor_scalar(zs[:, par, t:t + 1, :], src, g.mean[:, bass.ds(tile, 1)],
                                                      g.rstd[:, bass.ds(tile, 1)], ALU.subtract, ALU.mult)
                            ins.then_inc(zs_ready, 1)
                        if there(b, 2) and r > 0:
                            wait(dve, h2_ready, n - NB - 1)
                            wait(dve, y1_ready, n - 3)
                            wait(dve, ht_copied, n - NB - 3)
                            if r == 1:
                                wait(dve, act_done, NB)
                            v.scalar_tensor_tensor(out=hT[:, par, :], in0=H2[par][:, 0:T],
                                                   scalar=b2[:, r - 1:r], in1=HT[:, bass.ds((b - 2) * T, T)],
                                                   op0=ALU.add, op1=ALU.add).then_inc(h_ready, 1)
                        if there(b, 3):
                            wait(dve, y1_ready, n - 2)
                            y = Y1[par ^ 1][:, 0:T].rearrange("p (t o) -> p t o", t=TT)
                            if r < NBLOCK:
                                dst = g.XP[:, bass.ds((b - 3) * TT, TT), :]
                                v.tensor_tensor(dst, y, b1[:, r:r + 1, :].broadcast_to([P, TT, P]), ALU.add
                                                ).then_inc(y1_used, 1)
                                wait(dve, y1_used, n - 2)
                                for t in range(TT):
                                    tile = (b - 3) * TT + t
                                    v.bn_stats(g.bn6[:, bass.ds(tile * 6, 6)], g.XP[:, bass.ds(tile, 1), :]
                                               ).then_inc(st.bn_done, 1)
                            else:
                                dst = g.X[:, bass.ds((b - 3) * TT, TT), :]
                                v.tensor_tensor(dst, dst, y, ALU.add).then_inc(y1_used, 1)
                    in_order(dve, step, 3, 4)
        clear = list(st.sems)
        clear_semaphores(nc, clear)


def store_stage(nc, g, out):
    with ExitStack() as ctx:
        st = Scope(nc, ctx, "store")
        x_out = st.sem("x_out")
        with nc.Block() as block:
            @block.sync
            def _(sp):
                ov = out.rearrange("(n p) d -> p n d", p=P)
                for k in range(4):
                    sp.dma_start(ov[:, k * 8:(k + 1) * 8, :], g.X[:, k * 8:(k + 1) * 8, :]).then_inc(x_out, 16)
                sp.wait_ge(x_out, 64)


class Globals:
    pass


def build_program(nc, a, out, stages):
    g = Globals()
    g.nc = nc
    g.score_scale = float(np.float32(1.0) / np.sqrt(np.float32(8.0)))
    with ExitStack() as ctx:
        def sb(name, shape, dt=F32):
            return ctx.enter_context(nc.sbuf_tensor(name, shape, dt))
        ntp = NT + 2 * PAD
        g.X = sb("X", [P, ntp, P])
        g.XP = sb("XP", [P, ntp, P])
        g.bn6, g.mean, g.gap, g.rstd = sb("bn6", [P, ntp * 6]), sb("mean", [P, ntp]), sb("gap", [P, ntp]), sb("rstd", [P, ntp])
        g.neghalf, g.half = sb("neghalf", [P, TT * 2 * H]), sb("half", [P, TT * 2 * H])
        g.ident, g.identb = sb("ident", [P, P]), sb("identb", [P, P], BF16)
        g.maskb = sb("maskb", [P, 2, P], BF16)
        g.scratch, g.scratch2 = a["scratch"], a["scratch2"]
        load_stage(nc, a["x"], g)
        of = lambda prefix: {k[4:]: v for k, v in a.items() if k.startswith(prefix)}
        for n, s in enumerate(stages):
            name = f"s{n}"
            if s == "L0a":
                hyperbolic_attention_stage(nc, g, of("l0a_"), name)
            if s == "L0b":
                attention_stage(nc, g, of("l0b_"), causal=True, name=name)
            if s == "F":
                attention_stage(nc, g, of("ffn_"), causal=False, rope=True, moe=True, name=name)
            if s == "L1a":
                wide_attention_stage(nc, g, of("l1a_"), name)
            if s == "MOE":
                moe_stage(nc, g, of("moe_"), name)
            if s == "L1b":
                attention_stage(nc, g, of("l1b_"), causal=True, bias=True, name=name)
            if s == "Q":
                qlora_stage(nc, g, of("qlo_"), name)
        store_stage(nc, g, out)


def pad_heads(wo):
    p = np.zeros((HC, 32, NC, P), np.float32)
    p[:, 0:8] = wo.reshape(NC, HC, 8, P).transpose(1, 2, 0, 3)
    return p.reshape(P, NC, P)


def rope_tables(scale):
    inv = (np.float32(1.0) / np.float32(10000.0) ** (np.arange(0, 8, 2, dtype=np.float32) / np.float32(8)))
    ang = np.arange(T, dtype=np.float32)[:, None] * inv.astype(np.float32)[None, :]
    cos, sin = np.cos(ang).T, np.sin(ang).T
    f = np.arange(P)
    c = cos[(f % 8) // 2]
    s = sin[(f % 8) // 2] * np.where(f % 2 == 0, -1, 1)[:, None]
    both = lambda m: np.stack([m * scale, m], axis=1).astype(np.float32)
    return both(c), both(s)


def half_rope():
    inv = np.float32(1.0) / np.float32(6000.0) ** (np.arange(0, 32, 2, dtype=np.float32) / np.float32(32))
    ang = (np.arange(T, dtype=np.float32)[:, None] * inv.astype(np.float32)[None, :]).T
    cos, sin = np.ones((64, T), np.float32), np.zeros((64, T), np.float32)
    cos[0:16], cos[16:32] = np.cos(ang), np.cos(ang)
    sin[0:16], sin[16:32] = -np.sin(ang), np.sin(ang)
    return np.tile(np.concatenate([cos, sin], axis=1), (2, 1)).astype(np.float32)


def rows(v):
    return np.ascontiguousarray(np.broadcast_to(v.reshape(1, -1), (P, v.size)))


def layouts(inp):
    a = {"x": inp["L0_attn_a_x"].reshape(NB * T, P)}
    one = lambda n: inp["L0_attn_a_" + n]
    a["l0a_wall"] = np.concatenate([one("Wqkv"), one("Walpha"), one("Wimp")], axis=0).T
    a["l0a_ball"] = rows(np.concatenate([one("bqkv"), one("balpha"), one("bimp")]))
    a["l0a_wo"], a["l0a_bo"] = one("Wout").T, rows(one("bout"))
    a["l0a_thr"], a["l0a_qk_scale"], a["l0a_log_k"] = (rows(one(n)) for n in ("spike_threshold", "qk_scale", "log_k"))
    w = inp["L0_attn_b_Wqkv"]
    a["l0b_wq"], a["l0b_wk"], a["l0b_wv"] = w[0:P].T, w[P:2 * P].T, w[2 * P:].T
    a["l0b_wo"] = inp["L0_attn_b_Wout"].T
    w, b = inp["L1_attn_b_Wqkv"].transpose(1, 0, 2), inp["L1_attn_b_bqkv"]
    for k, n in enumerate("qkv"):
        a["l1b_w" + n] = w[:, :, 8 * k:8 * k + 8].reshape(P, P)
        bb = b[:, 8 * k:8 * k + 8].reshape(P)
        a["l1b_b" + n] = rows(bb) if n == "v" else bb.reshape(P, 1)
    a["l1b_wo"] = inp["L1_attn_b_Wout"]
    a["l1b_bo"] = rows(inp["L1_attn_b_bout"])
    swap = np.arange(P) ^ 1
    a["ffn_wq"], a["ffn_wqs"] = inp["L0_ffn_Wq"], inp["L0_ffn_Wq"][:, swap]
    a["ffn_wkcT"], a["ffn_wvcT"] = inp["L0_ffn_Wk_c"].T, inp["L0_ffn_Wv_c"].T
    a["ffn_wk"], a["ffn_wks"], a["ffn_wv"] = inp["L0_ffn_Wk"], inp["L0_ffn_Wk"][:, swap], inp["L0_ffn_Wv"]
    a["ffn_wo"] = inp["L0_ffn_Wo"]
    a["ffn_cosT"], a["ffn_sinT"] = rope_tables(np.float32(1.0) / np.sqrt(np.float32(8.0)))
    w = inp["L1_attn_a_W_qkv"]
    half = np.arange(64)
    half[0:16], half[16:32] = np.arange(16, 32), np.arange(16)
    for n, m in (("wq", w[0]), ("wqs", w[0][:, half]), ("wk", w[1]), ("wks", w[1][:, half])):
        a["l1a_" + n] = m.reshape(NPAIR, P, P).transpose(2, 0, 1)
    a["l1a_wv"] = w[2].reshape(H * 64, P).T
    a["l1a_wo"] = inp["L1_attn_a_W_o"].T.reshape(NPAIR, P, P).transpose(1, 0, 2)
    turn = half_rope()
    a["l1a_turn_q"], a["l1a_turn_k"] = turn * np.float32(0.125), turn
    ins, w1 = inp["L0_ffn_W_shared_in"], inp["L0_ffn_W1_shared"]
    a["moe_wa"] = np.concatenate([ins[:, 0:256], w1[:, 0:256]], axis=1).reshape(P, 4, P)
    a["moe_wb"] = np.concatenate([ins[:, 256:], w1[:, 256:]], axis=1).reshape(P, 4, P)
    a["moe_wso"] = inp["L0_ffn_W_shared_out"].reshape(2, P, P).transpose(1, 0, 2)
    a["moe_w2"] = inp["L0_ffn_W2_experts"].reshape(8, 2, P, P).transpose(2, 1, 0, 3).reshape(P, 2, 8 * P)
    a["moe_wg"] = np.concatenate([inp["L0_ffn_Wg_gate"], inp["L0_ffn_We_gate"]], axis=1)
    a["moe_bg"] = rows(np.concatenate([inp["L0_ffn_group_bias"], inp["L0_ffn_expert_bias"]]))
    a["moe_n1"], a["moe_n2"] = rows(inp["L0_ffn_norm1_w"]), rows(inp["L0_ffn_norm2_w"])
    a["qlo_qw"] = inp["L1_ffn_qweights"].transpose(2, 0, 1)
    a["qlo_scl"] = np.repeat(inp["L1_ffn_scales"], P // inp["L1_ffn_scales"].shape[2], axis=2).transpose(2, 0, 1)
    a["qlo_la"] = inp["L1_ffn_lora_a"].transpose(1, 0, 2)
    a["qlo_lb"] = inp["L1_ffn_lora_b"].transpose(2, 0, 1)
    a["qlo_b1"] = rows(inp["L1_ffn_biases"][0::2].reshape(-1)).reshape(P, 3, P)
    a["qlo_b2"] = inp["L1_ffn_biases"][1::2].T
    a["qlo_gam"], a["qlo_bet"] = inp["L1_ffn_ln_gamma"].T, inp["L1_ffn_ln_beta"].T
    return {k: np.ascontiguousarray(v) for k, v in a.items()}


STAGES = ("L0a", "F", "MOE", "L0b", "F", "MOE", "L1a", "Q", "L1b", "Q")


def kernel(**inputs):
    from concourse import bacc
    from concourse.bass_utils import run_bass_kernel_spmd

    arrays = layouts({k: np.asarray(v) for k, v in inputs.items()})
    nc = bacc.Bacc("TRN2", target_bir_lowering=False, num_devices=1)
    a = {k: nc.dram_tensor(k, v.shape, mybir.dt.from_np(v.dtype), kind="ExternalInput").ap()
         for k, v in arrays.items()}
    a["scratch"] = nc.dram_tensor("scratch", (2, 3, P, 2 * T), BF16, kind="Internal").ap()
    a["scratch2"] = nc.dram_tensor("scratch2", (2, 2, 3, P, 2 * T), BF16, kind="Internal").ap()
    out = nc.dram_tensor("out", (NB * T, P), F32, kind="ExternalOutput").ap()
    build_program(nc, a, out, STAGES)
    r = run_bass_kernel_spmd(nc, [arrays], core_ids=[0])
    return r.results[0]["out"].reshape(NB, T, P)
```

```python
from contextlib import ExitStack

import numpy as np

import concourse.bass as bass
from concourse import mybir

F32 = mybir.dt.float32
BF16 = mybir.dt.bfloat16
I32 = mybir.dt.int32
ALU = mybir.AluOpType
ACT = mybir.ActivationFunctionType
AX = mybir.AxisListType.X

P = 128
NB, T = 16, 256
TT = T // P
NT = NB * TT
PAD = 2
H = 16
HC = 4
NC = H // HC
UN = TT * NC
NPAIR = H // 2
LAG_T, LAG_V = 3, 4
PRING, SRING, TRING = 4, 2, 2
QPART = (0, 0, 1, 0, 2, 1)
KPART = (0, 1, 0, 2, 0, 1)
NBLK = len(QPART)
MASKED = -3.0e38


class Engine:

    def __init__(self, eng):
        self.eng = eng

    def wait_ge(self, sem, value):
        if not (isinstance(value, int) and value <= 0):
            self.eng.wait_ge(sem, value)

    def to_reg(self, value):
        return self.eng.to_reg(value)

    def dma_start(self, out, in_):
        return self.eng.dma_start(out, in_)

    def Fori(self, first, end):
        return self.eng.Fori(first, end)


def over_sequences(eng, body, epilogue=None):
    body(0, 0)
    with eng.Fori(0, (NB - 2) // 2) as i:
        body(i * 2 + 1, 1)
        body(i * 2 + 2, 0)
    body(NB - 1, (NB - 1) % 2)
    if epilogue is not None:
        epilogue(NB, NB % 2)


def clear_retired(pool, g):
    if g.retired is not None:
        for s in g.retired.sems:
            pool.sem_clear(s)


def retire(g, st):
    if g.retired is not None:
        g.retired.sem_ctx.close()
    g.retired = st


class Scope:

    def __init__(self, nc, ctx, stage):
        self.nc, self.ctx, self.stage, self.sems, self.sem_ctx = nc, ctx, stage, [], ExitStack()

    def sb(self, name, shape, dt=F32):
        return self.ctx.enter_context(self.nc.sbuf_tensor(f"{self.stage}_{name}", shape, dt))

    def ps(self, name, shape, dt=F32):
        return self.ctx.enter_context(self.nc.psum_tensor(f"{self.stage}_{name}", shape, dt))

    def sem(self, name):
        s = self.sem_ctx.enter_context(self.nc.semaphore(f"{self.stage}_{name}"))
        self.sems.append(s)
        return s


class Chain:

    def __init__(self, eng, sem, start=0):
        self.eng, self.sem, self.n = eng, sem, start

    def __call__(self, ins):
        self.n = self.n + 1
        ins.then_inc(self.sem, 1)
        self.eng.wait_ge(self.sem, self.n)


def load_stage(nc, x, g):
    with ExitStack() as ctx:
        st = Scope(nc, ctx, "load")
        x_in, made = st.sem("x_in"), st.sem("constants_made")
        with nc.Block() as block:
            @block.sync
            def _(sp):
                sp = Engine(sp)
                xv = x.rearrange("(n p) d -> p n d", p=P)
                for k in range(4):
                    sp.dma_start(g.X[:, k * 8:(k + 1) * 8, :], xv[:, k * 8:(k + 1) * 8, :]).then_inc(x_in, 16)
                sp.wait_ge(x_in, 64)

            @block.gpsimd
            def _(pool):
                clear_retired(pool, g)
                c = Chain(pool, made)
                c(pool.memset(g.ident[:, :], 0.0))
                c(pool.affine_select(out=g.ident[:, :], in_=g.ident[:, :], compare_op=ALU.not_equal, fill=1.0,
                                     base=0, pattern=[[-1, P]], channel_multiplier=1))
                c(pool.tensor_copy(g.identb[:, :], g.ident[:, :]))
                c(pool.memset(g.maskb[:, :, :], 0.0))
                c(pool.affine_select(out=g.maskb[:, :, :], in_=g.maskb[:, :, :], compare_op=ALU.is_ge, fill=MASKED,
                                     base=0, pattern=[[0, 2], [-1, P]], channel_multiplier=1))
                c(pool.memset(g.neghalf[:, :], -0.5))
                c(pool.memset(g.X[:, NT:, :], 0.0))
                c(pool.memset(g.bn6[:, :], 0.0))
        retire(g, st)


def moments_sems(st):
    st.bn_done, st.moment_step = st.sem("bn_done"), st.sem("moment_step")
    st.var_ready, st.rstd_ready, st.mean_ready = st.sem("var_ready"), st.sem("rstd_ready"), st.sem("mean_ready")


ALL, FIRST, LATER = slice(0, NT + 2 * PAD), slice(0, 2 * TT), slice(2 * TT, NT + 2 * PAD)


def halves_vector(dve, g, st, src, tiles, at_once=8):
    def one(tile):
        g.nc.vector.bn_stats(g.bn6[:, bass.ds(tile * 6, 6)], src[:, bass.ds(tile, 1), :]).then_inc(st.bn_done, 1)

    n = tiles.stop - tiles.start
    if n <= at_once:
        for k in range(n):
            one(tiles.start + k)
        return
    with dve.Fori(0, n // at_once) as i:
        for k in range(at_once):
            one(i * at_once + (tiles.start + k))


def moments_vector(dve, g, st, eps, bn_count, turn=0, rms=False, tiles=ALL):
    nc = g.nc
    six = g.bn6[:, :].rearrange("p (n k) -> p n k", k=6)[:, tiles, :]
    mean, rstd, gap = g.mean[:, tiles], g.rstd[:, tiles], g.gap[:, tiles]
    mean_e, sq_e, mean_o, sq_o = six[:, :, 1], six[:, :, 2], six[:, :, 4], six[:, :, 5]
    dve.wait_ge(st.bn_done, bn_count)
    step = Chain(dve, st.moment_step, 5 * turn)
    nc.vector.tensor_tensor(mean, mean_e, mean_o, ALU.mult if rms else ALU.add).then_inc(st.moment_step, 1)
    nc.vector.tensor_tensor(rstd, sq_e, sq_o, ALU.add).then_inc(st.moment_step, 1)
    step.n = step.n + 2
    step(nc.vector.tensor_tensor(gap, mean_e, mean_o, ALU.subtract))
    nc.vector.tensor_scalar(rstd, rstd, 1.0 / P, eps, ALU.mult, ALU.add).then_inc(st.moment_step, 1)
    step.n = step.n + 1
    step(nc.vector.tensor_tensor(gap, gap, gap, ALU.mult))
    if rms:
        nc.vector.scalar_tensor_tensor(out=mean, in0=gap, scalar=0.5, in1=mean,
                                       op0=ALU.mult, op1=ALU.add).then_inc(st.mean_ready, 1)
        dve.wait_ge(st.mean_ready, turn + 1)
        nc.vector.tensor_tensor(rstd, rstd, mean, ALU.add).then_inc(st.var_ready, 1)
    else:
        nc.vector.tensor_scalar(mean, mean, 0.5, None, ALU.mult).then_inc(st.mean_ready, 1)
        nc.vector.scalar_tensor_tensor(out=rstd, in0=gap, scalar=0.25, in1=rstd,
                                       op0=ALU.mult, op1=ALU.add).then_inc(st.var_ready, 1)
        dve.wait_ge(st.mean_ready, turn + 1)


def moments_done(eng, st, turn=0):
    eng.wait_ge(st.mean_ready, turn + 1)
    eng.wait_ge(st.rstd_ready, turn + 1)


def moments_pool(pool, g, st, turn=0, tiles=ALL):
    pool.wait_ge(st.var_ready, turn + 1)
    g.nc.gpsimd.tensor_tensor(g.rstd[:, tiles], g.rstd[:, tiles], g.neghalf[:, 0:tiles.stop - tiles.start], ALU.pow
                              ).then_inc(st.rstd_ready, 1)


def load_weights(sp, sem, pairs):
    for dst, src in pairs:
        sp.dma_start(dst[tuple(slice(None) for _ in dst.shape)], src).then_inc(sem, 16)
    sp.wait_ge(sem, 16 * len(pairs))


def in_order(eng, body, lag, head=4):
    for b in range(head):
        body(b, b % 2)
    with eng.Fori(0, (NB - head) // 4) as i:
        for k in range(4):
            body(i * 4 + (head + k), k % 2)
    for k in range(lag):
        body(NB + k, k % 2)


def there(b, lag):
    return not isinstance(b, int) or 0 <= b - lag < NB


class Jobs:

    def __init__(self, order, first):
        self.order, self.first = order, first
        self.start = len(first) + sum(j[4] >= 0 for j in order)

    def number(self, b, i):
        if isinstance(b, int) and b == 0:
            return len(self.first) + sum(j[4] >= 0 for j in self.order[:i])
        if isinstance(b, int) and b == NB:
            return self.start + (NB - 1) * len(self.order) + sum(j[4] < 0 for j in self.order[:i])
        return b * len(self.order) + (self.start - len(self.order) + i)

    def at(self, b, slot, place):
        out = []
        for i, (s, p, kind, k, of) in enumerate(self.order):
            if (s, p) != (slot, place):
                continue
            if isinstance(b, int) and (b + of < 0 or (b == NB and of >= 0)):
                continue
            out.append((kind, k, b + of, of % 2, self.number(b, i)))
        return out

    def after(self, b, kind, k):
        i = [(j[2], j[3]) for j in self.order].index((kind, k))
        if isinstance(b, int) and (b < 0 or b + self.order[i][4] < 0):
            return 0
        return self.number(b, i) + 1


def before_first(order, nseq):
    return [(kind, k, j) for j in range(nseq) for kind, k in order]


def attention_stage(nc, g, w, *, causal, rope=False, bias=False, moe=False, name):
    LAG_T, LAG_V = 3, 4
    with ExitStack() as ctx:
        st = Scope(nc, ctx, name)
        sb, ps, sem = st.sb, st.ps, st.sem
        wq, wk, wv, wo = sb("wq", [P, P]), sb("wk", [P, P]), sb("wv", [P, P]), sb("wo", [P, P])
        if rope:
            wqs, wks = sb("wqs", [P, P]), sb("wks", [P, P])
            wkcT, wvcT = sb("wkcT", [32, P]), sb("wvcT", [32, P])
            wk2, wks2, wv2 = sb("wk2", [32, P]), sb("wks2", [32, P]), sb("wv2", [32, P])
            cosT, sinT = sb("cosT", [P, 2, T]), sb("sinT", [P, 2, T])
            roc, ros, qkf = sb("roc", [P, 2 * T]), sb("ros", [P, 2 * T]), sb("qkf", [P, 2 * T])
        if bias:
            bq, bk, bv = sb("bq", [P, 1]), sb("bk", [P, 1]), sb("bv", [P, P])
            bo = sb("bo", [P, P])
        xs, xc = sb("xs", [P, 2, TT, P]), sb("xc", [P, TT, P])
        xnT = sb("xnT", [P, 2, T])
        resid, zero = sb("resid", [P, 2 * T]), sb("zero", [P, 1])
        parts = sb("parts", [P, 2, 3, 2 * T], BF16)
        KROWS = NBLK * 16
        qst = [sb(f"qst{i}", [KROWS, NPAIR, T], BF16) for i in range(2)]
        kst = [sb(f"kst{i}", [KROWS, NPAIR, 2, T], BF16) for i in range(2)]
        vp = [sb(f"vp{i}", [P, TT, H, 32]) for i in range(2)]
        probs = sb("probs", [P, PRING, HC, T])
        probsT = sb("probsT", [P, TRING, TT, HC * P])
        negmax = sb("negmax", [P, PRING, HC])
        osb = sb("osb", [P, TT, NC, P])
        rinv, y, yT = sb("rinv", [P, H]), sb("y", [P, P]), sb("yT", [P, P])
        S = [ps(f"S{i}", [P, HC * T]) for i in range(SRING)]
        PT = [ps(f"PT{k}", [P, HC * P]) for k in range(TT)]
        O = ps("O", [P, NC, P])
        M = ps("M", [P, 512])
        moments_sems(st)
        w_in, zeroed = sem("weights_in"), sem("zeroed")
        wc_ready, wc_copied = sem("weights_multiplied"), sem("weights_copied")
        m_ready, m_read = sem("job_ready"), sem("job_read")
        centred, xs_ready, xp_ready = sem("centred"), sem("xs_ready"), sem("xp_ready")
        qk_summed, hi_ready, res_ready = sem("rotated_sum_ready"), sem("hi_ready"), sem("residue_ready")
        mid_ready, parts_ready = sem("middle_ready"), sem("parts_ready")
        parts_out, st_in = sem("parts_out"), [sem("stacks_in0"), sem("stacks_in1")]
        s_ready, max_ready, exp_done = sem("s_ready"), sem("max_ready"), sem("exp_done")
        t_ready, t_copied = sem("t_ready"), [sem("t_copied0"), sem("t_copied1")]
        pv_done, o_copied, rinv_ready, bo_added = sem("pv_done"), sem("o_copied"), sem("rinv_ready"), sem("bo_added")
        scr = g.scratch
        NIN = NBLK * 3

        front = [("x", 0), ("qk", 0)] + ([("swapped", 0)] if rope else [])
        if rope:
            order = [(0, 1, "u", 0, -1), (1, 1, "w", 0, -1), (2, 0, "x", 0, 2), (2, 2, "o", 0, -1), (3, 1, "qk", 0, 2),
                     (4, 0, "swapped", 0, 2), (4, 2, "u", 1, -1), (5, 2, "w", 1, -1), (6, 1, "v", 0, 1),
                     (7, 1, "o", 1, -1)]
        else:
            order = [(0, 1, "u", 0, -1), (1, 1, "w", 0, -1), (2, 0, "o", 0, -1), (2, 1, "x", 0, 2), (3, 1, "qk", 0, 2),
                     (4, 1, "u", 1, -1), (5, 1, "w", 1, -1), (6, 0, "v", 0, 1), (6, 2, "o", 1, -1)]
        jobs = Jobs(order, before_first(front, 2) + [("v", 0, 0)])

        def keys(u):
            return 1 if causal and u // NC == 0 else TT

        def split(b, u, lag):
            return (b, u - lag, 0) if u >= lag else (b - 1, u - lag + UN, 1)

        def exists(b, u, lag):
            return not (isinstance(b, int) and not 0 <= UN * b + u - lag < UN * NB)

        def tiles_before(b, u, kt=None):
            kts = range(TT) if kt is None else (kt,)
            count = lambda units: sum(k < keys(v) for v in units for k in kts)
            return b * count(range(UN)) + count(range(u))

        def s_view(u):
            n = keys(u) * P
            return S[u % SRING][:, 0:HC * n].rearrange("p (h k) -> p h k", h=HC)

        wloads = [(wq, w["wq"]), (wo, w["wo"])]
        if rope:
            wloads += [(wqs, w["wqs"]), (wkcT, w["wkcT"]), (wvcT, w["wvcT"]), (wk2, w["wk"]), (wks2, w["wks"]),
                       (wv2, w["wv"]), (cosT, w["cosT"]), (sinT, w["sinT"])]
        else:
            wloads += [(wk, w["wk"]), (wv, w["wv"])]
        if bias:
            wloads += [(bq, w["bq"]), (bk, w["bk"]), (bv, w["bv"]), (bo, w["bo"])]
        WIN = 16 * len(wloads)

        with nc.Block() as block:
            @block.sync
            def _(sp):
                sp = Engine(sp)
                load_weights(sp, w_in, wloads)
                sp.wait_ge(zeroed, 3)

                def counts(j, par):
                    v = (j + 1, (j - par) * (8 * NIN), j * UN - UN, j * 16 + 16)
                    return v if isinstance(j, int) else tuple(sp.to_reg(x) for x in v)

                def bounce(par, first, n):
                    split_n, read_n, used_n, out_n = n
                    sp.wait_ge(parts_ready, split_n)
                    sp.wait_ge(st_in[par], read_n)
                    sp.dma_start(scr[par].rearrange("a p n -> p a n"), parts[:, par, :, :]).then_inc(parts_out, 16)
                    if not first:
                        sp.wait_ge(s_ready, used_n)
                    sp.wait_ge(parts_out, out_n)
                    for i in range(NBLK):
                        r = 16 * i
                        sp.dma_start(qst[par][r:r + 16, :, :],
                                     scr[par, QPART[i], :, 0:T].rearrange("(c r) t -> r c t", r=16)
                                     ).then_inc(st_in[par], 16)
                        for hh in range(2):
                            src = scr[par, KPART[i], :, T:2 * T].rearrange("(c h d) t -> h d c t", h=2, d=8)
                            sp.dma_start(kst[par][r + 8 * hh:r + 8 * hh + 8, :, hh, :], src[hh]
                                         ).then_inc(st_in[par], 16)

                bounce(0, True, counts(0, 0))
                bounce(1, True, counts(1, 1))
                bounce(0, False, counts(2, 0))
                with sp.Fori(0, (NB - 2) // 2) as i:
                    odd, even = counts(i * 2 + 3, 1), counts(i * 2 + 4, 0)
                    bounce(1, False, odd)
                    bounce(0, False, even)
                bounce(1, False, counts(NB + 1, 1))
                sp.wait_ge(parts_out, 16 * (NB + PAD))
                for i in range(2):
                    sp.wait_ge(st_in[i], 16 * NIN * (NB + PAD) // 2)

            @block.gpsimd
            def _(pool):
                clear_retired(pool, g)
                pool = Engine(pool)
                tt = nc.gpsimd.tensor_tensor
                nc.gpsimd.memset(zero[:, :], 0.0).then_inc(zeroed, 1)
                moments_pool(pool, g, st, tiles=FIRST)
                moments_done(pool, st)

                def x_normalise(j, par):
                    tiles = bass.ds(j * TT, TT)
                    spread = lambda x: x[:, tiles].unsqueeze(2).broadcast_to([P, TT, P])
                    pool.wait_ge(xs_ready, j)
                    if moe:
                        pool.wait_ge(xp_ready, j)
                    tt(xc[:, :, :], g.X[:, tiles, :], spread(g.mean), ALU.subtract).then_inc(centred, 1)
                    pool.wait_ge(centred, j + 1)
                    tt(xs[:, par, :, :], xc[:, :, :], spread(g.rstd), ALU.mult).then_inc(xs_ready, 1)
                    if moe:
                        tt(g.XP[:, tiles, :], xc[:, :, :], spread(g.rstd), ALU.mult).then_inc(xp_ready, 1)

                def split_parts(j, par):
                    if rope:
                        pool.wait_ge(m_read, last_read(j))
                        pool.wait_ge(res_ready, j)
                        tt(qkf[:, :], roc[:, :], ros[:, :], ALU.add).then_inc(qk_summed, 1)
                        pool.wait_ge(hi_ready, j + 1)
                        pool.wait_ge(parts_ready, j)
                        tt(resid[:, :], qkf[:, :], parts[:, par, 0, :], ALU.subtract).then_inc(res_ready, 1)
                        pool.wait_ge(res_ready, j + 1)
                    else:
                        pool.wait_ge(m_read, last_read(j))
                    tt(parts[:, par, 1, :], resid[:, :], zero[:, 0:1].broadcast_to([P, 2 * T]), ALU.add
                       ).then_inc(mid_ready, 1)
                    pool.wait_ge(mid_ready, j + 1)
                    tt(parts[:, par, 2, :], resid[:, :], parts[:, par, 1, :], ALU.subtract).then_inc(parts_ready, 1)

                def last_read(j):
                    if isinstance(j, int) and j < 2:
                        return len(front) * (j + 1)
                    return jobs.after(j - 2, *front[-1])

                x_normalise(0, 0)
                x_normalise(1, 1)
                for i in range(2):
                    nc.gpsimd.memset(kst[i][:, :, :, :], 0.0).then_inc(zeroed, 1)
                for i in range(2):
                    c = Chain(pool, zeroed, 3 + 2 * i)
                    c(nc.gpsimd.memset(vp[i][:, :, :, :], 0.0))
                    c(nc.gpsimd.memset(vp[i][:, :, :, 8:9], 1.0))
                for j in range(2):
                    split_parts(j, j)
                moments_pool(pool, g, st, 1, LATER)
                moments_done(pool, st, 1)

                def body(b, par):
                    x_normalise(b + 2, par)
                    split_parts(b + 2, par)

                over_sequences(pool, body)

            @block.tensor
            def _(pe):
                pe = Engine(pe)
                pe.wait_ge(w_in, WIN)
                if rope:
                    for k, (a, c) in enumerate(((wkcT, wk2), (wkcT, wks2), (wvcT, wv2))):
                        ins = nc.tensor.matmul(M[:, k * P:(k + 1) * P], a[:, :], c[:, :], start=True, stop=True)
                    ins.then_inc(wc_ready, 1)
                pe.wait_ge(wc_copied, 1)

                def run(kind, k, j, par, n):
                    pe.wait_ge(m_read, n)
                    if kind == "x":
                        pe.wait_ge(xs_ready, j + 1)
                        for t in range(TT):
                            ins = nc.tensor.transpose(M[:, t * P:(t + 1) * P], xs[:, par, t, :], g.ident[:, :])
                    elif kind in ("qk", "swapped"):
                        a, c = (wq, wk) if kind == "qk" else (wqs, wks)
                        nc.tensor.matmul(M[:, 0:T], a[:, :], xnT[:, par, :], start=True, stop=True)
                        ins = nc.tensor.matmul(M[:, T:2 * T], c[:, :], xnT[:, par, :], start=True, stop=True)
                    elif kind == "v":
                        for t in range(TT):
                            ins = nc.tensor.matmul(M[:, t * P:(t + 1) * P], xnT[:, par, t * P:(t + 1) * P], wv[:, :],
                                                   start=True, stop=True)
                    elif kind == "u":
                        pe.wait_ge(o_copied, j * TT + k + 1)
                        for c in range(NC):
                            ins = nc.tensor.transpose(M[:, c * P:(c + 1) * P], osb[:, k, c, :], g.ident[:, :])
                    elif kind == "w":
                        ins = nc.tensor.transpose(M[:, 0:P], y[:, :], g.ident[:, :])
                    else:
                        ins = nc.tensor.matmul(M[:, 0:P], yT[:, :], wo[:, :], start=True, stop=True)
                    ins.then_inc(m_ready, 1)

                def transposes(b, u):
                    if not exists(b, u, LAG_T):
                        return
                    sq, v, _ = split(b, u, LAG_T)
                    pe.wait_ge(exp_done, sq * UN + v + 1)
                    for kt in range(keys(v)):
                        pe.wait_ge(t_copied[kt], tiles_before(sq, v, kt))
                        for h in range(HC):
                            ins = nc.tensor.transpose(PT[kt][:, h * P:(h + 1) * P],
                                                      probs[:, v % PRING, h, kt * P:(kt + 1) * P], g.ident[:, :])
                        ins.then_inc(t_ready, 1)

                def scores(b, u, par):
                    if not exists(b, u, 0):
                        return
                    if u == 0:
                        pe.wait_ge(st_in[par], (b - par) * (8 * NIN) + 16 * NIN)
                    pe.wait_ge(exp_done, UN * b + u - SRING + 1)
                    t, c, nk = u // NC, u % NC, keys(u) * P
                    out = s_view(u)
                    for i in range(HC // 2):
                        o2 = out[:, 2 * i:2 * i + 2, :]
                        ins = nc.tensor.matmul(o2, qst[par][:, 2 * c + i, t * P:(t + 1) * P],
                                               kst[par][:, 2 * c + i, :, 0:nk], start=True, stop=True)
                        if causal:
                            ins = nc.tensor.matmul(o2[:, :, t * P:(t + 1) * P], g.identb[:, :], g.maskb[:, :, :],
                                                   start=False, stop=True, skip_group_check=True)
                    ins.then_inc(s_ready, 1)

                def values(b, u, par):
                    if not exists(b, u, LAG_V):
                        return
                    sq, v, shift = split(b, u, LAG_V)
                    c, t, nk = v % NC, v // NC, keys(v)
                    if v == 0:
                        pe.wait_ge(m_read, values_read(sq))
                    if c == 0:
                        pe.wait_ge(o_copied, TT * sq + t)
                    for kt in range(nk):
                        pe.wait_ge(t_copied[kt], tiles_before(sq, v, kt) + 1)
                        for h in range(HC):
                            ins = nc.tensor.matmul(O[32 * h:32 * h + 32, c, :], vp[par ^ shift][:, kt, HC * c + h, :],
                                                   probsT[:, v % TRING, kt, h * P:(h + 1) * P],
                                                   start=kt == 0, stop=kt == nk - 1, tile_position=(0, 32 * h))
                    ins.then_inc(pv_done, 1)

                def values_read(sq):
                    return len(jobs.first) if isinstance(sq, int) and sq == 0 else jobs.after(sq - 1, "v", 0)

                for n, (kind, k, j) in enumerate(jobs.first):
                    run(kind, k, j, j, n)

                def body(b, par):
                    for u in range(UN):
                        for place, part in enumerate((lambda: scores(b, u, par), lambda: transposes(b, u),
                                                      lambda: values(b, u, par))):
                            part()
                            for kind, k, j, shift, n in jobs.at(b, u, place):
                                run(kind, k, j, par ^ shift, n)

                over_sequences(pe, body, body)

            @block.scalar
            def _(act):
                act = Engine(act)
                if rope:
                    act.wait_ge(wc_ready, 1)
                    for k, dst in enumerate((wk, wks, wv)):
                        ins = nc.scalar.activation(dst[:, :], M[:, k * P:(k + 1) * P], ACT.Copy)
                    ins.then_inc(wc_copied, 1)
                else:
                    act.wait_ge(w_in, WIN)
                    if bias:
                        nc.scalar.activation(bq[:, :], bq[:, :], ACT.Copy, scale=g.score_scale).then_inc(wc_ready, 1)
                    nc.scalar.activation(wq[:, :], wq[:, :], ACT.Copy, scale=g.score_scale).then_inc(wc_copied, 1)
                    if bias:
                        act.wait_ge(wc_ready, 1)

                def exponentials(b, u):
                    if not exists(b, u, 0):
                        return
                    n, r, v = UN * b + u, u % PRING, s_view(u)
                    act.wait_ge(max_ready, n + 1)
                    if exists(b, u, PRING):
                        sq, old, _ = split(b, u, PRING)
                        act.wait_ge(t_ready, tiles_before(sq, old) + keys(old))
                    for h in range(HC):
                        ins = nc.scalar.activation(probs[:, r, h, 0:keys(u) * P], v[:, h, :], ACT.Exp,
                                                   bias=negmax[:, r, h:h + 1])
                    ins.then_inc(exp_done, 1)

                def t_copy(b, u):
                    if not exists(b, u, LAG_T):
                        return
                    sq, v, _ = split(b, u, LAG_T)
                    if keys(v) > 1:
                        act.wait_ge(t_ready, tiles_before(sq, v) + 2)
                        act.wait_ge(pv_done, sq * UN + v - TRING + 1)
                        nc.scalar.activation(probsT[:, v % TRING, 1, :], PT[1][:, :], ACT.Copy
                                             ).then_inc(t_copied[1], 1)

                def read(kind, k, j, par, n):
                    if kind == "x":
                        act.wait_ge(m_ready, n + 1)
                        nc.scalar.activation(xnT[:, par, :], M[:, 0:T], ACT.Copy).then_inc(m_read, 1)
                    elif kind == "qk" and not rope:
                        act.wait_ge(m_ready, n + 1)
                        act.wait_ge(parts_out, (j - 1) * 16)
                        if bias:
                            for half, bb in enumerate((bq, bk)):
                                part = slice(half * T, (half + 1) * T)
                                ins = nc.scalar.activation(parts[:, par, 0, part], M[:, part], ACT.Identity,
                                                           bias=bb[:, 0:1])
                        else:
                            ins = nc.scalar.activation(parts[:, par, 0, :], M[:, :], ACT.Copy)
                        ins.then_inc(hi_ready, 1)
                    elif kind == "v" and not bias:
                        act.wait_ge(m_ready, n + 1)
                        if isinstance(j, int) and j < 2:
                            act.wait_ge(zeroed, 7)
                        act.wait_ge(pv_done, UN * (j - 1))
                        nc.scalar.activation(vp[par][:, :, :, 0:8],
                                             M[:, 0:T].rearrange("p (t h d) -> p t h d", t=TT, h=H), ACT.Copy
                                             ).then_inc(m_read, 1)
                    elif kind == "w":
                        act.wait_ge(m_ready, n + 1)
                        nc.scalar.activation(yT[:, :], M[:, 0:P], ACT.Copy).then_inc(m_read, 1)

                def high_part(j, par):
                    act.wait_ge(qk_summed, j + 1)
                    act.wait_ge(parts_out, (j - 1) * 16)
                    nc.scalar.activation(parts[:, par, 0, :], qkf[:, :], ACT.Copy).then_inc(hi_ready, 1)

                def o_copy(sq, t, before):
                    if isinstance(sq, int) and not 0 <= sq < NB:
                        return
                    act.wait_ge(pv_done, sq * UN + (t + 1) * NC)
                    act.wait_ge(m_ready, before)
                    nc.scalar.activation(osb[:, t, :, :], O[:, :, :], ACT.Copy).then_inc(o_copied, 1)

                for n, (kind, k, j) in enumerate(jobs.first):
                    read(kind, k, j, j, n)
                    if kind == "swapped":
                        high_part(j, j)

                def body(b, par):
                    for u in range(UN):
                        for place, part in enumerate((lambda: t_copy(b, u), lambda: None, lambda: exponentials(b, u))):
                            part()
                            for kind, k, j, shift, n in jobs.at(b, u, place):
                                read(kind, k, j, par ^ shift, n)
                        if u == 3:
                            o_copy(b - 1, 1, jobs.after(b - 1, "u", 1))
                        if u == 5 and rope and not (isinstance(b, int) and b == NB):
                            high_part(b + 2, par)
                        if u == 7:
                            o_copy(b, 0, jobs.after(b, "u", 0))

                over_sequences(act, body, body)

            @block.vector
            def _(dve):
                dve = Engine(dve)
                v_ = nc.vector
                halves_vector(dve, g, st, g.X, FIRST)
                moments_vector(dve, g, st, 1e-5, 2 * TT, tiles=FIRST)
                dve.wait_ge(w_in, WIN)
                if bias:
                    dve.wait_ge(wc_ready, 1)

                def read(kind, k, j, par, n):
                    if kind == "qk" and rope:
                        dve.wait_ge(m_ready, n + 1)
                        dve.wait_ge(qk_summed, j)
                        v_.tensor_tensor(roc[:, :], M[:, :], cosT[:, :, :].rearrange("p a t -> p (a t)"), ALU.mult
                                         ).then_inc(m_read, 1)
                    elif kind == "swapped":
                        dve.wait_ge(m_ready, n + 1)
                        v_.tensor_tensor(ros[:, :], M[:, :], sinT[:, :, :].rearrange("p a t -> p (a t)"), ALU.mult
                                         ).then_inc(m_read, 1)
                    elif kind == "qk":
                        dve.wait_ge(hi_ready, j + 1)
                        dve.wait_ge(parts_ready, j)
                        if bias:
                            for half, bb in enumerate((bq, bk)):
                                part = slice(half * T, (half + 1) * T)
                                ins = v_.scalar_tensor_tensor(out=resid[:, part], in0=M[:, part], scalar=bb[:, 0:1],
                                                              in1=parts[:, par, 0, part], op0=ALU.add,
                                                              op1=ALU.subtract)
                        else:
                            ins = v_.tensor_tensor(resid[:, :], M[:, :], parts[:, par, 0, :], ALU.subtract)
                        ins.then_inc(m_read, 1)
                    elif kind == "v" and bias:
                        dve.wait_ge(m_ready, n + 1)
                        if isinstance(j, int) and j < 2:
                            dve.wait_ge(zeroed, 7)
                        dve.wait_ge(pv_done, UN * (j - 1))
                        bvb = bv[:, :].rearrange("p (h d) -> p h d", h=H)
                        for t in range(TT):
                            ins = v_.tensor_tensor(vp[par][:, t, :, 0:8],
                                                   M[:, t * P:(t + 1) * P].rearrange("p (h d) -> p h d", h=H),
                                                   bvb, ALU.add)
                        ins.then_inc(m_read, 1)
                    elif kind == "u":
                        dve.wait_ge(m_ready, n + 1)
                        heads = M[:, :].rearrange("p (h d) -> p h d", d=32)
                        v_.reciprocal(rinv[:, :], heads[:, :, 8]).then_inc(rinv_ready, 1)
                        dve.wait_ge(rinv_ready, j * TT + k + 1)
                        v_.tensor_tensor(y[:, :].rearrange("p (h d) -> p h d", d=8), heads[:, :, 0:8],
                                         rinv[:, :].unsqueeze(2).broadcast_to([P, H, 8]), ALU.mult
                                         ).then_inc(m_read, 1)
                    elif kind == "o":
                        dve.wait_ge(m_ready, n + 1)
                        dst = (g.XP if moe else g.X)[:, bass.ds(j * TT + k, 1), :]
                        if moe:
                            dve.wait_ge(xp_ready, j + 1)
                        if bias:
                            v_.tensor_tensor(dst, dst, bo[:, :].unsqueeze(1), ALU.add).then_inc(bo_added, 1)
                            dve.wait_ge(bo_added, j * TT + k + 1)
                        v_.tensor_tensor(dst, dst, M[:, 0:P].unsqueeze(1), ALU.add).then_inc(m_read, 1)

                def maxima(b, u):
                    if not exists(b, u, 0):
                        return
                    n = UN * b + u
                    dve.wait_ge(s_ready, n + 1)
                    dve.wait_ge(exp_done, n - PRING + 1)
                    v_.tensor_reduce(out=negmax[:, u % PRING, :], in_=s_view(u), axis=AX, op=ALU.max,
                                     negate=True).then_inc(max_ready, 1)

                def t_copy(b, u):
                    if not exists(b, u, LAG_T):
                        return
                    sq, v, _ = split(b, u, LAG_T)
                    dve.wait_ge(t_ready, tiles_before(sq, v) + 1)
                    dve.wait_ge(pv_done, sq * UN + v - TRING + 1)
                    v_.tensor_copy(probsT[:, v % TRING, 0, :], PT[0][:, :]).then_inc(t_copied[0], 1)

                for n, (kind, k, j) in enumerate(jobs.first):
                    read(kind, k, j, j, n)

                halves_vector(dve, g, st, g.X, LATER)
                moments_vector(dve, g, st, 1e-5, NT + 2 * PAD, 1, tiles=LATER)

                def body(b, par):
                    for u in range(UN):
                        for place, part in enumerate((lambda: maxima(b, u), lambda: t_copy(b, u), lambda: None)):
                            part()
                            for kind, k, j, shift, n in jobs.at(b, u, place):
                                read(kind, k, j, par ^ shift, n)

                over_sequences(dve, body, body)
        retire(g, st)


def wide_attention_stage(nc, g, w, name):
    DH, LAG_T, LAG_V = 64, 3, 4
    with ExitStack() as ctx:
        st = Scope(nc, ctx, name)
        sb, ps, sem = st.sb, st.ps, st.sem
        wq, wk = sb("wq", [P, NPAIR, P]), sb("wk", [P, NPAIR, P])
        wqs, wks = sb("wqs", [P, NPAIR // 2, P]), sb("wks", [P, NPAIR // 2, P])
        wv, wo = sb("wv", [P, H * DH]), sb("wo", [P, NPAIR, P])
        turn = {n: sb(f"turn_{n}", [P, 2 * T]) for n in "abcd"}
        xs, xnT = sb("xs", [P, 2, TT, P]), sb("xnT", [P, T])
        NTMP = 2
        tmp = {n: sb(f"tmp_{n}", [P, NTMP, 2 * T]) for n in "abcd"}
        qw = [sb(f"qw{i}", [P, NPAIR, T]) for i in range(2)]
        kw = [sb(f"kw{i}", [P, NPAIR, 2, T]) for i in range(2)]
        vw = [sb(f"vw{i}", [P, TT, H, DH]) for i in range(2)]
        probs, probsT = sb("probs", [P, PRING, HC, T]), sb("probsT", [P, TRING, TT, HC * P])
        negmax, rowsum, rinv = sb("negmax", [P, PRING, HC]), sb("rowsum", [P, PRING, HC]), sb("rinv", [P, PRING, HC])
        osb, yT = sb("osb", [P, NPAIR, T]), sb("yT", [P, T])
        S = [ps(f"S{i}", [P, HC * T]) for i in range(SRING)]
        PT, O, banks = ps("PT", [P, HC * P]), ps("O", [P, 4, P]), [ps(f"M{i}", [P, 512]) for i in range(2)]
        moments_sems(st)
        w_in, kw_zeroed = sem("weights_in"), sem("kw_zeroed")
        xs_ready, m_ready, qk_ready = sem("xs_ready"), sem("job_ready"), sem("qk_ready")
        m_read = [sem("even_job_read"), sem("odd_job_read")]
        s_ready, max_ready, exp_done = sem("s_ready"), sem("max_ready"), sem("exp_done")
        rinv_ready, norm_done, t_ready = sem("rinv_ready"), sem("norm_done"), sem("t_ready")
        t_copied, pv_done, o_copied = [sem("t_copied0"), sem("t_copied1")], sem("pv_done"), sem("o_copied")

        FRONT = [("x", 0), ("x", 1)] + [(n, pp) for pp in range(NPAIR // 2) for n in "abc"] + [("v", i) for i in range(4)]
        todo = [(kind, k, 1) for kind, k in FRONT]
        todo[11:11] = [("o", 0, -1)]
        todo[15:15] = [("r", 0, -1)]
        PLACES = 3
        places = [(u, p) for u, n in enumerate((2, 3, 3, 3, 3, 2, 2, 2)) for p in range(n)]
        jobs = Jobs([(*at, *job) for at, job in zip(places, todo)], before_first(FRONT, 1))
        assert jobs.start % 2 == 0 and len(todo) % 2 == 0

        def numbered(b, u, place):
            out = []
            for kind, k, j, shift, n in jobs.at(b, u, place):
                i = [(x[2], x[3]) for x in jobs.order].index((kind, k))
                if isinstance(n, int):
                    out.append((kind, k, j, shift, n, n % 2, n // 2))
                else:
                    const = jobs.start - len(jobs.order) + i
                    out.append((kind, k, j, shift, n, const % 2, b * (len(jobs.order) // 2) + const // 2))
            return out

        NADD = 3 * NPAIR

        def adds(kind, pp):
            return 6 * pp + "abc".index(kind)

        def keys(u):
            return 1 if u // NC == 0 else TT

        def split(b, u, lag):
            return (b, u - lag, 0) if u >= lag else (b - 1, u - lag + UN, 1)

        def exists(b, u, lag):
            return not (isinstance(b, int) and not 0 <= UN * b + u - lag < UN * NB)

        def tiles_before(b, u, kt=None):
            kts = range(TT) if kt is None else (kt,)
            count = lambda units: sum(k < keys(v) for v in units for k in kts)
            return b * count(range(UN)) + count(range(u))

        def s_view(u):
            n = keys(u) * P
            return S[u % SRING][:, 0:HC * n].rearrange("p (h k) -> p h k", h=HC)

        loads = [(wq, w["wq"]), (wqs, w["wqs"]), (wk, w["wk"]), (wks, w["wks"]), (wv, w["wv"]), (wo, w["wo"])] + [
            (turn[n], w["turn_" + n]) for n in "abcd"]

        with nc.Block() as block:
            @block.sync
            def _(sp):
                sp = Engine(sp)
                load_weights(sp, w_in, loads)

            @block.gpsimd
            def _(pool):
                clear_retired(pool, g)
                pool = Engine(pool)
                for i in range(2):
                    nc.gpsimd.memset(kw[i][:, :, :, :], 0.0).then_inc(kw_zeroed, 1)
                moments_pool(pool, g, st, tiles=FIRST)
                pool.wait_ge(kw_zeroed, 2)

                def add_turned(j, par, kind, pp, bank, before, normalised):
                    n = pp % NTMP
                    low, high = slice(0, T), slice(T, 2 * T)
                    pool.wait_ge(m_read[bank], before + 1)
                    pool.wait_ge(s_ready, UN * (j - 1))
                    done = adds(kind, pp)
                    if kind == "a":
                        pool.wait_ge(qk_ready, j * NADD + done)
                        nc.gpsimd.tensor_tensor(qw[par][:, 2 * pp, :], tmp["a"][:, n, low], tmp["a"][:, n, high],
                                                ALU.add).then_inc(qk_ready, 1)
                    elif kind == "b":
                        pool.wait_ge(qk_ready, j * NADD + done)
                        nc.gpsimd.tensor_tensor(qw[par][:, 2 * pp + 1, :], tmp["b"][:, n, low], tmp["d"][:, n, low],
                                                ALU.add).then_inc(qk_ready, 1)
                    else:
                        pool.wait_ge(norm_done, normalised)
                        for i, (cos, sin) in enumerate(((tmp["c"][:, n, low], tmp["b"][:, n, high]),
                                                        (tmp["c"][:, n, high], tmp["d"][:, n, high]))):
                            for hh in range(2):
                                pool.wait_ge(qk_ready, j * NADD + (done + 2 * i + hh))
                                r = slice(DH * hh, DH * hh + DH)
                                nc.gpsimd.tensor_tensor(kw[par][r, 2 * pp + i, hh, :], cos[r, :], sin[r, :], ALU.add
                                                        ).then_inc(qk_ready, 1)

                def normalise(b, u):
                    if not exists(b, u, 1):
                        return
                    sq, v, _ = split(b, u, 1)
                    r, nk = v % PRING, keys(v) * P
                    if exists(b, u, 0):
                        added = sum({"a": 1, "b": 1, "c": 4}.get(x[2], 0) for x in jobs.order if x[0] < u)
                        pool.wait_ge(qk_ready, (b + 1) * NADD + added)
                    else:
                        pool.wait_ge(qk_ready, (b + 1) * NADD)
                    pool.wait_ge(rinv_ready, sq * UN + v + 1)
                    pr = probs[:, r, :, 0:nk]
                    nc.gpsimd.tensor_tensor(pr, pr, rinv[:, r, :].unsqueeze(2).broadcast_to([P, HC, nk]),
                                            ALU.mult).then_inc(norm_done, 1)

                for n, (kind, k, j) in enumerate(jobs.first):
                    if kind in "abc":
                        add_turned(0, 0, kind, k, n % 2, n // 2, 0)
                pool.wait_ge(qk_ready, NADD)
                moments_pool(pool, g, st, 1, LATER)

                def body(b, par):
                    for u in range(UN):
                        normalise(b, u)
                        for place in range(PLACES):
                            for kind, k, j, shift, n, bank, before in numbered(b, u, place):
                                if kind in "abc":
                                    add_turned(j, par ^ shift, kind, k, bank, before, b * UN + u)

                over_sequences(pool, body, body)

            @block.tensor
            def _(pe):
                pe = Engine(pe)
                pe.wait_ge(w_in, 16 * len(loads))

                def run(kind, k, j, par, n, bank, before):
                    M = banks[bank]
                    pe.wait_ge(m_read[bank], before)
                    if (kind, k) in (("a", 0), ("r", 0)):
                        pe.wait_ge(m_read[bank ^ 1], before + 1 if bank else before)
                    if kind == "x":
                        pe.wait_ge(xs_ready, j + 1)
                        ins = nc.tensor.transpose(M[:, 0:P], xs[:, par, k, :], g.ident[:, :])
                    elif kind in "abc":
                        low, high = {"a": (wq[:, 2 * k, :], wqs[:, k, :]), "b": (wq[:, 2 * k + 1, :], wks[:, k, :]),
                                     "c": (wk[:, 2 * k, :], wk[:, 2 * k + 1, :])}[kind]
                        nc.tensor.matmul(M[:, 0:T], low, xnT[:, :], start=True, stop=True)
                        ins = nc.tensor.matmul(M[:, T:2 * T], high, xnT[:, :], start=True, stop=True)
                    elif kind == "v":
                        t, half = k // 2, k % 2
                        ins = nc.tensor.matmul(M[:, :], xnT[:, t * P:(t + 1) * P], wv[:, half * 512:(half + 1) * 512],
                                               start=True, stop=True)
                    elif kind == "o":
                        pe.wait_ge(o_copied, j * 4 + 4)
                        for p in range(NPAIR):
                            ins = nc.tensor.matmul(M[:, 0:T], wo[:, p, :], osb[:, p, :], start=p == 0,
                                                   stop=p == NPAIR - 1)
                    else:
                        for t in range(TT):
                            ins = nc.tensor.transpose(M[:, t * P:(t + 1) * P], yT[:, t * P:(t + 1) * P],
                                                      g.ident[:, :])
                    ins.then_inc(m_ready, 1)

                def transposes(b, u, kt):
                    if not exists(b, u, LAG_T):
                        return
                    sq, v, _ = split(b, u, LAG_T)
                    if kt >= keys(v):
                        return
                    if kt == 0:
                        pe.wait_ge(norm_done, sq * UN + v + 1)
                    pe.wait_ge(t_copied[0], tiles_before(sq, v, 0) + kt)
                    pe.wait_ge(t_copied[1], tiles_before(sq, v, 1))
                    for h in range(HC):
                        ins = nc.tensor.transpose(PT[:, h * P:(h + 1) * P],
                                                  probs[:, v % PRING, h, kt * P:(kt + 1) * P], g.ident[:, :])
                    ins.then_inc(t_ready, 1)

                def scores(b, u, par):
                    if not exists(b, u, 0):
                        return
                    if u == 0:
                        pe.wait_ge(qk_ready, (b + 1) * NADD)
                    pe.wait_ge(exp_done, UN * b + u - SRING + 1)
                    t, c, nk = u // NC, u % NC, keys(u) * P
                    out = s_view(u)
                    for i in range(HC // 2):
                        o2 = out[:, 2 * i:2 * i + 2, :]
                        nc.tensor.matmul(o2, qw[par][:, 2 * c + i, t * P:(t + 1) * P], kw[par][:, 2 * c + i, :, 0:nk],
                                         start=True, stop=True)
                        ins = nc.tensor.matmul(o2[:, :, t * P:(t + 1) * P], g.identb[:, :], g.maskb[:, :, :],
                                               start=False, stop=True, skip_group_check=True)
                    ins.then_inc(s_ready, 1)

                def values(b, u, par):
                    if not exists(b, u, LAG_V):
                        return
                    sq, v, shift = split(b, u, LAG_V)
                    n, c = sq * UN + v, v % NC
                    for kt in range(keys(v)):
                        pe.wait_ge(t_copied[kt], tiles_before(sq, v, kt) + 1)
                    if v == 0:
                        half = len(jobs.first) // 2
                        for bank in range(2):
                            pe.wait_ge(m_read[bank], half if isinstance(sq, int) and sq == 0 else
                                 (jobs.start // 2 - len(jobs.order) // 2) + sq * (len(jobs.order) // 2))
                    if c % 2 == 0:
                        pe.wait_ge(o_copied, sq * 4 + v // 2)
                    vv, nk = vw[par ^ shift], keys(v)
                    for i in range(2):
                        for kt in range(nk):
                            for hh in range(2):
                                h = 2 * i + hh
                                ins = nc.tensor.matmul(O[DH * hh:DH * hh + DH, 2 * (c % 2) + i, :],
                                                       vv[:, kt, HC * c + h, :],
                                                       probsT[:, v % TRING, kt, h * P:(h + 1) * P],
                                                       start=kt == 0, stop=kt == nk - 1, tile_position=(0, DH * hh))
                    ins.then_inc(pv_done, 1)

                for n, (kind, k, j) in enumerate(jobs.first):
                    run(kind, k, j, j, n, n % 2, n // 2)

                def body(b, par):
                    for u in range(UN):
                        for place, part in enumerate((
                                lambda: transposes(b, u, 0), lambda: scores(b, u, par), lambda: transposes(b, u, 1))):
                            part()
                            for kind, k, j, shift, n, bank, before in numbered(b, u, place):
                                run(kind, k, j, par ^ shift, n, bank, before)
                        values(b, u, par)

                over_sequences(pe, body, body)

            @block.scalar
            def _(act):
                act = Engine(act)
                def exponentials(b, u):
                    if not exists(b, u, 0):
                        return
                    n, r, v = UN * b + u, u % PRING, s_view(u)
                    act.wait_ge(max_ready, n + 1)
                    if exists(b, u, PRING):
                        sq, old, _ = split(b, u, PRING)
                        act.wait_ge(t_ready, tiles_before(sq, old) + keys(old))
                    for h in range(HC):
                        ins = nc.scalar.activation(probs[:, r, h, 0:keys(u) * P], v[:, h, :], ACT.Exp,
                                                   bias=negmax[:, r, h:h + 1], accum_out=rowsum[:, r, h:h + 1])
                    ins.then_inc(exp_done, 1)

                def t_copy(b, u):
                    if not exists(b, u, LAG_T):
                        return
                    sq, v, _ = split(b, u, LAG_T)
                    if keys(v) > 1:
                        act.wait_ge(t_ready, tiles_before(sq, v) + 2)
                        act.wait_ge(pv_done, sq * UN + v - TRING + 1)
                        nc.scalar.activation(probsT[:, v % TRING, 1, :], PT[:, :], ACT.Copy).then_inc(t_copied[1], 1)

                def read(kind, k, j, par, n, bank):
                    M = banks[bank]
                    if kind == "x":
                        act.wait_ge(m_ready, n + 1)
                        nc.scalar.activation(xnT[:, k * P:(k + 1) * P], M[:, 0:P], ACT.Copy
                                             ).then_inc(m_read[bank], 1)
                    elif kind == "v":
                        act.wait_ge(m_ready, n + 1)
                        act.wait_ge(pv_done, UN * (j - 1))
                        t, half = k // 2, k % 2
                        nc.scalar.activation(vw[par][:, t, half * 8:(half + 1) * 8, :],
                                             M[:, :].rearrange("p (h d) -> p h d", h=8), ACT.Copy
                                             ).then_inc(m_read[bank], 1)
                    elif kind == "o":
                        act.wait_ge(m_ready, n + 1)
                        nc.scalar.activation(yT[:, :], M[:, 0:T], ACT.Copy).then_inc(m_read[bank], 1)

                def o_copy(sq, group):
                    if isinstance(sq, int) and not 0 <= sq < NB:
                        return
                    t, c2 = group // 2, group % 2
                    act.wait_ge(pv_done, sq * UN + 2 * group + 2)
                    act.wait_ge(m_ready, jobs.after(sq, "o", 0))
                    nc.scalar.activation(osb[:, 4 * c2:4 * c2 + 4, t * P:(t + 1) * P], O[:, :, :], ACT.Copy
                                         ).then_inc(o_copied, 1)

                for n, (kind, k, j) in enumerate(jobs.first):
                    read(kind, k, j, j, n, n % 2)

                def body(b, par):
                    for u in range(UN):
                        for place, part in enumerate((lambda: None, lambda: [], lambda: [t_copy(b, u), exponentials(b, u)])):
                            part()
                            for kind, k, j, shift, n, bank, before in numbered(b, u, place):
                                read(kind, k, j, par ^ shift, n, bank)
                        if u in (1, 3):
                            o_copy(b - 1, 2 + u // 2)
                        if u in (5, 7):
                            o_copy(b, (u - 5) // 2)

                over_sequences(act, body, body)

            @block.vector
            def _(dve):
                dve = Engine(dve)
                halves_vector(dve, g, st, g.X, FIRST)
                moments_vector(dve, g, st, 1e-5, 2 * TT, tiles=FIRST)
                dve.wait_ge(w_in, 16 * len(loads))

                def x_normalise(j, par):
                    if not (isinstance(j, int) and j < 2):
                        dve.wait_ge(m_ready, 2 if isinstance(j, int) and j == 2 else jobs.after(j - 3, "x", 1))
                    for t in range(TT):
                        tile = j * TT + t
                        ins = nc.vector.tensor_scalar(xs[:, par, t:t + 1, :], g.X[:, bass.ds(tile, 1), :],
                                                      g.mean[:, bass.ds(tile, 1)], g.rstd[:, bass.ds(tile, 1)],
                                                      ALU.subtract, ALU.mult)
                    ins.then_inc(xs_ready, 1)

                def read(kind, k, j, n, bank):
                    M = banks[bank]
                    if kind in "abc":
                        dve.wait_ge(m_ready, n + 1)
                        dve.wait_ge(qk_ready, j * NADD + 6 * (k - NTMP + 1))
                        n2, high = k % NTMP, slice(T, 2 * T)
                        ins = nc.vector.tensor_tensor(tmp[kind][:, n2, :], M[:, :], turn[kind][:, :], ALU.mult)
                        if kind in "ab":
                            part = slice(0, T) if kind == "a" else high
                            ins = nc.vector.tensor_tensor(tmp["d"][:, n2, part], M[:, high], turn["d"][:, part],
                                                          ALU.mult)
                        ins.then_inc(m_read[bank], 1)
                    elif kind == "r":
                        dve.wait_ge(m_ready, n + 1)
                        dst = g.X[:, bass.ds(j * TT, TT), :]
                        nc.vector.tensor_tensor(dst, dst, M[:, 0:T].rearrange("p (t o) -> p t o", t=TT), ALU.add
                                                ).then_inc(m_read[bank], 1)

                def maxima(b, u):
                    if not exists(b, u, 0):
                        return
                    n = UN * b + u
                    dve.wait_ge(s_ready, n + 1)
                    dve.wait_ge(exp_done, n - PRING + 1)
                    nc.vector.tensor_reduce(out=negmax[:, u % PRING, :], in_=s_view(u), axis=AX, op=ALU.max,
                                            negate=True).then_inc(max_ready, 1)

                def reciprocals(b, u):
                    if not exists(b, u, 1):
                        return
                    sq, v, _ = split(b, u, 1)
                    n, r = sq * UN + v, v % PRING
                    dve.wait_ge(exp_done, n + 1)
                    dve.wait_ge(norm_done, n - PRING + 1)
                    nc.vector.reciprocal(rinv[:, r, :], rowsum[:, r, :]).then_inc(rinv_ready, 1)

                def t_copy(b, u):
                    if not exists(b, u, LAG_T):
                        return
                    sq, v, _ = split(b, u, LAG_T)
                    dve.wait_ge(t_ready, tiles_before(sq, v) + 1)
                    dve.wait_ge(pv_done, sq * UN + v - TRING + 1)
                    nc.vector.tensor_copy(probsT[:, v % TRING, 0, :], PT[:, :]).then_inc(t_copied[0], 1)

                moments_done(dve, st)
                for j in range(2):
                    x_normalise(j, j)
                for n, (kind, k, j) in enumerate(jobs.first):
                    read(kind, k, 0, n, n % 2)

                halves_vector(dve, g, st, g.X, LATER)
                moments_vector(dve, g, st, 1e-5, NT + 2 * PAD, 1, tiles=LATER)

                def body(b, par):
                    for u in range(UN):
                        for place, part in enumerate((lambda: t_copy(b, u), lambda: maxima(b, u),
                                                      lambda: reciprocals(b, u))):
                            part()
                            for kind, k, j, shift, n, bank, before in numbered(b, u, place):
                                read(kind, k, j, n, bank)
                        if u == 6 and isinstance(b, int) and b == 0:
                            moments_done(dve, st, 1)
                        if u == 6 and exists(b, u, 0):
                            x_normalise(b + 2, par)

                over_sequences(dve, body, body)
        retire(g, st)


def hyperbolic_attention_stage(nc, g, w, name):
    LAG_D, LAG_E, LAG_T, LAG_V = 2, 3, 5, 6
    NCOL = 3 * P + H + 1
    with ExitStack() as ctx:
        st = Scope(nc, ctx, name)
        sb, ps, sem = st.sb, st.ps, st.sem
        wall, ball, wo, bo = sb("wall", [P, NCOL]), sb("ball", [P, NCOL]), sb("wo", [P, P]), sb("bo", [P, P])
        thr, safe, curv = sb("thr", [P, 1]), sb("safe", [P, 1]), sb("curv", [P, H])
        soft, one = sb("soft", [P, H]), sb("one", [P, 1])
        xs, xc, xnT = sb("xs", [P, 2, TT, P]), sb("xc", [P, TT, P]), sb("xnT", [P, T])
        F = [sb(f"F{i}", [P, TT, NCOL]) for i in range(2)]
        sg, oma, sal = sb("sg", [P, TT, H + 1]), sb("oma", [P, TT, H]), sb("sal", [P, TT, H])
        SA, SPK = sb("SA", [P, NT + 2 * PAD, H]), sb("SPK", [P, NT + 2 * PAD])
        sq, ops = sb("sq", [P, TT, 2 * P]), sb("ops", [P, TT, 3, P])
        n2, rn, rn2, z, gz = (sb(n, [P, TT, 2 * H]) for n in ("n2", "rn", "rn2", "z", "gz"))
        squares, roots, work = ([sb(f"{n}{i}", [P, TT, width]) for i, width in enumerate((3 * H, 2 * H))]
                                for n in ("squares", "roots", "root_work"))
        zero, spare, resid, parts = sb("zero", [P, 1]), sb("spare", [P, 1]), sb("resid", [P, 2, 2 * T]), sb("parts", [P, 2, 2, 3, 2 * T], BF16)
        KROWS = NBLK * 16
        qst = [[sb(f"qst{i}{k}", [KROWS, NPAIR, T], BF16) for k in range(2)] for i in range(2)]
        kst = [[sb(f"kst{i}{k}", [KROWS, NPAIR, 2, T], BF16) for k in range(2)] for i in range(2)]
        vp = [sb(f"vp{i}", [P, TT, H, 32]) for i in range(2)]
        DRING, WRING = 2, 4
        dd, ww = sb("dd", [P, DRING, HC * T]), sb("ww", [P, WRING, HC * T])
        probs, probsT = sb("probs", [P, PRING, HC, T]), sb("probsT", [P, TRING, TT, HC * P])
        top, negtop = sb("top", [P, PRING, HC]), sb("negtop", [P, PRING, HC])
        rec, rinv, y, yT = sb("rec", [P, H]), sb("rinv", [P, H]), sb("y", [P, P]), sb("yT", [P, P])
        osb = sb("osb", [P, TT, NC, P])
        SE, SI = ps("SE", [P, HC * T]), ps("SI", [P, HC * T])
        PT, O, M = [ps(f"PT{k}", [P, HC * P]) for k in range(TT)], ps("O", [P, NC, P]), ps("M", [P, 512])
        moments_sems(st)
        w_in, setup, zeroed = sem("weights_in"), sem("setup"), sem("zeroed")
        centred, xs_ready, m_ready, m_read = sem("centred"), sem("xs_ready"), sem("job_ready"), sem("job_read")
        sig_ready, front, logs_ready, roots_ready, hi_ready, parts_ready = (sem(n) for n in (
            "sigmoid_exp_ready", "front_steps", "root_logs_ready", "roots_ready", "hi_ready", "parts_ready"))
        parts_out, st_in, v_ready = sem("parts_out"), [sem("stacks_in0"), sem("stacks_in1")], sem("v_ready")
        i_ready, d_ready, u_ready, root_ready, arg_ready, dist_ready = (sem(n) for n in (
            "inner_ready", "d_ready", "u_ready", "root_ready", "arg_ready", "dist_ready"))
        log_ready, acosh_ready, part_step = sem("log_ready"), sem("acosh_ready"), sem("middle_part_ready")
        e_ready, top_ready, neg_ready, exp_done = (sem(n) for n in ("e_ready", "top_ready", "neg_ready", "exp_done"))
        rec_ready, rinv_ready, t_ready = sem("rec_ready"), sem("rinv_ready"), sem("t_ready")
        t_copied, pv_done, o_copied, act_step = [sem("t_copied0"), sem("t_copied1")], sem("pv_done"), sem("o_copied"), sem("act_step")
        bo_added = sem("bias_added")
        scr = g.scratch2
        NIN = 2 * NBLK * 3

        early, late = [("x", 0), ("f", 0), ("f", 1)], [("s", 0), ("s", 1)]
        jobs = Jobs([(0, 1, "x", 0, 2), (1, 0, "s", 0, 1), (1, 2, "s", 1, 1), (2, 1, "f", 0, 2), (2, 2, "u", 0, -1),
                     (3, 1, "f", 1, 2), (3, 2, "w", 0, -1), (4, 1, "o", 0, -1), (6, 1, "u", 1, -1),
                     (7, 0, "w", 1, -1), (7, 2, "o", 1, -1)],
                    before_first(early + late, 1) + [(kind, k, 1) for kind, k in early])

        def after_front(j, kind, k):
            first = [(x[0], x[1], x[2]) for x in jobs.first]
            if isinstance(j, int) and (kind, k, j) in first:
                return first.index((kind, k, j)) + 1
            return jobs.after(j - (1 if kind == "s" else 2), kind, k)

        def keys(u):
            return 1 if u // NC == 0 else TT

        def split(b, u, lag):
            return (b, u - lag, 0) if u >= lag else (b - 1, u - lag + UN, 1)

        def exists(b, u, lag):
            return not (isinstance(b, int) and not 0 <= UN * b + u - lag < UN * NB)

        def unit(b, u, lag):
            sq_, v, shift = split(b, u, lag)
            return sq_, v, sq_ * UN + v, keys(v) * P, shift

        def tiles_before(b, u, kt=None):
            kts = range(TT) if kt is None else (kt,)
            count = lambda units: sum(k < keys(v) for v in units for k in kts)
            return b * count(range(UN)) + count(range(u))

        loads = [(wall, w["wall"]), (ball, w["ball"]), (wo, w["wo"]), (bo, w["bo"]), (thr, w["thr"]),
                 (safe, w["qk_scale"]), (curv, w["log_k"])]
        C = [1.0]
        NSERIES = 6
        for k in range(1, NSERIES + 1):
            C.append(C[-1] / (2 * k * (2 * k + 1)))
        SMALL = float(np.float32(1.0 + 1e-6) - np.float32(1.0))
        SC = g.score_scale
        STEPS_N, STEPS_A, STEPS_SA, STEPS_R, STEPS_Z, STEPS_S = 2, 9, 14, 16, 16 + 5 + 4, 16 + 5 + NSERIES + 1 + 6
        STEPS = STEPS_S + 5

        with nc.Block() as block:
            @block.sync
            def _(sp):
                sp = Engine(sp)
                load_weights(sp, w_in, loads)
                sp.wait_ge(zeroed, 5)

                def counts(j, par):
                    v = (2 * j + 2, (j - par) * (8 * NIN), (j - 1) * UN, j * 32 + 32)
                    return v if isinstance(j, int) else tuple(sp.to_reg(x) for x in v)

                def bounce(par, first, n):
                    split_n, read_n, used_n, out_n = n
                    sp.wait_ge(parts_ready, split_n)
                    sp.wait_ge(st_in[par], read_n)
                    for kind in range(2):
                        sp.dma_start(scr[par, kind].rearrange("a p n -> p a n"), parts[:, par, kind, :, :]
                                     ).then_inc(parts_out, 16)
                    if not first:
                        sp.wait_ge(e_ready, used_n)
                    sp.wait_ge(parts_out, out_n)
                    for kind in (1, 0):
                        for i in range(NBLK):
                            r = 16 * i
                            sp.dma_start(qst[par][kind][r:r + 16, :, :],
                                         scr[par, kind, QPART[i], :, 0:T].rearrange("(c r) t -> r c t", r=16)
                                         ).then_inc(st_in[par], 16)
                            for hh in range(2):
                                src = scr[par, kind, KPART[i], :, T:2 * T].rearrange("(c h d) t -> h d c t", h=2, d=8)
                                sp.dma_start(kst[par][kind][r + 8 * hh:r + 8 * hh + 8, :, hh, :], src[hh]
                                             ).then_inc(st_in[par], 16)

                bounce(0, True, counts(0, 0))
                bounce(1, True, counts(1, 1))
                bounce(0, False, counts(2, 0))
                with sp.Fori(0, (NB - 2) // 2) as i:
                    odd, even = counts(i * 2 + 3, 1), counts(i * 2 + 4, 0)
                    bounce(1, False, odd)
                    bounce(0, False, even)
                sp.wait_ge(parts_out, 32 * (NB + 1))
                for i in range(2):
                    sp.wait_ge(st_in[i], 16 * NIN * (NB // 2 + 1 - i))

            @block.gpsimd
            def _(pool):
                clear_retired(pool, g)
                pool = Engine(pool)
                tt = nc.gpsimd.tensor_tensor
                nc.gpsimd.memset(zero[:, :], 0.0).then_inc(zeroed, 1)
                nc.gpsimd.memset(spare[:, :], 0.0).then_inc(t_copied[1], 1)
                moments_pool(pool, g, st, tiles=FIRST)
                moments_done(pool, st)

                def x_normalise(j, par):
                    tiles = bass.ds(j * TT, TT)
                    spread = lambda x: x[:, tiles].unsqueeze(2).broadcast_to([P, TT, P])
                    pool.wait_ge(xs_ready, j)
                    tt(xc[:, :, :], g.X[:, tiles, :], spread(g.mean), ALU.subtract).then_inc(centred, 1)
                    pool.wait_ge(centred, j + 1)
                    tt(xs[:, par, :, :], xc[:, :, :], spread(g.rstd), ALU.mult).then_inc(xs_ready, 1)

                def split_parts(j, par, k):
                    pool.wait_ge(m_read, after_front(j, "s", k))
                    tt(parts[:, par, k, 1, :], resid[:, k, :], zero[:, 0:1].broadcast_to([P, 2 * T]), ALU.add
                       ).then_inc(part_step, 1)
                    pool.wait_ge(part_step, 2 * j + k + 1)
                    tt(parts[:, par, k, 2, :], resid[:, k, :], parts[:, par, k, 1, :], ALU.subtract
                       ).then_inc(parts_ready, 1)

                x_normalise(0, 0)
                x_normalise(1, 1)
                for i in range(2):
                    for k in range(2):
                        nc.gpsimd.memset(kst[i][k][:, :, :, :], 0.0).then_inc(zeroed, 1)
                for i in range(2):
                    c = Chain(pool, zeroed, 5 + 2 * i)
                    c(nc.gpsimd.memset(vp[i][:, :, :, :], 0.0))
                    c(nc.gpsimd.memset(vp[i][:, :, :, 8:9], 1.0))

                def argument(b, u):
                    if not exists(b, u, 0):
                        return
                    n, nk = UN * b + u, keys(u) * P * HC
                    pool.wait_ge(root_ready, n + 1)
                    x = ww[:, u % WRING, 0:nk]
                    nc.gpsimd.tensor_tensor(x, x, dd[:, u % DRING, 0:nk], ALU.add).then_inc(arg_ready, 1)

                for k in range(2):
                    split_parts(0, 0, k)
                moments_pool(pool, g, st, 1, LATER)
                moments_done(pool, st, 1)

                def body(b, par):
                    for u in range(UN):
                        last = isinstance(b, int) and b == NB
                        if u == 0 and not last:
                            x_normalise(b + 2, par)
                        argument(b, u)
                        if u in (1, 2) and not last:
                            split_parts(b + 1, par ^ 1, u - 1)

                over_sequences(pool, body, body)

            @block.tensor
            def _(pe):
                pe = Engine(pe)
                pe.wait_ge(w_in, 16 * len(loads))

                def run(kind, k, j, par, n):
                    pe.wait_ge(m_read, n)
                    if kind == "x":
                        pe.wait_ge(xs_ready, j + 1)
                        for t in range(TT):
                            ins = nc.tensor.transpose(M[:, t * P:(t + 1) * P], xs[:, par, t, :], g.ident[:, :])
                    elif kind == "f":
                        ins = nc.tensor.matmul(M[:, 0:NCOL], xnT[:, k * P:(k + 1) * P], wall[:, :], start=True,
                                               stop=True)
                    elif kind == "s":
                        pe.wait_ge(front, (j + 1) * STEPS)
                        for t in range(TT):
                            qop = ops[:, t, k, :]
                            kop = ops[:, t, 2, :] if k else F[par][:, t, P:2 * P]
                            nc.tensor.transpose(M[:, t * P:(t + 1) * P], qop, g.ident[:, :])
                            ins = nc.tensor.transpose(M[:, T + t * P:T + (t + 1) * P], kop, g.ident[:, :])
                    elif kind == "u":
                        pe.wait_ge(o_copied, j * TT + k + 1)
                        for c in range(NC):
                            ins = nc.tensor.transpose(M[:, c * P:(c + 1) * P], osb[:, k, c, :], g.ident[:, :])
                    elif kind == "w":
                        ins = nc.tensor.transpose(M[:, 0:P], y[:, :], g.ident[:, :])
                    else:
                        ins = nc.tensor.matmul(M[:, 0:P], yT[:, :], wo[:, :], start=True, stop=True)
                    ins.then_inc(m_ready, 1)

                def transposes(b, u):
                    if not exists(b, u, LAG_T):
                        return
                    sq_, v, n, nk, _ = unit(b, u, LAG_T)
                    pe.wait_ge(exp_done, n + 1)
                    for kt in range(nk // P):
                        pe.wait_ge(t_copied[kt], tiles_before(sq_, v, kt) + kt)
                        for h in range(HC):
                            ins = nc.tensor.transpose(PT[kt][:, h * P:(h + 1) * P],
                                                      probs[:, v % PRING, h, kt * P:(kt + 1) * P], g.ident[:, :])
                        ins.then_inc(t_ready, 1)

                def products(out, par, kind, v, nk, mask):
                    t, c = v // NC, v % NC
                    out = out[:, 0:HC * nk].rearrange("p (h k) -> p h k", h=HC)
                    for i in range(HC // 2):
                        o2 = out[:, 2 * i:2 * i + 2, :]
                        ins = nc.tensor.matmul(o2, qst[par][kind][:, 2 * c + i, t * P:(t + 1) * P],
                                               kst[par][kind][:, 2 * c + i, :, 0:nk], start=True, stop=True)
                        if mask:
                            ins = nc.tensor.matmul(o2[:, :, t * P:(t + 1) * P], g.identb[:, :], g.maskb[:, :, :],
                                                   start=False, stop=True, skip_group_check=True)
                    return ins

                def inner(b, u, par):
                    if not exists(b, u, 0):
                        return
                    if u == 0:
                        pe.wait_ge(st_in[par], (b - par) * (8 * NIN) + 16 * NIN)
                    pe.wait_ge(d_ready, UN * b + u)
                    products(SI, par, 1, u, keys(u) * P, False).then_inc(i_ready, 1)

                def euclid(b, u, par):
                    if not exists(b, u, LAG_E):
                        return
                    sq_, v, n, nk, shift = unit(b, u, LAG_E)
                    pe.wait_ge(top_ready, n)
                    products(SE, par ^ shift, 0, v, nk, True).then_inc(e_ready, 1)

                def values(b, u, par):
                    if not exists(b, u, LAG_V):
                        return
                    sq_, v, n, nk, shift = unit(b, u, LAG_V)
                    c, t = v % NC, v // NC
                    for kt in range(nk // P):
                        pe.wait_ge(t_copied[kt], tiles_before(sq_, v, kt) + kt + 1)
                    if v == 0:
                        pe.wait_ge(v_ready, sq_ + 1)
                    if c == 0:
                        pe.wait_ge(o_copied, 2 * sq_ + t)
                    for kt in range(nk // P):
                        for h in range(HC):
                            ins = nc.tensor.matmul(O[32 * h:32 * h + 32, c, :], vp[par ^ shift][:, kt, HC * c + h, :],
                                                   probsT[:, v % TRING, kt, h * P:(h + 1) * P],
                                                   start=kt == 0, stop=kt == nk // P - 1, tile_position=(0, 32 * h))
                    ins.then_inc(pv_done, 1)

                for n, (kind, k, j) in enumerate(jobs.first):
                    run(kind, k, j, j, n)

                def body(b, par):
                    for u in range(UN):
                        for place, part in enumerate((
                                lambda: [inner(b, u, par), transposes(b, u)], lambda: euclid(b, u, par),
                                lambda: values(b, u, par))):
                            part()
                            for kind, k, j, shift, n in jobs.at(b, u, place):
                                run(kind, k, j, par ^ shift, n)

                over_sequences(pe, body, body)

            @block.scalar
            def _(act):
                act = Engine(act)
                nc.scalar.preload_act_table_set("natural_log_exp_and_others")
                act.wait_ge(w_in, 16 * len(loads))
                act.wait_ge(setup, 3)
                nc.scalar.activation(soft[:, :], soft[:, :], ACT.Exp).then_inc(act_step, 1)
                nc.scalar.activation(safe[:, :], safe[:, :], ACT.Exp, scale=-1.0).then_inc(act_step, 1)
                act.wait_ge(act_step, 1)
                nc.scalar.activation(soft[:, :], soft[:, :], ACT.Ln, bias=one[:, 0:1]).then_inc(act_step, 1)

                def read(kind, k, j, par, n):
                    if kind == "x":
                        act.wait_ge(m_ready, n + 1)
                        nc.scalar.activation(xnT[:, :], M[:, 0:T], ACT.Copy).then_inc(m_read, 1)
                    elif kind == "s":
                        act.wait_ge(m_ready, n + 1)
                        act.wait_ge(parts_out, (j - 1) * 32)
                        nc.scalar.activation(parts[:, par, k, 0, :], M[:, :], ACT.Copy).then_inc(hi_ready, 1)
                    elif kind == "w":
                        act.wait_ge(m_ready, n + 1)
                        nc.scalar.activation(yT[:, :], M[:, 0:P], ACT.Copy).then_inc(m_read, 1)

                def sigmoid_exp(j, par):
                    act.wait_ge(front, j * STEPS + STEPS_N)
                    nc.scalar.activation(sg[:, :, :], F[par][:, :, 3 * P:], ACT.Exp, scale=-1.0
                                         ).then_inc(sig_ready, 1)

                def inverse_roots(j, i):
                    act.wait_ge(front, j * STEPS + (STEPS_A, STEPS_S)[i])
                    nc.scalar.activation(roots[i][:, :, :], squares[i][:, :, :], ACT.Ln).then_inc(logs_ready, 1)
                    act.wait_ge(logs_ready, 2 * j + i + 1)
                    nc.scalar.activation(roots[i][:, :, :], roots[i][:, :, :], ACT.Exp, scale=-0.5
                                         ).then_inc(roots_ready, 1)

                def v_copy(j, par):
                    act.wait_ge(front, j * STEPS + STEPS_N)
                    if isinstance(j, int) and j < 2:
                        act.wait_ge(zeroed, 9)
                    act.wait_ge(pv_done, UN * (j - 1))
                    nc.scalar.activation(vp[par][:, :, :, 0:8],
                                         F[par][:, :, 2 * P:3 * P].rearrange("p t (h d) -> p t h d", d=8), ACT.Copy
                                         ).then_inc(v_ready, 1)

                def t_copy(b, u):
                    if not exists(b, u, LAG_T):
                        return
                    _, v, n, nk, _ = unit(b, u, LAG_T)
                    if nk > P:
                        sq_, _, _ = split(b, u, LAG_T)
                        act.wait_ge(t_ready, tiles_before(sq_, v) + 2)
                        act.wait_ge(pv_done, n - TRING + 1)
                        nc.scalar.activation(probsT[:, v % TRING, 1, :], PT[1][:, :], ACT.Copy
                                             ).then_inc(t_copied[1], 1)

                def root(b, u):
                    if not exists(b, u, 0):
                        return
                    n, nk = UN * b + u, keys(u) * P * HC
                    x = ww[:, u % WRING, 0:nk]
                    act.wait_ge(u_ready, n + 1)
                    nc.scalar.activation(x, x, ACT.Ln).then_inc(log_ready, 1)
                    act.wait_ge(log_ready, n + 1)
                    nc.scalar.activation(x, x, ACT.Exp, scale=0.5).then_inc(root_ready, 1)

                def distance(b, u):
                    if not exists(b, u, LAG_D):
                        return
                    sq_, v, n, nk, _ = unit(b, u, LAG_D)
                    x = ww[:, v % WRING, 0:HC * nk]
                    t, c = v // NC, v % NC
                    act.wait_ge(arg_ready, n + 1)
                    nc.scalar.activation(x, x, ACT.Ln, bias=one[:, 0:1]).then_inc(acosh_ready, 1)
                    act.wait_ge(acosh_ready, n + 1)
                    if v == 0:
                        act.wait_ge(front, sq_ * STEPS + STEPS_SA)
                    for h in range(HC):
                        y = x[:, h * nk:(h + 1) * nk]
                        sa = SA[:, bass.ds(sq_ * TT + t, 1), HC * c + h:HC * c + h + 1].rearrange("p a b -> p (a b)")
                        ins = nc.scalar.activation(y, y, ACT.Square, scale=sa)
                    ins.then_inc(dist_ready, 1)

                def exponentials(b, u):
                    if not exists(b, u, LAG_E):
                        return
                    sq_, v, n, nk, _ = unit(b, u, LAG_E)
                    r = v % PRING
                    act.wait_ge(neg_ready, n + 1)
                    for h in range(HC):
                        y = probs[:, r, h, 0:nk]
                        ins = nc.scalar.activation(y, y, ACT.Exp, bias=negtop[:, r, h:h + 1])
                    ins.then_inc(exp_done, 1)

                def o_copy(sq_, t):
                    if isinstance(sq_, int) and sq_ < 0:
                        return
                    act.wait_ge(pv_done, sq_ * UN + (t + 1) * NC)
                    act.wait_ge(m_ready, jobs.after(sq_, "u", t))
                    nc.scalar.activation(osb[:, t, :, :], O[:, :, :], ACT.Copy).then_inc(o_copied, 1)

                for n, (kind, k, j) in enumerate(jobs.first):
                    read(kind, k, j, j, n)
                    if (kind, k) == ("f", 1):
                        sigmoid_exp(j, j)
                        inverse_roots(j, 0)
                        inverse_roots(j, 1)
                v_copy(0, 0)

                def body(b, par):
                    last = isinstance(b, int) and b == NB
                    for u in range(UN):
                        for place, part in enumerate((lambda: t_copy(b, u), lambda: distance(b, u),
                                                      lambda: [root(b, u), exponentials(b, u)])):
                            part()
                            for kind, k, j, shift, n in jobs.at(b, u, place):
                                read(kind, k, j, par ^ shift, n)
                        if u == 1:
                            o_copy(b - 1, 0)
                        if u == 3 and not last:
                            sigmoid_exp(b + 2, par)
                        if u in (4, 7) and not last:
                            inverse_roots(b + 2, u // 7)
                        if u == 5:
                            o_copy(b - 1, 1)
                        if u == 6 and not last:
                            v_copy(b + 1, par ^ 1)

                over_sequences(act, body, body)

            @block.vector
            def _(dve):
                dve = Engine(dve)
                v_ = nc.vector
                halves_vector(dve, g, st, g.X, FIRST)
                moments_vector(dve, g, st, 1e-5, 2 * TT, tiles=FIRST)
                dve.wait_ge(w_in, 16 * len(loads))
                c = Chain(dve, setup)
                c(v_.memset(one[:, :], 1.0))
                c(v_.tensor_scalar(soft[:, :], curv[:, :], -1.0, None, ALU.mult))
                c(v_.tensor_tensor(soft[:, :], soft[:, :], curv[:, :], ALU.min))
                c(v_.tensor_scalar(curv[:, :], curv[:, :], 0.0, None, ALU.max))
                dve.wait_ge(act_step, 3)
                c(v_.tensor_tensor(curv[:, :], curv[:, :], soft[:, :], ALU.add))
                c(v_.tensor_scalar(curv[:, :], curv[:, :], 1e-6, None, ALU.add))
                c(v_.reciprocal(curv[:, :], curv[:, :]))
                c(v_.tensor_scalar(safe[:, :], safe[:, :], 1.0, None, ALU.add))
                c(v_.reciprocal(safe[:, :], safe[:, :]))
                c(v_.tensor_scalar(safe[:, :], safe[:, :], 1.5, None, ALU.mult))

                def read(kind, k, j, par, n):
                    if kind == "f":
                        dve.wait_ge(m_ready, n + 1)
                        dve.wait_ge(v_ready, j - 1)
                        v_.tensor_tensor(F[par][:, k, :], M[:, 0:NCOL], ball[:, :], ALU.add).then_inc(m_read, 1)
                    elif kind == "s":
                        dve.wait_ge(hi_ready, 2 * j + k + 1)
                        dve.wait_ge(parts_ready, 2 * j + k - 1)
                        v_.tensor_tensor(resid[:, k, :], M[:, :], parts[:, par, k, 0, :], ALU.subtract
                                         ).then_inc(m_read, 1)
                    elif kind == "u":
                        dve.wait_ge(m_ready, n + 1)
                        heads = M[:, :].rearrange("p (h d) -> p h d", d=32)
                        v_.reciprocal(rec[:, :], heads[:, :, 8]).then_inc(rec_ready, 1)
                        dve.wait_ge(rec_ready, j * TT + k + 1)
                        v_.tensor_scalar(rinv[:, :], rec[:, :], SPK[:, bass.ds(j * TT + k, 1)], None, ALU.mult
                                         ).then_inc(rinv_ready, 1)
                        dve.wait_ge(rinv_ready, j * TT + k + 1)
                        v_.tensor_tensor(y[:, :].rearrange("p (h d) -> p h d", d=8), heads[:, :, 0:8],
                                         rinv[:, :].unsqueeze(2).broadcast_to([P, H, 8]), ALU.mult
                                         ).then_inc(m_read, 1)
                    elif kind == "o":
                        dve.wait_ge(m_ready, n + 1)
                        dst = g.X[:, bass.ds(j * TT + k, 1), :]
                        v_.tensor_tensor(dst, dst, bo[:, :].unsqueeze(1), ALU.add).then_inc(bo_added, 1)
                        dve.wait_ge(bo_added, j * TT + k + 1)
                        v_.tensor_tensor(dst, dst, M[:, 0:P].unsqueeze(1), ALU.add).then_inc(m_read, 1)

                def front_operands(j, par, piece):
                    f = F[par]
                    fl = lambda x: x[:, :, :].rearrange("p t k -> p (t k)")
                    space = squares[1]
                    first = sq[:, :, :].rearrange("p t (k d) -> p (t k) d", d=8)[:, :, 0]
                    c = Chain(dve, front, j * STEPS + (0, STEPS_N, STEPS_A, STEPS_R, STEPS_Z, STEPS_S)[piece])

                    def refine(i):
                        x, y_, a = squares[i][:, :, :], roots[i][:, :, :], work[i][:, :, :]
                        dve.wait_ge(roots_ready, 2 * j + i + 1)
                        c(v_.tensor_tensor(a, y_, y_, ALU.mult))
                        c(v_.tensor_tensor(a, a, x, ALU.mult))
                        c(v_.tensor_scalar(a, a, -0.5, 1.5, ALU.mult, ALU.add))
                        c(v_.tensor_tensor(y_, y_, a, ALU.mult))

                    if piece == 0:
                        dve.wait_ge(m_read, after_front(j, "f", 1))
                        qk = f[:, :, 0:2 * P]
                        c(v_.tensor_tensor(sq[:, :, :], qk, qk, ALU.mult))
                        c(v_.tensor_reduce(out=fl(n2), in_=sq[:, :, :].rearrange("p t (k d) -> p (t k) d", d=8),
                                           axis=AX, op=ALU.add))
                        done = STEPS_N
                    elif piece == 1:
                        dve.wait_ge(sig_ready, j + 1)
                        c(v_.tensor_scalar(sg[:, :, :], sg[:, :, :], 1.0, None, ALU.add))
                        c(v_.reciprocal(sg[:, :, :], sg[:, :, :]))
                        alpha = sg[:, :, 0:H]
                        c(v_.tensor_scalar(SPK[:, bass.ds(j * TT, TT)], sg[:, :, H], thr[:, 0:1], None, ALU.is_gt))
                        c(v_.tensor_tensor(sal[:, :, :], alpha,
                                           curv[:, :].unsqueeze(1).broadcast_to([P, TT, H]), ALU.mult))
                        c(v_.tensor_scalar(oma[:, :, :], alpha, -SC, SC, ALU.mult, ALU.add))
                        for t in range(TT):
                            v_.tensor_tensor(ops[:, t, 0, :].rearrange("p (h d) -> p h d", d=8),
                                             f[:, t, 0:P].rearrange("p (h d) -> p h d", d=8),
                                             oma[:, t, :].unsqueeze(2).broadcast_to([P, H, 8]), ALU.mult)
                        c(v_.tensor_scalar(squares[0][:, :, 0:H], sal[:, :, :], 1e-30, None, ALU.max))
                        c(v_.tensor_scalar(squares[0][:, :, H:], n2[:, :, :], 1e-24, None, ALU.max))
                        done = STEPS_A
                    elif piece == 2:
                        refine(0)
                        c(v_.tensor_tensor(SA[:, bass.ds(j * TT, TT), :], sal[:, :, :], roots[0][:, :, 0:H], ALU.mult))
                        c(v_.tensor_scalar(rn[:, :, :], roots[0][:, :, H:], safe[:, 0:1], None, ALU.mult))
                        c(v_.tensor_tensor(fl(rn2), fl(rn), fl(rn), ALU.mult))
                        done = STEPS_R
                    elif piece == 3:
                        c(v_.scalar_tensor_tensor(out=fl(z), in0=first, scalar=-2.0, in1=fl(n2), op0=ALU.mult,
                                                  op1=ALU.add))
                        c(v_.tensor_tensor(fl(space), fl(n2), first, ALU.subtract))
                        c(v_.tensor_tensor(fl(z), fl(z), fl(rn2), ALU.mult))
                        c(v_.tensor_tensor(fl(space), fl(space), fl(rn2), ALU.mult))
                        c(v_.tensor_scalar(fl(z), fl(z), 1e-8, None, ALU.max))
                        c(v_.tensor_scalar(fl(gz), fl(z), C[NSERIES], None, ALU.mult))
                        for k in range(NSERIES - 1, NSERIES - 4, -1):
                            c(v_.scalar_tensor_tensor(out=fl(gz), in0=fl(gz), scalar=C[k], in1=fl(z), op0=ALU.add,
                                                      op1=ALU.mult))
                        done = STEPS_Z
                    elif piece == 4:
                        for k in range(NSERIES - 4, 0, -1):
                            c(v_.scalar_tensor_tensor(out=fl(gz), in0=fl(gz), scalar=C[k], in1=fl(z), op0=ALU.add,
                                                      op1=ALU.mult))
                        c(v_.tensor_scalar(fl(gz), fl(gz), C[0], None, ALU.add))
                        c(v_.tensor_tensor(fl(rn), fl(rn), fl(gz), ALU.mult))
                        c(v_.tensor_tensor(fl(gz), fl(gz), fl(gz), ALU.mult))
                        c(v_.tensor_tensor(fl(space), fl(space), fl(gz), ALU.mult))
                        c(v_.tensor_scalar(fl(space), fl(space), 1.0, None, ALU.add))
                        c(v_.tensor_scalar(rn[:, :, 0:H], rn[:, :, 0:H], -1.0, None, ALU.mult))
                        for t in range(TT):
                            ins = v_.tensor_tensor(ops[:, t, 1:3, :].rearrange("p s (h d) -> p (s h) d", d=8),
                                                   f[:, t, 0:2 * P].rearrange("p (k d) -> p k d", d=8),
                                                   rn[:, t, :].unsqueeze(2).broadcast_to([P, 2 * H, 8]), ALU.mult)
                        c(ins)
                        done = STEPS_S
                    else:
                        refine(1)
                        out = ops[:, :, 1:3, :].rearrange("p t s (h d) -> p t (s h) d", d=8)[:, :, :, 0]
                        c(v_.tensor_tensor(out, space[:, :, :], roots[1][:, :, :], ALU.mult))
                        done = STEPS
                    if isinstance(j, int):
                        assert c.n == j * STEPS + done, (c.n, done)

                def excess(b, u):
                    if not exists(b, u, 0):
                        return
                    n, nk = UN * b + u, keys(u) * P * HC
                    d, x = dd[:, u % DRING, 0:nk], ww[:, u % WRING, 0:nk]
                    dve.wait_ge(i_ready, n + 1)
                    dve.wait_ge(arg_ready, n - DRING + 1)
                    v_.tensor_scalar(d, SI[:, 0:nk], 1.0, SMALL, ALU.subtract, ALU.max).then_inc(d_ready, 1)
                    dve.wait_ge(d_ready, n + 1)
                    dve.wait_ge(top_ready, n - WRING + 1)
                    v_.scalar_tensor_tensor(out=x, in0=d, scalar=2.0, in1=d, op0=ALU.add, op1=ALU.mult
                                            ).then_inc(u_ready, 1)

                def scores(b, u):
                    if exists(b, u, LAG_E):
                        _, ev, en, nk, _ = unit(b, u, LAG_E)
                        r, x = ev % PRING, ww[:, ev % WRING, 0:HC * nk]
                        for h in range(HC):
                            part = slice(h * nk, (h + 1) * nk)
                            ins = v_.tensor_tensor_reduce(
                                out=probs[:, r, h, 0:nk], in0=SE[:, part], in1=x[:, part], scale=1.0, scalar=MASKED,
                                op0=ALU.subtract, op1=ALU.max, accum_out=top[:, r, h:h + 1])
                        ins.then_inc(top_ready, 1)
                        dve.wait_ge(top_ready, en + 1)
                        v_.tensor_scalar(negtop[:, r, :], top[:, r, :], -1.0, None, ALU.mult).then_inc(neg_ready, 1)

                def score_waits(b, u):
                    if not exists(b, u, LAG_E):
                        return
                    _, _, n, _, _ = unit(b, u, LAG_E)
                    dve.wait_ge(e_ready, n + 1)
                    dve.wait_ge(dist_ready, n + 1)
                    if exists(b, u, LAG_E + PRING):
                        old_sq, old, _, _, _ = unit(b, u, LAG_E + PRING)
                        dve.wait_ge(t_ready, tiles_before(old_sq, old) + keys(old))

                def t_copy(b, u):
                    if not exists(b, u, LAG_T):
                        return score_waits(b, u)
                    sq_, v, n, nk, _ = unit(b, u, LAG_T)
                    dve.wait_ge(t_ready, tiles_before(sq_, v) + 1)
                    dve.wait_ge(pv_done, n - TRING + 1)
                    score_waits(b, u)
                    v_.tensor_copy(probsT[:, v % TRING, 0, :], PT[0][:, :]).then_inc(t_copied[0], 1)

                for n, (kind, k, j) in enumerate(jobs.first):
                    read(kind, k, j, j, n)
                    if (kind, k) == ("f", 1):
                        for piece in range(6 - j):
                            front_operands(j, j, piece)

                halves_vector(dve, g, st, g.X, LATER)
                moments_vector(dve, g, st, 1e-5, NT + 2 * PAD, 1, tiles=LATER)

                def body(b, par):
                    last = isinstance(b, int) and b == NB
                    for u in range(UN):
                        for place, part in enumerate((lambda: [excess(b, u), t_copy(b, u)], lambda: None,
                                                      lambda: scores(b, u))):
                            part()
                            for kind, k, j, shift, n in jobs.at(b, u, place):
                                read(kind, k, j, par ^ shift, n)
                        if u == 0 and not last:
                            front_operands(b + 1, par ^ 1, 5)
                        if u in (3, 4, 5, 6, 7) and not last:
                            front_operands(b + 2, par, u - 3)

                over_sequences(dve, body, body)
        retire(g, st)


def moe_stage(nc, g, w, name):
    E, G, EPG, HK = 8, 2, 4, 2
    with ExitStack() as ctx:
        st = Scope(nc, ctx, name)
        sb, ps, sem = st.sb, st.ps, st.sem
        wa, wb = sb("wa", [P, 2 * HK, P]), sb("wb", [P, 2 * HK, P])
        wso, w2 = sb("wso", [P, HK, P]), sb("w2", [P, HK, E * P])
        wg, bg = sb("wg", [P, G + E]), sb("bg", [P, G + E])
        n1, n2 = sb("n1", [P, P]), sb("n2", [P, P])
        XPT = sb("XPT", [P, NB * T])
        xs, xc, xt = sb("xs", [P, 2, TT, P]), sb("xc", [P, TT, P]), sb("xt", [P, 2, T])
        logits = sb("logits", [P, NT + 2 * PAD, G + E])
        gmax, gexp, gsum, gsel = sb("gmax", [P, NT]), sb("gexp", [P, NT, G]), sb("gsum", [P, NT]), sb("gsel", [P, NT, G])
        emax, esum = sb("emax", [P, NT * G]), sb("esum", [P, NT * G])
        prob, ahead, tie = sb("prob", [P, NT * G, EPG]), sb("ahead", [P, NT * G, EPG, EPG]), sb("tie", [P, NT * G, EPG, EPG])
        rank, earlier = sb("rank", [P, NT * G, EPG]), sb("earlier", [P, EPG, EPG])
        weight = sb("weight", [P, NT * E])
        gate, hid = sb("gate", [P, 2 * HK * T]), sb("hid", [P, 2, 2 * HK, T])
        acc = sb("acc", [P, 2, 2, P])
        GA, GB = ps("GA", [P, 2 * HK * T]), ps("GB", [P, 2 * HK * T])
        Y = [ps(f"Y{i}", [P, 4 * P]) for i in range(2)]
        SH, M = ps("SH", [P, 512]), ps("M", [P, 512])
        moments_sems(st)
        scaled = sem("scaled")
        w_in, made = sem("weights_in"), sem("earlier_made")
        xs_ready, xT_ready, xt_ready, xp_ready, xpt_ready = (sem(n) for n in (
            "xs_ready", "xT_ready", "xt_ready", "xp_ready", "xpt_ready"))
        lg_ready, lg_used, gate_step, gate_act = (sem(n) for n in ("lg_ready", "lg_used", "gate_step", "gate_act"))
        ga_ready, gb_ready, silu_done, hid_ready = (sem(n) for n in ("ga_ready", "gb_ready", "silu_done", "hid_ready"))
        sh_ready, sh_used, y_ready, acc_step = (sem(n) for n in ("sh_ready", "sh_used", "y_ready", "acc_step"))
        add_step, x_done = sem("add_step"), sem("x_done")
        loads = [(wa, w["wa"]), (wb, w["wb"]), (wso, w["wso"]), (w2, w["w2"]), (wg, w["wg"]), (bg, w["bg"]),
                 (n1, w["n1"]), (n2, w["n2"])]

        with nc.Block() as block:
            @block.sync
            def _(sp):
                sp = Engine(sp)
                load_weights(sp, w_in, loads)

            @block.gpsimd
            def _(pool):
                clear_retired(pool, g)
                pool = Engine(pool)
                c = Chain(pool, made)
                c(nc.gpsimd.memset(earlier[:, :, :], 1.0))
                c(nc.gpsimd.affine_select(out=earlier[:, :, :], in_=earlier[:, :, :], compare_op=ALU.is_gt, fill=0.0,
                                          base=0, pattern=[[1, EPG], [-1, EPG]], channel_multiplier=0))
                moments_pool(pool, g, st, 0)
                moments_done(pool, st, 0)
                pool.wait_ge(w_in, 16 * len(loads))

                def gating(b, par):
                    tiles = bass.ds(b * TT, TT)
                    pool.wait_ge(xs_ready, b)
                    nc.gpsimd.tensor_tensor(xc[:, :, :], g.XP[:, tiles, :],
                                            g.rstd[:, tiles].unsqueeze(2).broadcast_to([P, TT, P]), ALU.mult
                                            ).then_inc(scaled, 1)
                    pool.wait_ge(scaled, b + 1)
                    pool.wait_ge(xT_ready, b - 1)
                    pool.wait_ge(xp_ready, b - 1)
                    nc.gpsimd.tensor_tensor(xs[:, par, :, :], xc[:, :, :],
                                            n1[:, :].unsqueeze(1).broadcast_to([P, TT, P]), ALU.mult
                                            ).then_inc(xs_ready, 1)

                in_order(pool, gating, 0)
                moments_pool(pool, g, st, 1)

            @block.tensor
            def _(pe):
                pe = Engine(pe)
                pe.wait_ge(w_in, 16 * len(loads))

                def gating(b, par):
                    if there(b, 0):
                        pe.wait_ge(xs_ready, b + 1)
                        pe.wait_ge(xpt_ready, b - 1)
                        xT = (GA, GB)[par]
                        for t in range(TT):
                            ins = nc.tensor.transpose(xT[:, t * P:(t + 1) * P], xs[:, par, t, :], g.ident[:, :])
                        ins.then_inc(xT_ready, 1)
                    if there(b, 1):
                        pe.wait_ge(xt_ready, b)
                        pe.wait_ge(lg_used, b - 1)
                        for t in range(TT):
                            ins = nc.tensor.matmul(M[:, t * 16:t * 16 + G + E], xt[:, par ^ 1, t * P:(t + 1) * P],
                                                   wg[:, :], start=True, stop=True)
                        ins.then_inc(lg_ready, 1)

                in_order(pe, gating, 1)

                def up(b, which, dst, used, done):
                    if not there(b, 0):
                        return
                    pe.wait_ge(used, b)
                    for k in range(2 * HK):
                        ins = nc.tensor.matmul(dst[:, k * T:(k + 1) * T], which[:, k, :], XPT[:, bass.ds(b * T, T)],
                                               start=True, stop=True)
                    ins.then_inc(done, 1)

                def down(b, par, t):
                    pe.wait_ge(sh_used, b * TT + t)
                    for kk in range(HK):
                        ins = nc.tensor.matmul(SH[:, 0:P], hid[:, par, kk, t * P:(t + 1) * P], wso[:, kk, :],
                                               start=kk == 0, stop=kk == HK - 1)
                    ins.then_inc(sh_ready, 1)
                    for half in range(2):
                        pe.wait_ge(acc_step, (b * TT + t - 1) * (E + 1) + 4 * (half + 1))
                        for kk in range(HK):
                            ins = nc.tensor.matmul(Y[half][:, :], hid[:, par, HK + kk, t * P:(t + 1) * P],
                                                   w2[:, kk, half * 4 * P:(half + 1) * 4 * P],
                                                   start=kk == 0, stop=kk == HK - 1)
                        ins.then_inc(y_ready, 1)

                pe.wait_ge(xpt_ready, NB)
                pe.wait_ge(xp_ready, NB)

                def experts(b, par):
                    up(b, wa, GA, silu_done, ga_ready)
                    if there(b, 1):
                        pe.wait_ge(hid_ready, b)
                        down(b - 1, par ^ 1, 0)
                    up(b, wb, GB, hid_ready, gb_ready)
                    if there(b, 1):
                        down(b - 1, par ^ 1, 1)

                in_order(pe, experts, 1)

            @block.scalar
            def _(act):
                act = Engine(act)
                def gating(b, par):
                    if there(b, 0):
                        act.wait_ge(xT_ready, b + 1)
                        act.wait_ge(lg_ready, b - 1)
                        xT = (GA, GB)[par]
                        nc.scalar.activation(xt[:, par, :], xT[:, 0:T], ACT.Copy).then_inc(xt_ready, 1)
                        nc.scalar.activation(XPT[:, bass.ds(b * T, T)], xT[:, 0:T], ACT.Copy).then_inc(xpt_ready, 1)
                        nc.scalar.activation(g.XP[:, bass.ds(b * TT, TT), :], xs[:, par, :, :], ACT.Copy
                                             ).then_inc(xp_ready, 1)

                in_order(act, gating, 0)
                act.wait_ge(gate_act, 1)
                nc.scalar.activation(gexp[:, :, :], gexp[:, :, :], ACT.Exp).then_inc(gate_act, 1)
                act.wait_ge(gate_act, 3)
                nc.scalar.activation(prob[:, :, :], prob[:, :, :], ACT.Exp).then_inc(gate_act, 1)

                def experts(b, par):
                    act.wait_ge(ga_ready, b + 1)
                    act.wait_ge(hid_ready, b)
                    nc.scalar.activation(gate[:, :], GA[:, :], ACT.Silu).then_inc(silu_done, 1)

                in_order(act, experts, 0)

            @block.vector
            def _(dve):
                dve = Engine(dve)
                halves_vector(dve, g, st, g.XP, slice(0, NT))
                moments_vector(dve, g, st, 1e-6, NT, 0, rms=True)
                dve.wait_ge(w_in, 16 * len(loads))

                def gating(b, par):
                    if there(b, 1):
                        dve.wait_ge(lg_ready, b)
                        ins = nc.vector.tensor_tensor(
                            logits[:, bass.ds((b - 1) * TT, TT), :],
                            M[:, 0:32].rearrange("p (t k) -> p t k", t=TT)[:, :, 0:G + E],
                            bg[:, :].unsqueeze(1).broadcast_to([P, TT, G + E]), ALU.add)
                        ins.then_inc(lg_used, 1)

                in_order(dve, gating, 1)
                dve.wait_ge(lg_used, NB)
                c = Chain(dve, gate_step)
                v = nc.vector
                gl, el = logits[:, 0:NT, 0:G], logits[:, 0:NT, G:].rearrange("p n (g e) -> p n g e", g=G)
                flat = lambda x: x.rearrange("p (n g) e -> p n g e", g=G)
                pairs = lambda x: x.rearrange("p (n g) -> p n g", g=G)
                c(v.tensor_reduce(out=gmax[:, :], in_=gl, axis=AX, op=ALU.max))
                v.tensor_tensor(gexp[:, :, :], gl, gmax[:, :].unsqueeze(2).broadcast_to([P, NT, G]), ALU.subtract
                                ).then_inc(gate_act, 1)
                c(v.tensor_reduce(out=pairs(emax[:, :]), in_=el, axis=AX, op=ALU.max))
                dve.wait_ge(gate_act, 2)
                v.tensor_tensor(flat(prob[:, :, :]), el,
                                pairs(emax[:, :]).unsqueeze(3).broadcast_to([P, NT, G, EPG]), ALU.subtract
                                ).then_inc(gate_act, 1)
                c(v.tensor_reduce(out=gsum[:, :], in_=gexp[:, :, :], axis=AX, op=ALU.add))
                c(v.reciprocal(gsum[:, :], gsum[:, :]))
                c(v.tensor_tensor(gsel[:, :, 0], gexp[:, :, 0], gexp[:, :, 1], ALU.is_ge))
                c(v.tensor_scalar(gsel[:, :, 1], gsel[:, :, 0], -1.0, 1.0, ALU.mult, ALU.add))
                c(v.tensor_tensor(gexp[:, :, :], gexp[:, :, :], gsel[:, :, :], ALU.mult))
                c(v.tensor_tensor(gexp[:, :, :], gexp[:, :, :], gsum[:, :].unsqueeze(2).broadcast_to([P, NT, G]),
                                  ALU.mult))
                dve.wait_ge(gate_act, 4)
                c(v.tensor_reduce(out=esum[:, :], in_=prob[:, :, :], axis=AX, op=ALU.add))
                c(v.reciprocal(esum[:, :], esum[:, :]))
                c(v.tensor_tensor(esum[:, :], esum[:, :], gexp[:, :, :].rearrange("p n g -> p (n g)"), ALU.mult))
                c(v.tensor_tensor(prob[:, :, :], prob[:, :, :], esum[:, :].unsqueeze(2).broadcast_to([P, NT * G, EPG]),
                                  ALU.mult))
                full = [P, NT * G, EPG, EPG]
                mine_, other = prob[:, :, :].unsqueeze(3).broadcast_to(full), prob[:, :, :].unsqueeze(2).broadcast_to(full)
                c(v.tensor_tensor(ahead[:, :, :, :], other, mine_, ALU.is_gt))
                c(v.tensor_tensor(tie[:, :, :, :], other, mine_, ALU.is_equal))
                dve.wait_ge(made, 2)
                c(v.tensor_tensor(tie[:, :, :, :], tie[:, :, :, :],
                                  earlier[:, :, :].unsqueeze(1).broadcast_to(full), ALU.mult))
                c(v.tensor_tensor(ahead[:, :, :, :], ahead[:, :, :, :], tie[:, :, :, :], ALU.add))
                c(v.tensor_reduce(out=rank[:, :, :], in_=ahead[:, :, :, :], axis=AX, op=ALU.add))
                c(v.scalar_tensor_tensor(out=weight[:, :].rearrange("p (n e) -> p n e", e=EPG), in0=rank[:, :, :],
                                         scalar=2.0, in1=prob[:, :, :], op0=ALU.is_lt, op1=ALU.mult))
                dve.wait_ge(xp_ready, NB)

                def combine(b, t):
                    tile = b * TT + t
                    a = acc[:, t, :, :]
                    n = tile * 9
                    dve.wait_ge(sh_ready, tile + 1)
                    v.tensor_tensor(a[:, 0:1, :], g.XP[:, bass.ds(tile, 1), :], SH[:, 0:P].unsqueeze(1), ALU.add
                                    ).then_inc(sh_used, 1)
                    for e in range(E):
                        if e % 4 == 0:
                            dve.wait_ge(y_ready, tile * 2 + e // 4 + 1)
                        src = Y[e // 4][:, (e % 4) * P:(e % 4 + 1) * P]
                        we = weight[:, bass.ds(tile * E + e, 1)]
                        k = e % 2
                        if e == 0:
                            dve.wait_ge(sh_used, tile + 1)
                        elif e >= 2:
                            dve.wait_ge(acc_step, n + e - 1)
                        if e == 1:
                            ins = v.tensor_scalar(a[:, 1, :], src, we, None, ALU.mult)
                        else:
                            ins = v.scalar_tensor_tensor(out=a[:, k, :], in0=src, scalar=we, in1=a[:, k, :],
                                                         op0=ALU.mult, op1=ALU.add)
                        ins.then_inc(acc_step, 1)
                    dve.wait_ge(acc_step, n + E)
                    v.tensor_tensor(g.XP[:, bass.ds(tile, 1), :], a[:, 0:1, :], a[:, 1:2, :], ALU.add
                                    ).then_inc(acc_step, 1)
                    dve.wait_ge(acc_step, n + 9)
                    v.bn_stats(g.bn6[:, bass.ds(tile * 6, 6)], g.XP[:, bass.ds(tile, 1), :]).then_inc(st.bn_done, 1)
                    dve.wait_ge(st.bn_done, NT + tile + 1)
                    row = g.XP[:, bass.ds(tile, 1), :]
                    v.tensor_tensor(row, row, n2[:, :].unsqueeze(1), ALU.mult).then_inc(add_step, 1)

                def experts(b, par):
                    if there(b, 1):
                        combine(b - 1, 0)
                    if there(b, 0):
                        dve.wait_ge(gb_ready, b + 1)
                        dve.wait_ge(silu_done, b + 1)
                        v.tensor_tensor(hid[:, par, :, :], gate[:, :].rearrange("p (k t) -> p k t", t=T),
                                        GB[:, :].rearrange("p (k t) -> p k t", t=T), ALU.mult).then_inc(hid_ready, 1)
                    if there(b, 1):
                        combine(b - 1, 1)

                in_order(dve, experts, 1)
                moments_vector(dve, g, st, 1e-6, 2 * NT, 1, rms=True)
                moments_done(dve, st, 1)
                dve.wait_ge(add_step, NT)
                with dve.Fori(0, NT // 8) as i:
                    for k in range(8):
                        tile = bass.ds(i * 8 + k, 1)
                        out = g.X[:, tile, :]
                        v.scalar_tensor_tensor(out=out, in0=g.XP[:, tile, :], scalar=g.rstd[:, tile], in1=out,
                                               op0=ALU.mult, op1=ALU.add).then_inc(x_done, 1)
        retire(g, st)


def qlora_stage(nc, g, w, name):
    NBLOCK, R = 3, 32
    with ExitStack() as ctx:
        st = Scope(nc, ctx, name)
        sb, ps, sem = st.sb, st.ps, st.sem
        NL = 2 * NBLOCK
        qw, scl = sb("qw", [P, NL, P], I32), sb("scl", [P, NL, P])
        la, lb = sb("la", [R, NL, P]), sb("lb", [R, NL, P])
        wt = sb("wt", [P, NL, P])
        b1, b2 = sb("b1", [P, NBLOCK, P]), sb("b2", [P, NBLOCK])
        gam, bet = sb("gam", [P, NBLOCK]), sb("bet", [P, NBLOCK])
        HT = sb("HT", [P, NB * T])
        zs, zc, yT, hT = sb("zs", [P, 2, TT, P]), sb("zc", [P, TT, P]), sb("yT", [P, 2, T]), sb("hT", [P, 2, T])
        ZT = [ps(f"ZT{i}", [P, 512]) for i in range(2)]
        H2 = [ps(f"H2{i}", [P, 512]) for i in range(2)]
        Y1 = [ps(f"Y1{i}", [P, 512]) for i in range(2)]
        moments_sems(st)
        centred = sem("centred")
        w_in, deq, lora_ready, w_ready = sem("weights_in"), sem("dequantised"), sem("lora_ready"), sem("weights_ready")
        zs_ready, zT_ready, act_done, h2_ready, h_ready, ht_copied, y1_ready, y1_used = (sem(n) for n in (
            "zs_ready", "zT_ready", "act_done", "h2_ready", "h_ready", "ht_copied", "y1_ready", "y1_used"))
        loads = [(qw, w["qw"]), (scl, w["scl"]), (la, w["la"]), (lb, w["lb"]), (b1, w["b1"]), (b2, w["b2"]),
                 (gam, w["gam"]), (bet, w["bet"])]
        ROUNDS = range(NBLOCK + 1)

        with nc.Block() as block:
            @block.sync
            def _(sp):
                sp = Engine(sp)
                load_weights(sp, w_in, loads)

            @block.gpsimd
            def _(pool):
                clear_retired(pool, g)
                pool = Engine(pool)
                for r in ROUNDS:
                    moments_pool(pool, g, st, r)
                    moments_done(pool, st, r)

                    def step(b, par, r=r):
                        n = r * NB + b
                        tiles = bass.ds(b * TT, TT)
                        spread = lambda x: x[:, tiles].unsqueeze(2).broadcast_to([P, TT, P])
                        pool.wait_ge(zs_ready, n)
                        nc.gpsimd.tensor_tensor(zc[:, :, :], (g.X if r == 0 else g.XP)[:, tiles, :], spread(g.mean),
                                                ALU.subtract).then_inc(centred, 1)
                        pool.wait_ge(centred, n + 1)
                        pool.wait_ge(zT_ready, n - 1)
                        nc.gpsimd.tensor_tensor(zs[:, par, :, :], zc[:, :, :], spread(g.rstd), ALU.mult
                                                ).then_inc(zs_ready, 1)

                    in_order(pool, step, 0)

            @block.tensor
            def _(pe):
                pe = Engine(pe)
                pe.wait_ge(w_in, 16 * len(loads))
                lo = [ZT[0], H2[0]]
                for i in range(NL):
                    ins = nc.tensor.matmul(lo[i // 4][:, (i % 4) * P:(i % 4 + 1) * P], la[:, i, :], lb[:, i, :],
                                           start=True, stop=True)
                ins.then_inc(lora_ready, 1)
                pe.wait_ge(w_ready, 2)
                for r in ROUNDS:
                    def step(b, par, r=r):
                        n = r * NB + b
                        if there(b, 0):
                            pe.wait_ge(zs_ready, n + 1)
                            pe.wait_ge(act_done, n - 1)
                            for t in range(TT):
                                ins = nc.tensor.transpose(ZT[par][:, t * P:(t + 1) * P], zs[:, par, t, :],
                                                          g.ident[:, :])
                            ins.then_inc(zT_ready, 1)
                        if there(b, 1) and r > 0:
                            pe.wait_ge(act_done, n)
                            pe.wait_ge(h_ready, n - 2)
                            nc.tensor.matmul(H2[par ^ 1][:, 0:T], wt[:, 2 * r - 1, :], yT[:, par ^ 1, :],
                                             start=True, stop=True).then_inc(h2_ready, 1)
                        if there(b, 2):
                            pe.wait_ge(h_ready, n - 1)
                            pe.wait_ge(y1_used, n - 3)
                            for t in range(TT):
                                if r < NBLOCK:
                                    ins = nc.tensor.matmul(Y1[par][:, t * P:(t + 1) * P],
                                                           hT[:, par, t * P:(t + 1) * P], wt[:, 2 * r, :],
                                                           start=True, stop=True)
                                else:
                                    ins = nc.tensor.transpose(Y1[par][:, t * P:(t + 1) * P],
                                                              hT[:, par, t * P:(t + 1) * P], g.ident[:, :])
                            ins.then_inc(y1_ready, 1)
                    in_order(pe, step, 2)

            @block.scalar
            def _(act):
                act = Engine(act)
                act.wait_ge(w_in, 16 * len(loads))
                for r in ROUNDS:
                    def step(b, par, r=r):
                        n = r * NB + b
                        if there(b, 0):
                            act.wait_ge(zT_ready, n + 1)
                            if r == 0:
                                act.wait_ge(y1_ready, n - 1)
                                nc.scalar.activation(hT[:, par, :], ZT[par][:, 0:T], ACT.Copy).then_inc(h_ready, 1)
                                nc.scalar.activation(HT[:, bass.ds(b * T, T)], ZT[par][:, 0:T], ACT.Copy
                                                     ).then_inc(act_done, 1)
                            else:
                                act.wait_ge(h2_ready, n - NB - 1)
                                nc.scalar.activation(yT[:, par, :], ZT[par][:, 0:T], ACT.Gelu,
                                                     scale=gam[:, r - 1:r], bias=bet[:, r - 1:r]
                                                     ).then_inc(act_done, 1)
                        if there(b, 1) and 0 < r:
                            act.wait_ge(h_ready, n)
                            nc.scalar.activation(HT[:, bass.ds((b - 1) * T, T)], hT[:, par ^ 1, :], ACT.Copy
                                                 ).then_inc(ht_copied, 1)
                    in_order(act, step, 1)

            @block.vector
            def _(dve):
                dve = Engine(dve)
                v = nc.vector
                dve.wait_ge(w_in, 16 * len(loads))
                c = Chain(dve, deq)
                c(v.tensor_copy(wt[:, :, :], qw[:, :, :]))
                c(v.tensor_scalar(wt[:, :, :], wt[:, :, :], 1.0 / 7.5, -1.0, ALU.mult, ALU.add))
                c(v.tensor_tensor(wt[:, :, :], wt[:, :, :], scl[:, :, :], ALU.mult))
                dve.wait_ge(lora_ready, 1)
                v.tensor_tensor(wt[:, 0:4, :], wt[:, 0:4, :], ZT[0][:, :].rearrange("p (l o) -> p l o", l=4), ALU.add
                                ).then_inc(w_ready, 1)
                v.tensor_tensor(wt[:, 4:6, :], wt[:, 4:6, :], H2[0][:, 0:2 * P].rearrange("p (l o) -> p l o", l=2),
                                ALU.add).then_inc(w_ready, 1)
                halves_vector(dve, g, st, g.X, slice(0, NT))
                for r in ROUNDS:
                    moments_vector(dve, g, st, 1e-5, (r + 1) * NT, r)

                    def step(b, par, r=r):
                        n = r * NB + b
                        if there(b, 2) and r > 0:
                            dve.wait_ge(h2_ready, n - NB - 1)
                            dve.wait_ge(y1_ready, n - 3)
                            dve.wait_ge(ht_copied, n - NB - 3)
                            if r == 1:
                                dve.wait_ge(act_done, NB)
                            v.scalar_tensor_tensor(out=hT[:, par, :], in0=H2[par][:, 0:T],
                                                   scalar=b2[:, r - 1:r], in1=HT[:, bass.ds((b - 2) * T, T)],
                                                   op0=ALU.add, op1=ALU.add).then_inc(h_ready, 1)
                        if there(b, 3):
                            dve.wait_ge(y1_ready, n - 2)
                            y = Y1[par ^ 1][:, 0:T].rearrange("p (t o) -> p t o", t=TT)
                            if r < NBLOCK:
                                dst = g.XP[:, bass.ds((b - 3) * TT, TT), :]
                                v.tensor_tensor(dst, y, b1[:, r:r + 1, :].broadcast_to([P, TT, P]), ALU.add
                                                ).then_inc(y1_used, 1)
                                dve.wait_ge(y1_used, n - 2)
                                for t in range(TT):
                                    tile = (b - 3) * TT + t
                                    v.bn_stats(g.bn6[:, bass.ds(tile * 6, 6)], g.XP[:, bass.ds(tile, 1), :]
                                               ).then_inc(st.bn_done, 1)
                            else:
                                dst = g.X[:, bass.ds((b - 3) * TT, TT), :]
                                v.tensor_tensor(dst, dst, y, ALU.add).then_inc(y1_used, 1)
                    in_order(dve, step, 3)
        retire(g, st)


def store_stage(nc, g, out):
    with ExitStack() as ctx:
        st = Scope(nc, ctx, "store")
        x_out = st.sem("x_out")
        with nc.Block() as block:
            @block.sync
            def _(sp):
                sp = Engine(sp)
                ov = out.rearrange("(n p) d -> p n d", p=P)
                for k in range(4):
                    sp.dma_start(ov[:, k * 8:(k + 1) * 8, :], g.X[:, k * 8:(k + 1) * 8, :]).then_inc(x_out, 16)
                sp.wait_ge(x_out, 64)
        g.retired.sem_ctx.close()
        st.sem_ctx.close()


class Globals:
    pass


def build_program(nc, a, out, stages):
    g = Globals()
    g.nc, g.retired = nc, None
    g.score_scale = float(np.float32(1.0) / np.sqrt(np.float32(8.0)))
    with ExitStack() as ctx:
        def sb(name, shape, dt=F32):
            return ctx.enter_context(nc.sbuf_tensor(name, shape, dt))
        ntp = NT + 2 * PAD
        g.X = sb("X", [P, ntp, P])
        g.XP = sb("XP", [P, ntp, P])
        g.bn6, g.mean, g.gap, g.rstd = sb("bn6", [P, ntp * 6]), sb("mean", [P, ntp]), sb("gap", [P, ntp]), sb("rstd", [P, ntp])
        g.neghalf = sb("neghalf", [P, ntp])
        g.ident, g.identb = sb("ident", [P, P]), sb("identb", [P, P], BF16)
        g.maskb = sb("maskb", [P, 2, P], BF16)
        g.scratch, g.scratch2 = a["scratch"], a["scratch2"]
        load_stage(nc, a["x"], g)
        of = lambda prefix: {k[4:]: v for k, v in a.items() if k.startswith(prefix)}
        for n, s in enumerate(stages):
            name = f"s{n}"
            if s == "L0a":
                hyperbolic_attention_stage(nc, g, of("l0a_"), name)
            if s == "L0b":
                attention_stage(nc, g, of("l0b_"), causal=True, name=name)
            if s == "F":
                attention_stage(nc, g, of("ffn_"), causal=False, rope=True, moe=True, name=name)
            if s == "L1a":
                wide_attention_stage(nc, g, of("l1a_"), name)
            if s == "MOE":
                moe_stage(nc, g, of("moe_"), name)
            if s == "L1b":
                attention_stage(nc, g, of("l1b_"), causal=True, bias=True, name=name)
            if s == "Q":
                qlora_stage(nc, g, of("qlo_"), name)
        store_stage(nc, g, out)


def rope_tables(scale):
    inv = (np.float32(1.0) / np.float32(10000.0) ** (np.arange(0, 8, 2, dtype=np.float32) / np.float32(8)))
    ang = np.arange(T, dtype=np.float32)[:, None] * inv.astype(np.float32)[None, :]
    cos, sin = np.cos(ang).T, np.sin(ang).T
    f = np.arange(P)
    c = cos[(f % 8) // 2]
    s = sin[(f % 8) // 2] * np.where(f % 2 == 0, -1, 1)[:, None]
    both = lambda m: np.stack([m * scale, m], axis=1).astype(np.float32)
    return both(c), both(s)


def half_rope(odd):
    inv = np.float32(1.0) / np.float32(6000.0) ** (np.arange(0, 32, 2, dtype=np.float32) / np.float32(32))
    ang = (np.arange(T, dtype=np.float32)[:, None] * inv.astype(np.float32)[None, :]).T
    cos, sin = np.ones((64, T), np.float32), np.zeros((64, T), np.float32)
    at = 32 if odd else 0
    cos[at:at + 16], cos[at + 16:at + 32] = np.cos(ang), np.cos(ang)
    sin[at:at + 16], sin[at + 16:at + 32] = -np.sin(ang), np.sin(ang)
    return np.tile(cos, (2, 1)), np.tile(sin, (2, 1))


def rows(v):
    return np.ascontiguousarray(np.broadcast_to(v.reshape(1, -1), (P, v.size)))


def layouts(inp):
    a = {"x": inp["L0_attn_a_x"].reshape(NB * T, P)}
    one = lambda n: inp["L0_attn_a_" + n]
    a["l0a_wall"] = np.concatenate([one("Wqkv"), one("Walpha"), one("Wimp")], axis=0).T
    a["l0a_ball"] = rows(np.concatenate([one("bqkv"), one("balpha"), one("bimp")]))
    a["l0a_wo"], a["l0a_bo"] = one("Wout").T, rows(one("bout"))
    a["l0a_thr"], a["l0a_qk_scale"], a["l0a_log_k"] = (rows(one(n)) for n in ("spike_threshold", "qk_scale", "log_k"))
    w = inp["L0_attn_b_Wqkv"]
    a["l0b_wq"], a["l0b_wk"], a["l0b_wv"] = w[0:P].T, w[P:2 * P].T, w[2 * P:].T
    a["l0b_wo"] = inp["L0_attn_b_Wout"].T
    w, b = inp["L1_attn_b_Wqkv"].transpose(1, 0, 2), inp["L1_attn_b_bqkv"]
    for k, n in enumerate("qkv"):
        a["l1b_w" + n] = w[:, :, 8 * k:8 * k + 8].reshape(P, P)
        bb = b[:, 8 * k:8 * k + 8].reshape(P)
        a["l1b_b" + n] = rows(bb) if n == "v" else bb.reshape(P, 1)
    a["l1b_wo"] = inp["L1_attn_b_Wout"]
    a["l1b_bo"] = rows(inp["L1_attn_b_bout"])
    swap = np.arange(P) ^ 1
    a["ffn_wq"], a["ffn_wqs"] = inp["L0_ffn_Wq"], inp["L0_ffn_Wq"][:, swap]
    a["ffn_wkcT"], a["ffn_wvcT"] = inp["L0_ffn_Wk_c"].T, inp["L0_ffn_Wv_c"].T
    a["ffn_wk"], a["ffn_wks"], a["ffn_wv"] = inp["L0_ffn_Wk"], inp["L0_ffn_Wk"][:, swap], inp["L0_ffn_Wv"]
    a["ffn_wo"] = inp["L0_ffn_Wo"]
    a["ffn_cosT"], a["ffn_sinT"] = rope_tables(np.float32(1.0) / np.sqrt(np.float32(8.0)))
    w = inp["L1_attn_a_W_qkv"]
    swap = np.r_[16:32, 0:16]
    for n, m in (("q", w[0]), ("k", w[1])):
        pairs = m.reshape(NPAIR // 2, 2, 2, 64, P)
        odd = np.concatenate([pairs[:, 1, :, 32:], pairs[:, 1, :, 0:32]], axis=2)
        plain = np.stack([pairs[:, 0], odd], axis=1)
        a["l1a_w" + n] = plain.reshape(NPAIR, P, P).transpose(2, 0, 1)
        turning = pairs[:, :, :, swap].transpose(0, 2, 1, 3, 4)
        a[f"l1a_w{n}s"] = turning.reshape(NPAIR // 2, P, P).transpose(2, 0, 1)
    a["l1a_wv"] = w[2].reshape(H * 64, P).T
    a["l1a_wo"] = inp["L1_attn_a_W_o"].T.reshape(NPAIR, P, P).transpose(1, 0, 2)
    (cos_e, sin_e), (cos_o, sin_o), scale = half_rope(False), half_rope(True), np.float32(0.125)
    for n, m in (("a", (cos_e * scale, sin_e * scale)), ("b", (cos_o * scale, sin_e)), ("c", (cos_e, cos_o)),
                 ("d", (sin_o * scale, sin_o))):
        a["l1a_turn_" + n] = np.concatenate(m, axis=1).astype(np.float32)
    ins, w1 = inp["L0_ffn_W_shared_in"], inp["L0_ffn_W1_shared"]
    a["moe_wa"] = np.concatenate([ins[:, 0:256], w1[:, 0:256]], axis=1).reshape(P, 4, P)
    a["moe_wb"] = np.concatenate([ins[:, 256:], w1[:, 256:]], axis=1).reshape(P, 4, P)
    a["moe_wso"] = inp["L0_ffn_W_shared_out"].reshape(2, P, P).transpose(1, 0, 2)
    a["moe_w2"] = inp["L0_ffn_W2_experts"].reshape(8, 2, P, P).transpose(2, 1, 0, 3).reshape(P, 2, 8 * P)
    a["moe_wg"] = np.concatenate([inp["L0_ffn_Wg_gate"], inp["L0_ffn_We_gate"]], axis=1)
    a["moe_bg"] = rows(np.concatenate([inp["L0_ffn_group_bias"], inp["L0_ffn_expert_bias"]]))
    a["moe_n1"], a["moe_n2"] = rows(inp["L0_ffn_norm1_w"]), rows(inp["L0_ffn_norm2_w"])
    a["qlo_qw"] = inp["L1_ffn_qweights"].transpose(2, 0, 1)
    a["qlo_scl"] = np.repeat(inp["L1_ffn_scales"], P // inp["L1_ffn_scales"].shape[2], axis=2).transpose(2, 0, 1)
    a["qlo_la"] = inp["L1_ffn_lora_a"].transpose(1, 0, 2)
    a["qlo_lb"] = inp["L1_ffn_lora_b"].transpose(2, 0, 1)
    a["qlo_b1"] = rows(inp["L1_ffn_biases"][0::2].reshape(-1)).reshape(P, 3, P)
    a["qlo_b2"] = inp["L1_ffn_biases"][1::2].T
    a["qlo_gam"], a["qlo_bet"] = inp["L1_ffn_ln_gamma"].T, inp["L1_ffn_ln_beta"].T
    return {k: np.ascontiguousarray(v) for k, v in a.items()}


STAGES = ("L0a", "F", "MOE", "L0b", "F", "MOE", "L1a", "Q", "L1b", "Q")


def kernel(**inputs):
    from concourse import bacc
    from concourse.bass_utils import run_bass_kernel_spmd

    arrays = layouts({k: np.asarray(v) for k, v in inputs.items()})
    nc = bacc.Bacc("TRN2", target_bir_lowering=False, num_devices=1)
    a = {k: nc.dram_tensor(k, v.shape, mybir.dt.from_np(v.dtype), kind="ExternalInput").ap()
         for k, v in arrays.items()}
    a["scratch"] = nc.dram_tensor("scratch", (2, 3, P, 2 * T), BF16, kind="Internal").ap()
    a["scratch2"] = nc.dram_tensor("scratch2", (2, 2, 3, P, 2 * T), BF16, kind="Internal").ap()
    out = nc.dram_tensor("out", (NB * T, P), F32, kind="ExternalOutput").ap()
    build_program(nc, a, out, STAGES)
    r = run_bass_kernel_spmd(nc, [arrays], core_ids=[0])
    return r.results[0]["out"].reshape(NB, T, P)
```
